# Optimizing a Trainium2 kernel written in Bass

```python
import numpy as np
import jax
import jax.numpy as jnp

def _softmax(x, axis=-1):
    return jax.nn.softmax(x, axis=axis)

def _gelu(x):
    return jax.nn.gelu(x, approximate=True)

def _silu(x):
    return jax.nn.silu(x)

def _sigmoid(x):
    return jax.nn.sigmoid(x)

def _layernorm(x, axis=-1, eps=1e-05):
    m = jnp.mean(x, axis=axis, keepdims=True)
    v = jnp.var(x, axis=axis, keepdims=True)
    return (x - m) / jnp.sqrt(v + eps)

def _scatter_add(tgt, idx, src, axis=0):
    return tgt.at[idx].add(src)

def _segment_sum(src, seg, n):
    return jax.ops.segment_sum(src, seg, n)
kernel_name = 'mk_prb_d2_jaxref_r8_98476b'

def setup_inputs(seed: int=0):
    np.random.seed(seed)
    _w = jnp.asarray

    def _L0_attn_setup():
        import jax, jax.numpy as jnp
        import numpy as np
        B, T, H, S, F, G = (2, 256, 512, 128, 1248, 6)
        GRAD_ORDER_MIN = 4
        THD = 2.5
        key = jax.random.key(seed)
        ks = jax.random.split(key, 9)
        sc = 0.02
        hidden_states = jax.random.normal(ks[0], (B, T, H), jnp.float32)
        up_w = jax.random.normal(ks[1], (S, H), jnp.float32) * sc
        gate_w = jax.random.normal(ks[2], (S, H), jnp.float32) / np.sqrt(H)
        local_point = jax.random.normal(ks[3], (S,), jnp.float32)
        local_approx_output = jax.random.normal(ks[4], (H, S), jnp.float32) * sc
        fuse_weight = jax.random.normal(ks[5], (H, S, G), jnp.float32) * sc
        discount_factor = jnp.asarray(np.cumsum(np.log(np.arange(1, G + 1, dtype=np.float64))), jnp.float32)
        ffn_gate_w = jax.random.normal(ks[6], (F, H), jnp.float32) * sc
        ffn_up_w = jax.random.normal(ks[7], (F, H), jnp.float32) * sc
        ffn_down_w = jax.random.normal(ks[8], (H, F), jnp.float32) * sc
        return {'hidden_states': hidden_states, 'up_w': up_w, 'gate_w': gate_w, 'local_point': local_point, 'local_approx_output': local_approx_output, 'fuse_weight': fuse_weight, 'discount_factor': discount_factor, 'ffn_gate_w': ffn_gate_w, 'ffn_up_w': ffn_up_w, 'ffn_down_w': ffn_down_w}
    _L0_attn_in = _L0_attn_setup()

    def _L0_ffn_setup():
        import jax, jax.numpy as jnp
        import numpy as np
        B_, S, D = (4, 512, 512)
        E, R, O = (8, 16, 512)
        TOP_K = 2
        SCALING = 8.0 / R
        key = jax.random.key(seed)
        ks = jax.random.split(key, 5)
        x = jax.random.normal(ks[0], (B_, S, D), dtype=jnp.float32)
        router_w = jax.random.normal(ks[1], (E, D), dtype=jnp.float32) * (1.0 / np.sqrt(D))
        router_b = jax.random.normal(ks[2], (E,), dtype=jnp.float32) * 0.01
        A = jax.random.normal(ks[3], (E, R, D), dtype=jnp.float32) * (1.0 / np.sqrt(D))
        Bm = jax.random.normal(ks[4], (E, O, R), dtype=jnp.float32) * 0.02
        return {'x': x, 'router_w': router_w, 'router_b': router_b, 'A': A, 'Bm': Bm}
    _L0_ffn_in = _L0_ffn_setup()

    def _L1_attn_setup():
        import jax, jax.numpy as jnp
        import numpy as np
        import math
        B, L, D, H = (32, 64, 512, 32)
        HD = D // H
        key = jax.random.key(seed)
        ks = jax.random.split(key, 9)
        s = 1.0 / math.sqrt(D)
        return {'x': jax.random.normal(ks[0], (B, L, D), jnp.float32), 'Wq': jax.random.normal(ks[1], (D, D), jnp.float32) * s, 'bq': jax.random.normal(ks[2], (D,), jnp.float32) * s, 'Wk': jax.random.normal(ks[3], (D, D), jnp.float32) * s, 'bk': jax.random.normal(ks[4], (D,), jnp.float32) * s, 'Wv': jax.random.normal(ks[5], (D, D), jnp.float32) * s, 'bv': jax.random.normal(ks[6], (D,), jnp.float32) * s, 'Wo': jax.random.normal(ks[7], (D, D), jnp.float32) * s, 'bo': jax.random.normal(ks[8], (D,), jnp.float32) * s}
    _L1_attn_in = _L1_attn_setup()

    def _L1_ffn_setup():
        import jax, jax.numpy as jnp
        import numpy as np
        SCALING = 32.0 / 16.0
        key = jax.random.key(seed)
        ks = jax.random.split(key, 7)
        B, T, D, O, R, E = (4, 256, 512, 512, 16, 8)
        x = jax.random.normal(ks[0], (B, T, D), dtype=jnp.float32)
        base_W = jax.random.normal(ks[1], (O, D), dtype=jnp.float32) * D ** (-0.5)
        base_b = jax.random.normal(ks[2], (O,), dtype=jnp.float32) * 0.01
        router_W = jax.random.normal(ks[3], (2 * E - 1, D), dtype=jnp.float32) * D ** (-0.5)
        router_b = jax.random.normal(ks[4], (2 * E - 1,), dtype=jnp.float32) * 0.01
        A = jax.random.normal(ks[5], (E, R, D), dtype=jnp.float32) * D ** (-0.5)
        Bm = jax.random.normal(ks[6], (E, O, R), dtype=jnp.float32) * R ** (-0.5)
        assigned_idx = 0
        others = [i for i in range(E) if i != assigned_idx]
        expert_map = jnp.array([assigned_idx] * E + others, dtype=jnp.int32)
        return {'x': x, 'base_W': base_W, 'base_b': base_b, 'router_W': router_W, 'router_b': router_b, 'A': A, 'B': Bm, 'expert_map': expert_map}
    _L1_ffn_in = _L1_ffn_setup()
    _d = {'L0_attn_hidden_states': _L0_attn_in['hidden_states'], 'L0_attn_up_w': _L0_attn_in['up_w'], 'L0_attn_gate_w': _L0_attn_in['gate_w'], 'L0_attn_local_point': _L0_attn_in['local_point'], 'L0_attn_local_approx_output': _L0_attn_in['local_approx_output'], 'L0_attn_fuse_weight': _L0_attn_in['fuse_weight'], 'L0_attn_discount_factor': _L0_attn_in['discount_factor'], 'L0_attn_ffn_gate_w': _L0_attn_in['ffn_gate_w'], 'L0_attn_ffn_up_w': _L0_attn_in['ffn_up_w'], 'L0_attn_ffn_down_w': _L0_attn_in['ffn_down_w'], 'L0_ffn_router_w': _L0_ffn_in['router_w'], 'L0_ffn_router_b': _L0_ffn_in['router_b'], 'L0_ffn_A': _L0_ffn_in['A'], 'L0_ffn_Bm': _L0_ffn_in['Bm'], 'L1_attn_Wq': _L1_attn_in['Wq'], 'L1_attn_bq': _L1_attn_in['bq'], 'L1_attn_Wk': _L1_attn_in['Wk'], 'L1_attn_bk': _L1_attn_in['bk'], 'L1_attn_Wv': _L1_attn_in['Wv'], 'L1_attn_bv': _L1_attn_in['bv'], 'L1_attn_Wo': _L1_attn_in['Wo'], 'L1_attn_bo': _L1_attn_in['bo'], 'L1_ffn_base_W': _L1_ffn_in['base_W'], 'L1_ffn_base_b': _L1_ffn_in['base_b'], 'L1_ffn_router_W': _L1_ffn_in['router_W'], 'L1_ffn_router_b': _L1_ffn_in['router_b'], 'L1_ffn_A': _L1_ffn_in['A'], 'L1_ffn_B': _L1_ffn_in['B'], 'L1_ffn_expert_map': _L1_ffn_in['expert_map']}
    _x0 = _d['L0_attn_hidden_states']
    _d['L0_attn_hidden_states'] = jax.random.normal(jax.random.fold_in(jax.random.key(seed), 1), (1, 1024, 512), dtype=_x0.dtype)
    del _x0
    return _d

def reference(L0_attn_hidden_states, L0_attn_up_w, L0_attn_gate_w, L0_attn_local_point, L0_attn_local_approx_output, L0_attn_fuse_weight, L0_attn_discount_factor, L0_attn_ffn_gate_w, L0_attn_ffn_up_w, L0_attn_ffn_down_w, L0_ffn_router_w, L0_ffn_router_b, L0_ffn_A, L0_ffn_Bm, L1_attn_Wq, L1_attn_bq, L1_attn_Wk, L1_attn_bk, L1_attn_Wv, L1_attn_bv, L1_attn_Wo, L1_attn_bo, L1_ffn_base_W, L1_ffn_base_b, L1_ffn_router_W, L1_ffn_router_b, L1_ffn_A, L1_ffn_B, L1_ffn_expert_map):

    def _L0_attn_ref(hidden_states, up_w, gate_w, local_point, local_approx_output, fuse_weight, discount_factor, ffn_gate_w, ffn_up_w, ffn_down_w):
        import jax, jax.numpy as jnp
        import numpy as np
        B, T, H, S, F, G = (2, 256, 512, 128, 1248, 6)
        GRAD_ORDER_MIN = 4
        THD = 2.5
        approx_up = hidden_states @ up_w.T
        gate_pre = hidden_states @ gate_w.T
        delta = gate_pre - local_point
        neg_factor = jnp.where(delta > 0, 1.0, -1.0).astype(hidden_states.dtype)
        delta_abs = jnp.abs(delta)
        log_delta = jnp.log(delta_abs)
        keep = (delta_abs <= THD).astype(hidden_states.dtype)
        approx_out = approx_up @ local_approx_output.T
        for idx in range(G):
            m = idx + 1
            dterm = jnp.exp(log_delta * m - discount_factor[idx])
            if m % 2 == 1:
                dterm = dterm * neg_factor
            tmp = dterm * approx_up
            if m > GRAD_ORDER_MIN:
                tmp = tmp * keep
            approx_out = approx_out + tmp @ fuse_weight[:, :, idx].T
        ffn_out = jax.nn.silu(hidden_states @ ffn_gate_w.T) * (hidden_states @ ffn_up_w.T) @ ffn_down_w.T
        return approx_out + ffn_out

    def _L0_ffn_ref(x, router_w, router_b, A, Bm):
        import jax, jax.numpy as jnp
        import numpy as np
        B_, S, D = (4, 512, 512)
        E, R, O = (8, 16, 512)
        TOP_K = 2
        SCALING = 8.0 / R
        flat = x.reshape(-1, x.shape[-1])
        N = flat.shape[0]
        logits = flat @ router_w.T + router_b
        probs = jax.nn.softmax(logits, axis=-1)
        topv, topi = jax.lax.top_k(probs, TOP_K)
        gates = topv / jnp.sum(topv, axis=-1, keepdims=True)
        w = jnp.zeros((N, E), dtype=flat.dtype).at[jnp.arange(N)[:, None], topi].add(gates)
        h = jnp.einsum('nd,erd->ner', flat, A)
        hw = h * w[:, :, None]
        out = jnp.einsum('ner,eor->no', hw, Bm) * SCALING
        return out.reshape(*x.shape[:-1], O)

    def _L1_attn_ref(x, Wq, bq, Wk, bk, Wv, bv, Wo, bo):
        import jax, jax.numpy as jnp
        import numpy as np
        import math
        B, L, D, H = (32, 64, 512, 32)
        HD = D // H
        b, l, d = x.shape
        h, hd = (H, HD)
        q = (x @ Wq.T + bq).reshape(b, l, h, hd).transpose(0, 2, 1, 3)
        k = (x @ Wk.T + bk).reshape(b, l, h, hd).transpose(0, 2, 1, 3)
        v = (x @ Wv.T + bv).reshape(b, l, h, hd).transpose(0, 2, 1, 3)
        scores = jnp.einsum('bhqd,bhkd->bhqk', q, k) / math.sqrt(hd)
        causal = jnp.tril(jnp.ones((l, l), bool))
        scores = jnp.where(causal, scores, -jnp.inf)
        att = jax.nn.softmax(scores, axis=-1)
        out = jnp.einsum('bhqk,bhkd->bhqd', att, v)
        out = out.transpose(0, 2, 1, 3).reshape(b, l, d)
        return out @ Wo.T + bo

    def _L1_ffn_ref(x, base_W, base_b, router_W, router_b, A, B, expert_map):
        import jax, jax.numpy as jnp
        import numpy as np
        SCALING = 32.0 / 16.0
        E = A.shape[0]
        base_out = jnp.einsum('btd,od->bto', x, base_W) + base_b
        logits = jnp.einsum('btd,nd->btn', x, router_W) + router_b
        probs = jax.nn.softmax(logits, axis=-1)
        topk_p, topk_i = jax.lax.top_k(probs, E)
        mapped = expert_map[topk_i]
        onehot = (mapped[..., None] == jnp.arange(E)).astype(x.dtype)
        w = jnp.einsum('btk,btke->bte', topk_p, onehot)
        h = jnp.einsum('btd,erd->bter', x, A)
        lora = jnp.einsum('bter,eor->bto', h * w[..., None], B) * SCALING
        return base_out + lora
    x = L0_attn_hidden_states
    xn = _layernorm(x, axis=-1)
    x = x + _L0_attn_ref(xn, L0_attn_up_w, L0_attn_gate_w, L0_attn_local_point, L0_attn_local_approx_output, L0_attn_fuse_weight, L0_attn_discount_factor, L0_attn_ffn_gate_w, L0_attn_ffn_up_w, L0_attn_ffn_down_w) + _L0_ffn_ref(xn, L0_ffn_router_w, L0_ffn_router_b, L0_ffn_A, L0_ffn_Bm)
    xn = _layernorm(x, axis=-1)
    x = x + _L1_attn_ref(xn, L1_attn_Wq, L1_attn_bq, L1_attn_Wk, L1_attn_bk, L1_attn_Wv, L1_attn_bv, L1_attn_Wo, L1_attn_bo) + _L1_ffn_ref(xn, L1_ffn_base_W, L1_ffn_base_b, L1_ffn_router_W, L1_ffn_router_b, L1_ffn_A, L1_ffn_B, L1_ffn_expert_map)
    return x

_drawn_inputs = setup_inputs


def setup_inputs(seed=0):
    import zlib

    import numpy as np

    out = dict(_drawn_inputs(seed))
    spreads = {}
    factors = {'L0_ffn_router_b': 189.919,
     'L1_attn_bq': 8.0,
     'L1_attn_bk': 200.0,
     'L1_ffn_base_b': 8.0,
     'L1_ffn_router_b': 6.319}
    for name, (base, spread) in spreads.items():
        noise = np.random.default_rng([zlib.crc32(name.encode()), seed]).standard_normal(out[name].shape)
        drawn = base * np.exp(spread * noise) if base else spread * noise
        out[name] = jnp.asarray(drawn.astype(out[name].dtype))
    for name, factor in factors.items():
        out[name] = (out[name] * factor).astype(out[name].dtype)
    return out
```

```python
from contextlib import ExitStack

import numpy as np

import concourse.bass as bass
from concourse import mybir

F32 = mybir.dt.float32
F32R = mybir.dt.float32r
BF16 = mybir.dt.bfloat16
I32 = mybir.dt.int32
ALU = mybir.AluOpType
ACT = mybir.ActivationFunctionType
AX = mybir.AxisListType

P = 128
TOK, D = 1024, 512
KD = D // P
NT = TOK // P
HALF = TOK // 2
HT = HALF // P
FF = 1248
FC = -(-FF // P)
FSHORT = FF - (FC - 1) * P
ORDERS = 6
ORDER_MIN = 4
DELTA_MAX = 2.5
NE = 8
RANK = 16
SCALE0 = 8.0 / RANK
SCALE1 = 32.0 / 16.0
ROUTES = 2 * NE - 1
ROUTES_PAD = 16
HEADS, HD = 32, 16
GH = 4
GROUPS = HEADS // GH
QK_ROWS = 3 * HD
ST_ROWS = QK_ROWS + 2
EPS = 1e-5
MASKED = -1.0e30
SLOT = 1024

RESIDENT = ["lora_a", "lora_b"]
for _c in range(7):
    RESIDENT += [f"down{_c}", f"term{_c}"]
RESIDENT += ["down7", "down8", "down9", "pad"]
RES_AT = {name: n for n, name in enumerate(RESIDENT)}


def weight_items():
    items, arrays = [], []

    def add(dest, name):
        if name not in arrays:
            arrays.append(name)
        items.append((dest, name))

    for half in range(2):
        add("ring", "gate_up")
        for c in range(FC):
            add("ring", f"ffn{c}")
            if half == 0:
                add("resident", f"res{c}")
    add("ring", "qk0")
    add("ring", "lora1")
    for n in range(2):
        add(f"v{n}", f"wv{n}")
    for n in range(2):
        add(f"base{n}", f"base{n}")
    for m in range(1, KD):
        add("ring", f"qk{m}")
    for n in range(2):
        add(f"wo{n}", f"wo{n}")
    return items, arrays


ITEMS, ARRAYS = weight_items()


def lay_out_weights(w):
    def kxm(a):
        t = a.T
        return t.reshape(t.shape[0] // P, P, t.shape[1]).transpose(1, 0, 2)

    ffn_gate, ffn_up = kxm(w["L0_attn_ffn_gate_w"]), kxm(w["L0_attn_ffn_up_w"])
    down = w["L0_attn_ffn_down_w"].T
    router0 = kxm(w["L0_ffn_router_w"])
    out = np.zeros((len(ARRAYS), P, SLOT), np.float32)
    at = {name: n for n, name in enumerate(ARRAYS)}

    def put(name, n, a):
        if a.ndim == 3:
            a = a.reshape(P, -1)
        out[at[name], :a.shape[0], n:n + a.shape[1]] = a

    def pair(name, left, right):
        v = out[at[name]].reshape(P, KD, 2, P)
        v[:, :, 0, :left.shape[2]] = left
        v[:, :, 1, :right.shape[2]] = right

    pair("gate_up", kxm(w["L0_attn_gate_w"]), kxm(w["L0_attn_up_w"]))
    bounds = [0, FSHORT] + [FSHORT + P * c for c in range(1, FC)]
    for c in range(FC):
        a, b = bounds[c], bounds[c + 1]
        left = ffn_gate[:, :, a:b]
        if c == 0:
            left = np.concatenate([left, router0], axis=2)
        pair(f"ffn{c}", left, ffn_up[:, :, a:b])

    def resident(name):
        if name == "lora_a":
            return kxm(w["L0_ffn_A"].reshape(NE * RANK, D)).reshape(P, -1)
        if name == "lora_b":
            return w["L0_ffn_Bm"].transpose(0, 2, 1).reshape(NE * RANK, D)
        if name == "term0":
            return w["L0_attn_local_approx_output"].T
        if name.startswith("term"):
            return w["L0_attn_fuse_weight"][:, :, int(name[4:]) - 1].T
        c = int(name[4:])
        return down[bounds[c]:bounds[c + 1]]

    for n, name in enumerate(RESIDENT):
        if name != "pad":
            put(f"res{n // 2}", (n % 2) * D, resident(name))
    wq, wk = kxm(w["L1_attn_Wq"]), kxm(w["L1_attn_Wk"])
    for m in range(KD):
        pair(f"qk{m}", wq[:, :, m * P:(m + 1) * P], wk[:, :, m * P:(m + 1) * P])
    put("lora1", 0, kxm(w["L1_ffn_A"].reshape(NE * RANK, D)))
    put("lora1", D, w["L1_ffn_B"].transpose(0, 2, 1).reshape(NE * RANK, D))
    for name, a in (("wv", w["L1_attn_Wv"]), ("base", w["L1_ffn_base_W"]), ("wo", w["L1_attn_Wo"])):
        t = kxm(a)
        for n in range(2):
            put(f"{name}{n}", 0, t[:, 2 * n:2 * n + 2])
    router1 = np.zeros((P, KD, ROUTES_PAD), np.float32)
    router1[:, :, :ROUTES] = kxm(w["L1_ffn_router_W"])
    return out, router1

LAG = 1
NPROB = 8
VEC_POINT, VEC_ROUTER0, VEC_ROUTER1, VEC_Q, VEC_K = 0, 1, 2, 3, 3 + KD
VECS = VEC_K + KD


def psum_users():
    users = [("x", 0), ("x", 1)]
    for half in range(2):
        users += [("s", half), ("f", half * FC), ("l", half)]
        for c in range(1, FC):
            users.append(("f", half * FC + c))
            if c in X_AFTER:
                users.append(("x", 2 + 2 * half + X_AFTER.index(c)))
    users += [("x", 6), ("x", 7), ("q", 0), ("k", 0), ("r", 0), ("a", 0), ("w", 0)]
    users += [("max", u) for u in range(UNITS)] + [("m", 0)]
    for g in range(GROUPS):
        for s in range(STEPS):
            users += extras(g, s)
    return users


X_AFTER = (3, 4)
QSTEPS = [(0, j) for j in range(HT)] + [(1, j) for j in range(NT)]
STEPS = len(QSTEPS)
UNITS = GH * NT
MAX_STEPS = 9


def extras(g, s):
    todo = []
    if g + 1 < GROUPS:
        if s < MAX_STEPS:
            todo += [("max", (g + 1) * UNITS + u)
                     for u in range(UNITS * s // MAX_STEPS, UNITS * (s + 1) // MAX_STEPS)]
        if s == MAX_STEPS:
            todo.append(("m", g + 1))
    if g % 2 == 0 and g // 2 + 1 < KD:
        if s == 4:
            todo.append(("q", g // 2 + 1))
        if s == 6:
            todo.append(("k", g // 2 + 1))
    if g == GROUPS - 1 and s in (2, 4):
        todo.append(("o", (s - 2) // 2))
    return todo


USERS = psum_users()
USER_AT = {u: n for n, u in enumerate(USERS)}


def build(nc, stream, router1, x_in, vec, bias_rows, discount, expert_map, out):
    nodes = ExitStack()
    with nodes:
        def sem(name):
            return nodes.enter_context(nc.semaphore(name))

        def sb(stack, name, shape, dt=F32):
            return stack.enter_context(nc.sbuf_tensor(name, shape, dt))

        ident = sb(nodes, "ident", [P, P])
        causal = sb(nodes, "causal", [P, NT * P], BF16)
        x_sb = sb(nodes, "x_sb", [P, NT, D])
        xt_hi = sb(nodes, "xt_hi", [P, KD, TOK], F32R)
        xt_lo = sb(nodes, "xt_lo", [P, KD, TOK], F32R)
        stage = sb(nodes, "stage", [P, 2, SLOT])
        ring_hi = sb(nodes, "ring_hi", [P, 2, SLOT], F32R)
        ring_lo = sb(nodes, "ring_lo", [P, 2, SLOT], F32R)
        stats = sb(nodes, "stats", [P, NT, 6])
        mean_var = sb(nodes, "mean_var", [P, NT, 2])
        rstd = sb(nodes, "rstd", [P, NT])
        eps_col = sb(nodes, "eps_col", [P, 1])
        vec_sb = sb(nodes, "vec_sb", [P, VECS])
        disc = sb(nodes, "disc", [P, ORDERS])
        ratio = sb(nodes, "ratio", [P, ORDERS])
        logit = sb(nodes, "logit", [P, NT, ROUTES_PAD])
        prob = sb(nodes, "prob", [P, NT, ROUTES_PAD])
        rest = sb(nodes, "rest", [P, NT, ROUTES_PAD])
        chosen = sb(nodes, "chosen", [P, NT, ROUTES_PAD])
        top = sb(nodes, "top", [P, NT, 8])
        rowmax = sb(nodes, "rowmax", [P, NT])
        norm = sb(nodes, "norm", [P, NT])
        gate = sb(nodes, "gate", [P, NT, NE])
        map_i = sb(nodes, "map_i", [P, ROUTES], I32)
        map_f = sb(nodes, "map_f", [P, ROUTES])
        expert_id = sb(nodes, "expert_id", [P, NE])
        onehot = sb(nodes, "onehot", [P, NE, ROUTES])
        rw_stage = sb(nodes, "rw_stage", [P, KD * ROUTES_PAD])
        rw_hi = sb(nodes, "rw_hi", [P, KD, ROUTES_PAD], F32R)
        rw_lo = sb(nodes, "rw_lo", [P, KD, ROUTES_PAD], F32R)

        block0 = ExitStack()
        with block0:
            res_hi = sb(block0, "res_hi", [P, len(RESIDENT), D], F32R)
            res_lo = sb(block0, "res_lo", [P, len(RESIDENT), D], F32R)
            h_hi = sb(block0, "h_hi", [P, 2, HALF], F32R)
            h_lo = sb(block0, "h_lo", [P, 2, HALF], F32R)
            term_hi = sb(block0, "term_hi", [P, 3, HALF], F32R)
            term_lo = sb(block0, "term_lo", [P, 3, HALF], F32R)
            hw_hi = sb(block0, "hw_hi", [P, HALF], F32R)
            hw_lo = sb(block0, "hw_lo", [P, HALF], F32R)
            silu = sb(block0, "silu", [P, HALF])
            h_f = sb(block0, "h_f", [P, HALF])
            delta = sb(block0, "delta", [P, HALF])
            keep = sb(block0, "keep", [P, HALF])
            term_f = sb(block0, "term_f", [P, 2, HALF])
            lora_h = sb(block0, "lora_h", [P, HALF])
            gate_x = sb(block0, "gate_x", [P, HT, NE, RANK])
            lgt = sb(block0, "lgt", [P, HALF])
            xn = sb(block0, "xn", [P, 2, D])
        block1 = ExitStack()
        nodes.enter_context(block1)
        qst = sb(block1, "qst", [P, 3, 2, TOK], F32R)
        kst = sb(block1, "kst", [P, 3, 2, TOK], F32R)
        attn_hi = sb(block1, "attn_hi", [P, KD, TOK], F32R)
        attn_lo = sb(block1, "attn_lo", [P, KD, TOK], F32R)
        v_sb = sb(block1, "v_sb", [P, NT, HEADS, HD + 1])
        probs = sb(block1, "probs", [P, NPROB, HALF])
        u_sb = sb(block1, "u_sb", [P, 2, HALF])
        u_all = sb(block1, "u_all", [P, TOK])
        den_all = sb(block1, "den_all", [P, TOK])
        maxcol = sb(block1, "maxcol", [P, 2, GH, NT])
        negm = sb(block1, "negm", [GH * NT, 2, 2, P], F32R)
        hw1 = (qst[:, 1, 0, :], kst[:, 1, 0, :])
        xn1 = u_all[:].rearrange("p (a n) -> p a n", n=D)
        bv_bc = u_sb[:, 0, :]
        bo_bc = den_all[:, 0:D]
        lgt1 = probs[0:ROUTES_PAD, 0:2, :].rearrange("p a n -> p (a n)")
        lora_h1 = probs[:, 2:4, :].rearrange("p a n -> p (a n)")
        gate_x1 = probs[:, 4:6, :].rearrange("p a (t e r) -> p (a t) e r", e=NE, r=RANK)
        hw_f1 = probs[:, 6:8, :].rearrange("p a n -> p (a n)")
        base_bc = u_sb[:, 1, :]

        slot = [nodes.enter_context(nc.psum_tensor(f"slot{n}", [P, 2, 512], F32)) for n in range(2)]
        bank = [nodes.enter_context(nc.psum_tensor(f"bank{n}", [P, 512], F32)) for n in range(4)]

        S = {name: sem(name) for name in (
            "ident_ready const_ready x_landed0 x_landed1 x_landed2 x_landed3 vec_landed "
            "w_landed0 w_landed1 w_hi w_lo "
            "stat_ready std_ready xn_ready x_turned xt_hi_ready x_free "
            "ratio_diff ratio_ready s_ready t_hi t_f t_lo t_used "
            "f_ready silu_ready h_f_ready h_hi_ready f_free h_used "
            "lgt_ready l_a_ready lora_h_ready logit_ready exp_ready gate_ready l_b_ready hw_f_ready hw_hi_ready l_free "
            "out_ready out_free bias_landed rw_ready hw1_ready "
            "q_ready q_hi q_free k_ready k_hi k_free r_ready r_free a_ready a_free lt_ready w_ready w_free "
            "v_done v_free y_done y_free "
            "max_ready max_free m_ready m_hi m_free "
            "stacks0 stacks1 stacks2 negm_landed "
            "st_ready exp_done masked pv_done u_free u_landed0 u_landed1 "
            "attn_f attn_hi_ready attn_lo_ready y_biased o_ready out_sb_ready stored dve k_ones kst2 "
        ).split()}

        def slot_of(user):
            return slot[USER_AT[user] % 2]

        def freed(user):
            n = USER_AT[user]
            if n < 2:
                return None
            kind, k = USERS[n - 2]
            if kind == "s":
                return S["t_lo"], 7 * k + 1
            return S[f"{kind}_free"], k + 1

        def o_bank(t):
            return slot_of(("o", t // 2))[:, t % 2, :] if t < 4 else bank[t - 4][:, :]

        def wait_slot(pe, user):
            f = freed(user)
            if f is not None:
                pe.wait_ge(*f)

        item_at, ring_at = {}, {}
        for n, (dest, name) in enumerate(ITEMS):
            item_at[(name, sum(1 for d, m in ITEMS[:n] if m == name))] = n
            if dest == "ring":
                ring_at[n] = len(ring_at)

        def ring_of(name, half=0):
            n = item_at[(name, half)]
            r = ring_at[n] % 2
            return n, ring_hi[:, r, :], ring_lo[:, r, :]

        def ring_done(r):
            name = [m for d, m in ITEMS if d == "ring"][r]
            half = int(r > FC)
            if name == "gate_up":
                return S["s_ready"], half + 1
            if name.startswith("ffn"):
                return S["f_ready"], half * FC + int(name[3:]) + 1
            if name == "lora1":
                return S["y_done"], NT
            return S["k_ready"], int(name[2:]) + 1

        def destination(n):
            dest, name = ITEMS[n]
            if dest == "ring":
                r = ring_at[n] % 2
                return ring_hi[:, r, :], ring_lo[:, r, :]
            if dest == "resident":
                c = int(name[3:])
                return tuple(t[:, 2 * c:2 * c + 2, :].rearrange("p a n -> p (a n)") for t in (res_hi, res_lo))
            i = int(dest[-1])
            if dest[0] == "v":
                return attn_hi[:, i, :], attn_lo[:, i, :]
            if dest[0] == "b":
                return qst[:, 2, i, :], kst[:, 2, i, :]
            return tuple(t[:, i, :] for t in (xt_hi, xt_lo))

        def res(name):
            return res_hi[:, RES_AT[name], :], res_lo[:, RES_AT[name], :]

        v_w = [t[:, 0:2, :].rearrange("p a (b n) -> p (a b) n", n=D) for t in (attn_hi, attn_lo)]
        base_w = [t[:, 2, :, :].rearrange("p a (b n) -> p (a b) n", n=D) for t in (qst, kst)]
        wo_w = [t[:, 0:2, :].rearrange("p a (b n) -> p (a b) n", n=D) for t in (xt_hi, xt_lo)]
        nat = {("q", 0): attn_hi[:, 2, :], ("q", 1): attn_lo[:, 2, :],
               ("k", 0): attn_hi[:, 3, :], ("k", 1): attn_lo[:, 3, :]}

        block = nodes.enter_context(nc.Block())

        @block.sync
        def _(sp):
            def weights(n):
                if n >= 2:
                    sp.wait_ge(S["w_lo"], n - 1)
                sp.dma_start(stage[:, n % 2, :], stream[ARRAYS.index(ITEMS[n][1])]).then_inc(S[f"w_landed{n % 2}"], 16)

            sp.dma_start(x_sb[:, 0, :], x_in[0]).then_inc(S["x_landed0"], 16)
            sp.dma_start(x_sb[:, 1, :], x_in[1]).then_inc(S["x_landed1"], 16)
            weights(0)
            sp.dma_start(x_sb[:, 2:4, :], x_in[2:4].rearrange("t p d -> p t d")).then_inc(S["x_landed2"], 16)
            weights(1)
            sp.dma_start(x_sb[:, 4:8, :], x_in[4:8].rearrange("t p d -> p t d")).then_inc(S["x_landed3"], 16)
            for n in range(2, item_at[("base1", 0)] + 1):
                weights(n)

            def stack(g):
                m, z = g // 2, g % 3
                if g >= 3:
                    sp.wait_ge(S["st_ready"], GH * STEPS * (g - 2))
                if g == 1:
                    sp.wait_ge(S["kst2"], 1)
                sp.wait_ge(S["k_ones"], 1)
                sp.wait_ge(S["q_free"], m + 1)
                sp.wait_ge(S["k_free"], m + 1)
                for hh in range(GH):
                    row = HD * (GH * (g % 2) + hh)
                    at = 64 * (hh % 2)
                    for st, which, parts in ((qst, "q", (0, 1, 0)), (kst, "k", (0, 0, 1))):
                        for n, part in enumerate(parts):
                            sp.dma_start(st[at + HD * n:at + HD * (n + 1), z, hh // 2, :].bitcast(F32),
                                         nat[which, part][row:row + HD, :].bitcast(F32)
                                         ).then_inc(S[f"stacks{z}"], 16)

            def neg_max(g):
                sp.wait_ge(S["m_free"], g + 1)
                for hh in range(GH):
                    for part in range(2):
                        at = 64 * (hh % 2) + QK_ROWS + part
                        sp.dma_start(qst[at:at + 1, g % 3, hh // 2, :].rearrange("p (i n) -> p i n", n=P).bitcast(F32),
                                     negm[NT * hh:NT * (hh + 1), g % 2, part, :].bitcast(F32)
                                     ).then_inc(S["negm_landed"], 16)

            def gather(g, half):
                e = 2 * g + half
                sp.wait_ge(S["u_free"], e + 1)
                if e == 0:
                    sp.wait_ge(S["y_biased"], NT)
                if g % 2 == 0 and g > 0:
                    sp.wait_ge(S["attn_lo_ready"], g // 2 * 2)
                for hh in range(GH):
                    row = HD * (GH * (g % 2) + hh)
                    to = (slice(row, row + HD), slice(half * HALF, (half + 1) * HALF))
                    sp.dma_start(u_all[to], u_sb[32 * hh:32 * hh + HD, e % 2, :]
                                 ).then_inc(S[f"u_landed{half}"], 16)
                    den = u_sb[32 * hh + HD:32 * hh + HD + 1, e % 2, :]
                    sp.dma_start(den_all[to], bass.AP(den.tensor, den.offset, [den.ap[0], [0, HD], [1, HALF]])
                                 ).then_inc(S[f"u_landed{half}"], 16)

            stack(0)
            weights(item_at[("qk1", 0)])
            neg_max(0)
            stack(1)
            for g in range(GROUPS):
                for s in range(STEPS):
                    if s == 3 and g > 0:
                        gather(g - 1, 1)
                    if s == 0 and g % 2 == 1 and g + 2 < GROUPS:
                        stack(g + 2)
                    if s == 7:
                        gather(g, 0)
                        if g % 2 == 0 and g + 2 < GROUPS:
                            for name in {0: ["qk2"], 2: ["qk3"], 4: ["wo0", "wo1"]}[g]:
                                weights(item_at[(name, 0)])
                    if s == 10 and g + 1 < GROUPS:
                        neg_max(g + 1)
                        if g % 2 == 0 and g + 2 < GROUPS:
                            stack(g + 2)
            gather(GROUPS - 1, 1)
            for t in range(NT):
                sp.wait_ge(S["out_sb_ready"], t + 1)
                sp.dma_start(out[t], x_sb[:, t, :]).then_inc(S["stored"], 16)
            sp.wait_ge(S["stored"], 16 * NT)

        @block.gpsimd
        def _(pool):
            pool.memset(ident[:], 0.0).then_inc(S["ident_ready"], 1)
            pool.wait_ge(S["ident_ready"], 1)
            pool.affine_select(out=ident[:], in_=ident[:], compare_op=ALU.not_equal, fill=1.0, base=0,
                               pattern=[[-1, P]], channel_multiplier=1).then_inc(S["ident_ready"], 1)
            pool.memset(eps_col[:], EPS).then_inc(S["const_ready"], 1)
            pool.memset(prob[:], -1.0).then_inc(S["const_ready"], 1)
            pool.memset(causal[:], 0.0).then_inc(S["const_ready"], 1)
            pool.dma_start(vec_sb[:], vec).then_inc(S["vec_landed"], 16)
            pool.dma_start(disc[:], discount.partition_broadcast(P)).then_inc(S["vec_landed"], 16)
            pool.dma_start(map_i[:], expert_map.partition_broadcast(P)).then_inc(S["vec_landed"], 16)
            pool.dma_start(rw_stage[:], router1).then_inc(S["vec_landed"], 16)
            pool.wait_ge(S["const_ready"], 3)
            pool.affine_select(out=causal[:, (NT - 1) * P:], in_=causal[:, (NT - 1) * P:], compare_op=ALU.is_ge,
                               fill=MASKED, base=0, pattern=[[-1, P]], channel_multiplier=1
                               ).then_inc(S["const_ready"], 1)
            pool.iota(expert_id[:], pattern=[[1, NE]], base=0, channel_multiplier=0,
                      allow_small_or_imprecise_dtypes=True).then_inc(S["const_ready"], 1)
            pool.wait_ge(S["out_free"], 8)
            for n, row in enumerate((bv_bc, base_bc, bo_bc)):
                pool.dma_start(row, bias_rows[n].partition_broadcast(P)).then_inc(S["bias_landed"], 16)
            pool.memset(kst[:, 0].rearrange("p b n -> p (b n)").bitcast(F32), 1.0).then_inc(S["k_ones"], 1)
            pool.memset(v_sb[:], 1.0).then_inc(S["k_ones"], 1)
            pool.wait_ge(S["bias_landed"], 48)
            pool.tensor_tensor(bo_bc, bo_bc, base_bc, ALU.add).then_inc(S["k_ones"], 1)
            pool.wait_ge(S["k_ones"], 3)
            for t in range(NT):
                pool.wait_ge(S["y_free"], t + 1)
                pool.tensor_tensor(x_sb[:, t, :], x_sb[:, t, :], bo_bc, ALU.add).then_inc(S["y_biased"], 1)
            pool.wait_ge(S["y_done"], NT)
            pool.memset(kst[:, 1:3].rearrange("p a b n -> p (a b n)").bitcast(F32), 1.0).then_inc(S["kst2"], 1)
            for g in range(GROUPS):
                for s, (half, j) in enumerate(QSTEPS):
                    if j >= HT * half:
                        b = GH * (STEPS * g + s)
                        pool.wait_ge(S["exp_done"], b + GH)
                        part = probs[:, b % NPROB:b % NPROB + GH, 0:P]
                        pool.affine_select(out=part, in_=part, compare_op=ALU.is_ge, fill=0.0, base=0,
                                           pattern=[[0, GH], [1, P]], channel_multiplier=-1
                                           ).then_inc(S["masked"], 1)

        @block.scalar
        def _(act):
            def split_hi(n):
                dest, name = ITEMS[n]
                act.wait_ge(S[f"w_landed{n % 2}"], 16 * (n // 2 + 1))
                if dest == "ring" and ring_at[n] >= 2:
                    act.wait_ge(*ring_done(ring_at[n] - 2))
                if dest in ("v0", "base0"):
                    act.wait_ge(S["out_free"], 8)
                if dest == "wo0":
                    act.wait_ge(S["k_ready"], KD)
                act.activation(destination(n)[0], stage[:, n % 2, :], ACT.Copy).then_inc(S["w_hi"], 1)

            def std(quad):
                act.wait_ge(S["stat_ready"], quad + 1)
                t = HT * (quad % 2)
                if quad == 0:
                    act.wait_ge(S["const_ready"], 1)
                act.activation(rstd[:, t:t + HT], mean_var[:, t:t + HT, 1], ACT.Sqrt, bias=eps_col[:, 0:1]
                               ).then_inc(S["std_ready"], 1)

            def turned_hi(q):
                t = 2 * (q % 4) * P
                act.wait_ge(S["x_turned"], q + 1)
                act.activation(xt_hi[:, :, t:t + 2 * P].rearrange("p k (t n) -> p t k n", t=2),
                               slot_of(("x", q))[:].rearrange("p t (k n) -> p t k n", k=KD), ACT.Copy
                               ).then_inc(S["xt_hi_ready"], 1)

            def term(half, o):
                k = 7 * half + o
                if o == 0:
                    act.wait_ge(S["s_ready"], half + 1)
                else:
                    act.wait_ge(S["t_f"], 6 * half + o)
                if k >= 3:
                    act.wait_ge(S["t_used"], k - 2)
                src = slot_of(("s", half))[:, 1, :] if o == 0 else term_f[:, o % 2, :]
                act.activation(term_hi[:, k % 3, :], src, ACT.Copy).then_inc(S["t_hi"], 1)

            act.wait_ge(S["ratio_diff"], 1)
            act.activation(ratio[:], disc[:], ACT.Exp).then_inc(S["ratio_ready"], 1)
            std(0)
            for n in range(1):
                split_hi(n)
            turned_hi(0)
            turned_hi(1)
            for n in range(1, 3):
                split_hi(n)
            for half in range(2):
                term(half, 0)
                for c in range(FC):
                    if c + 1 < FC:
                        split_hi(item_at[(f"ffn{c + 1}", half)])
                        if half == 0:
                            split_hi(item_at[(f"res{c + 1}", 0)])
                    elif half == 0:
                        split_hi(item_at[("gate_up", 1)])
                    else:
                        split_hi(item_at[("qk0", 0)])
                    k = half * FC + c
                    m = FSHORT if c == 0 else P
                    if c == 1:
                        act.wait_ge(S["hw_f_ready"], half + 1)
                        act.activation(hw_hi[:], lora_h[:], ACT.Copy).then_inc(S["hw_hi_ready"], 1)
                    act.wait_ge(S["f_ready"], k + 1)
                    if k >= 1:
                        act.wait_ge(S["h_f_ready"], k)
                    act.activation(silu[0:m, :], slot_of(("f", k))[0:m, 0, :], ACT.Silu).then_inc(S["silu_ready"], 1)
                    act.wait_ge(S["h_f_ready"], k + 1)
                    if k >= 2:
                        act.wait_ge(S["h_used"], k - 1)
                    act.activation(h_hi[0:m, c % 2, :], h_f[0:m, :], ACT.Copy).then_inc(S["h_hi_ready"], 1)
                    if c == 0:
                        act.wait_ge(S["l_a_ready"], half + 1)
                        act.activation(lora_h[:], slot_of(("l", half))[:, 0, :], ACT.Copy
                                       ).then_inc(S["lora_h_ready"], 1)
                        act.wait_ge(S["const_ready"], 2)
                        act.wait_ge(S["logit_ready"], half + 1)
                        act.activation(prob[:, 0:HT, 0:NE], logit[:, 0:HT, 0:NE], ACT.Exp).then_inc(S["exp_ready"], 1)
                    if 1 <= c <= ORDERS:
                        term(half, c)
                    if c == 2:
                        std(1 + half)
                    if c in X_AFTER:
                        turned_hi(2 + 2 * half + X_AFTER.index(c))
                    if c == FC - 1:
                        if half == 0:
                            split_hi(item_at[("ffn0", 1)])
                        else:
                            split_hi(item_at[("lora1", 0)])

            std(3)
            turned_hi(6)
            turned_hi(7)
            for name in ("wv0", "wv1", "base0", "base1"):
                split_hi(item_at[(name, 0)])

            def project_hi(which, m):
                bias = vec_sb[:, VEC_Q + m:VEC_Q + m + 1] if which == "q" else vec_sb[:, VEC_K + m:VEC_K + m + 1]
                act.wait_ge(S[f"{which}_ready"], m + 1)
                if m >= 1:
                    for g in (2 * m - 2, 2 * m - 1):
                        act.wait_ge(S[f"stacks{g % 3}"], 16 * 6 * GH * (g // 3 + 1))
                act.activation(nat[which, 0], slot_of((which, m))[:].rearrange("p a n -> p (a n)"), ACT.Identity,
                               bias=bias).then_inc(S[f"{which}_hi"], 1)

            def neg_max_hi(g):
                act.wait_ge(S["m_ready"], g + 1)
                if g >= 2:
                    act.wait_ge(S["negm_landed"], 16 * 2 * GH * (g - 1))
                act.activation(negm[:, g % 2, 0, :], slot_of(("m", g))[0:GH * NT, 0, 0:P], ACT.Copy, scale=-1.0
                               ).then_inc(S["m_hi"], 1)

            def take_u(g, half):
                e = 2 * g + half
                act.wait_ge(S["pv_done"], STEPS * g + HT + NT * half)
                if g >= 1:
                    act.wait_ge(S[f"u_landed{half}"], 16 * 2 * GH * g)
                act.activation(u_sb[:, e % 2, :], bank[3][:], ACT.Copy).then_inc(S["u_free"], 1)

            def attn_split_hi(m, half):
                k = 2 * m + half
                act.wait_ge(S["attn_f"], k + 1)
                if m == 2:
                    act.wait_ge(S["stacks0"], 16 * 6 * GH * 3)
                    act.wait_ge(S["stacks1"], 16 * 6 * GH * 3)
                at = slice(half * HALF, (half + 1) * HALF)
                act.activation(attn_hi[:, m, at], u_all[:, at], ACT.Copy).then_inc(S["attn_hi_ready"], 1)

            project_hi("q", 0)
            project_hi("k", 0)
            act.wait_ge(S["a_ready"], 1)
            act.activation(lora_h1, slot_of(("a", 0))[:].rearrange("p a n -> p (a n)"), ACT.Copy
                           ).then_inc(S["a_free"], 1)
            act.wait_ge(S["logit_ready"], 3)
            act.activation(prob[:, :, 0:ROUTES], logit[:, :, 0:ROUTES], ACT.Exp).then_inc(S["exp_ready"], 1)
            act.wait_ge(S["w_free"], 1)
            act.activation(hw1[0], hw_f1, ACT.Copy).then_inc(S["hw_hi_ready"], 1)
            neg_max_hi(0)
            split_hi(item_at[("qk1", 0)])
            for g in range(GROUPS):
                for s, (half, j) in enumerate(QSTEPS):
                    if s == HT + LAG:
                        take_u(g, 0)
                    if s == LAG and g > 0:
                        take_u(g - 1, 1)
                    n = HALF - max(0, P * j - HALF * half)
                    for hh in range(GH):
                        b = GH * (STEPS * g + s) + hh
                        act.wait_ge(S["st_ready"], b + 1)
                        if b >= NPROB:
                            act.wait_ge(S["pv_done"], (b - NPROB) // GH + 1)
                        act.activation(probs[:, b % NPROB, 0:n], bank[b % 3][:, 0:n], ACT.Exp, scale=HD ** -0.5
                                       ).then_inc(S["exp_done"], 1)
                    for kind, k in extras(g, s):
                        if kind in ("q", "k"):
                            project_hi(kind, k)
                        if kind == "m":
                            neg_max_hi(k)
                    if g % 2 == 0 and g > 0 and s in (5, 6):
                        attn_split_hi(g // 2 - 1, s - 5)
                    if s == 10 and g in (0, 2, 4):
                        for name in {0: ["qk2"], 2: ["qk3"], 4: ["wo0", "wo1"]}[g]:
                            split_hi(item_at[(name, 0)])
            take_u(GROUPS - 1, 1)
            for half in range(2):
                attn_split_hi(KD - 1, half)

        @block.tensor
        def _(pe):
            def product(out_ap, a, b, start, stop):
                pe.matmul(out_ap, a[0], b[0], start=start, stop=False)
                pe.matmul(out_ap, a[0], b[1], start=False, stop=False)
                return pe.matmul(out_ap, a[1], b[0], start=False, stop=stop)

            xt = (xt_hi, xt_lo)

            def turn(q):
                src = xn if q < 4 + 2 else xn1
                wait_slot(pe, ("x", q))
                for n in range(2):
                    pe.wait_ge(S["xn_ready"], 2 * q + n + 1)
                    for k in range(KD):
                        last = pe.transpose(slot_of(("x", q))[:, n, k * P:(k + 1) * P],
                                            src[:, n, k * P:(k + 1) * P], ident[:])
                last.then_inc(S["x_turned"], 1)

            def from_xt(dst, w, m0, m1, tok0, n, last_sem=None):
                for k in range(KD):
                    last = product(dst, (w[0][:, k, m0:m1], w[1][:, k, m0:m1]),
                                   (xt_hi[:, k, tok0:tok0 + n], xt_lo[:, k, tok0:tok0 + n]), k == 0, k == KD - 1)
                return last

            def weight(name, half=0):
                n, hi, lo = ring_of(name, half)
                pe.wait_ge(S["w_lo"], n + 1)
                return tuple(t.rearrange("p (k m) -> p k m", k=KD) for t in (hi, lo))

            pe.wait_ge(S["ident_ready"], 2)
            turn(0)
            turn(1)
            for half in range(2):
                tok0 = half * HALF
                pe.wait_ge(S["x_free"], 2 + 2 * half)
                w = weight("gate_up", half)
                ps = slot_of(("s", half))
                wait_slot(pe, ("s", half))
                from_xt(ps[:, 0, :], w, 0, P, tok0, HALF)
                from_xt(ps[:, 1, :], w, P, 2 * P, tok0, HALF).then_inc(S["s_ready"], 1)

                def out_products(a, names, sem_name, start=False, stop=False, k_rows=P):
                    for t in range(HT):
                        last = product(bank[t][:, :], (a[0][0:k_rows, t * P:(t + 1) * P], a[1][0:k_rows, t * P:(t + 1) * P]),
                                       tuple(x[0:k_rows] for x in res(names)), start, stop)
                    if sem_name:
                        last.then_inc(S[sem_name], 1)
                    return last

                def down(c):
                    k = half * FC + c
                    pe.wait_ge(S["f_free"], k + 1)
                    pe.wait_ge(S["w_lo"], res_item(f"down{c}") + 1)
                    if c == 0 and half == 1:
                        pe.wait_ge(S["out_free"], HT)
                    last = out_products((h_hi[:, c % 2, :], h_lo[:, c % 2, :]), f"down{c}", "h_used",
                                        start=(c == 0), stop=(c == FC - 1), k_rows=FSHORT if c == 0 else P)
                    return last

                def res_item(name):
                    return item_at[(f"res{RES_AT[name] // 2}", 0)]

                for c in range(FC):
                    k = half * FC + c
                    w = weight(f"ffn{c}", half)
                    wait_slot(pe, ("f", k))
                    ps = slot_of(("f", k))
                    mg, mu = (FSHORT + NE, FSHORT) if c == 0 else (P, P)
                    from_xt(ps[0:mg, 0, :], w, 0, mg, tok0, HALF)
                    from_xt(ps[0:mu, 1, :], w, P, P + mu, tok0, HALF).then_inc(S["f_ready"], 1)
                    if c == 0:
                        wait_slot(pe, ("l", half))
                        pe.wait_ge(S["w_lo"], res_item("lora_a") + 1)
                        ps = slot_of(("l", half))
                        w = tuple(t.rearrange("p (k m) -> p k m", k=KD) for t in res("lora_a"))
                        from_xt(ps[:, 0, :], w, 0, P, tok0, HALF)
                        pe.wait_ge(S["lgt_ready"], half + 1)
                        for t in range(HT):
                            last = pe.transpose(ps[:, 1, t * NE:(t + 1) * NE], lgt[FSHORT:FSHORT + NE, t * P:(t + 1) * P],
                                                ident[FSHORT:FSHORT + NE, FSHORT:FSHORT + NE])
                        last.then_inc(S["l_a_ready"], 1)
                    if c == 1:
                        pe.wait_ge(S["gate_ready"], half + 1)
                        ps = slot_of(("l", half))
                        for t in range(HT):
                            last = pe.transpose(ps[:, 1, t * P:(t + 1) * P],
                                                gate_x[:, t].rearrange("p e r -> p (e r)"), ident[:])
                        last.then_inc(S["l_b_ready"], 1)
                    if c in X_AFTER:
                        turn(2 + 2 * half + X_AFTER.index(c))
                    if c >= 1:
                        down(c - 1)
                        if c - 1 <= ORDERS:
                            o = 7 * half + c - 1
                            pe.wait_ge(S["t_lo"], o + 1)
                            out_products((term_hi[:, o % 3, :], term_lo[:, o % 3, :]), f"term{c - 1}", "t_used")
                    if c == FC - 2:
                        pe.wait_ge(S["l_free"], half + 1)
                        out_products((hw_hi, hw_lo), "lora_b", None)
                down(FC - 1)
            turn(6)
            turn(7)

            def project(which, m):
                w = weight(f"qk{m}")
                if m == 0:
                    pe.wait_ge(S["x_free"], 8)
                at = 0 if which == "q" else P
                wait_slot(pe, (which, m))
                for n in range(2):
                    last = from_xt(slot_of((which, m))[:, n, :], w, at, at + P, n * HALF, HALF)
                last.then_inc(S[f"{which}_ready"], 1)

            project("q", 0)
            project("k", 0)
            wait_slot(pe, ("r", 0))
            pe.wait_ge(S["rw_ready"], 1)
            for n in range(2):
                last = from_xt(slot_of(("r", 0))[0:ROUTES_PAD, n, :], (rw_hi, rw_lo), 0, ROUTES_PAD, n * HALF, HALF)
            last.then_inc(S["r_ready"], 1)
            w1 = weight("lora1")
            wait_slot(pe, ("a", 0))
            n1, hi1, lo1 = ring_of("lora1")
            a1 = tuple(t[:, 0:D].rearrange("p (k m) -> p k m", k=KD) for t in (hi1, lo1))
            b1 = (hi1[:, D:], lo1[:, D:])
            for n in range(2):
                last = from_xt(slot_of(("a", 0))[:, n, :], a1, 0, P, n * HALF, HALF)
            last.then_inc(S["a_ready"], 1)
            pe.wait_ge(S["r_free"], 1)
            pe.wait_ge(S["out_free"], 8)
            for t in range(NT):
                last = pe.transpose(bank[0][:, t * ROUTES_PAD:(t + 1) * ROUTES_PAD], lgt1[:, t * P:(t + 1) * P],
                                    ident[0:ROUTES_PAD, 0:ROUTES_PAD])
            last.then_inc(S["lt_ready"], 1)

            def maxima(u):
                g, i, hh = u // UNITS, u % UNITS // GH, u % GH
                wait_slot(pe, ("max", u))
                if u % UNITS == 0:
                    pe.wait_ge(S[f"stacks{g % 3}"], 16 * 6 * GH * (g // 3 + 1))
                at = 64 * (hh % 2)
                n = (i + 1) * P
                for b in range(-(-n // 512)):
                    c = min(n, 512 * (b + 1))
                    last = pe.matmul(slot_of(("max", u))[:, b, 0:c - 512 * b],
                                     qst[at:at + QK_ROWS, g % 3, hh // 2, i * P:(i + 1) * P],
                                     kst[at:at + QK_ROWS, g % 3, hh // 2, 512 * b:c], start=True, stop=True)
                last.then_inc(S["max_ready"], 1)

            def turn_maxima(g):
                pe.wait_ge(S["max_free"], UNITS * (g + 1))
                wait_slot(pe, ("m", g))
                pe.transpose(slot_of(("m", g))[0:GH * NT, 0, 0:P],
                             maxcol[:, g % 2].rearrange("p h i -> p (h i)"), ident[:]).then_inc(S["m_ready"], 1)

            def values(t):
                if t >= 2:
                    pe.wait_ge(S["v_free"], t - 1)
                for k in range(KD):
                    last = product(bank[2 * (t % 2)][:, :], tuple(x[:, k, t * P:(t + 1) * P] for x in xt),
                                   tuple(x[:, k, :] for x in v_w), k == 0, k == KD - 1)
                last.then_inc(S["v_done"], 1)

            def linear(t):
                if t >= 2:
                    pe.wait_ge(S["y_free"], t - 1)
                dst = bank[2 * (t % 2) + 1][:, :]
                for k in range(KD):
                    product(dst, tuple(x[:, k, t * P:(t + 1) * P] for x in xt), tuple(x[:, k, :] for x in base_w),
                            k == 0, False)
                product(dst, tuple(x[:, t * P:(t + 1) * P] for x in hw1), b1, False, True
                        ).then_inc(S["y_done"], 1)

            pe.wait_ge(S["gate_ready"], 3)
            wait_slot(pe, ("w", 0))
            for t in range(NT):
                last = pe.transpose(slot_of(("w", 0))[:, t // 4, t % 4 * P:(t % 4 + 1) * P],
                                    gate_x1[:, t].rearrange("p e r -> p (e r)"), ident[:])
            last.then_inc(S["w_ready"], 1)
            pe.wait_ge(S["w_lo"], item_at[("base1", 0)] + 1)
            for t in range(NT):
                values(t)
                if t == 0:
                    pe.wait_ge(S["hw1_ready"], 1)
                linear(t)
                for u in range(GH * t, GH * (t + 1)):
                    maxima(u)
            turn_maxima(0)

            def score(g, s, hh):
                half, j = QSTEPS[s]
                b = GH * (STEPS * g + s) + hh
                q0 = max(P * j, HALF * half)
                n = HALF * (half + 1) - q0
                at = 64 * (hh % 2)
                if b >= 3:
                    pe.wait_ge(S["exp_done"], b - 2)
                else:
                    pe.wait_ge(S["v_free"], NT)
                    pe.wait_ge(S["y_free"], NT)
                if s == 0 and hh == 0:
                    pe.wait_ge(S["negm_landed"], 16 * 2 * GH * (g + 1))
                pe.matmul(bank[b % 3][:, 0:n], kst[at:at + ST_ROWS, g % 3, hh // 2, j * P:(j + 1) * P],
                          qst[at:at + ST_ROWS, g % 3, hh // 2, q0:q0 + n], start=True, stop=True
                          ).then_inc(S["st_ready"], 1)

            def weigh_values(k):
                g, s = k // STEPS, k % STEPS
                half, j = QSTEPS[s]
                c0 = max(0, P * j - HALF * half)
                pe.wait_ge(S["exp_done"], GH * (k + 1))
                if j >= HT * half:
                    pe.wait_ge(S["masked"], NT * g + j + 1)
                if j == 0 and 2 * g + half > 0:
                    pe.wait_ge(S["u_free"], 2 * g + half)
                stop = j == HT * (half + 1) - 1
                for hh in range(GH):
                    last = pe.matmul(bank[3][32 * hh:32 * hh + HD + 1, c0:HALF], v_sb[:, j, GH * g + hh, :],
                                     probs[:, (GH * k + hh) % NPROB, 0:HALF - c0], start=(j == 0), stop=stop)
                last.then_inc(S["pv_done"], 1)
                return last


            def out_project(t, ks):
                for k in ks:
                    last = product(o_bank(t), tuple(x[:, k, t * P:(t + 1) * P] for x in (attn_hi, attn_lo)),
                                   tuple(x[:, k, :] for x in wo_w), k == 0, k == KD - 1)
                return last

            for g in range(GROUPS):
                for s in range(STEPS):
                    for hh in range(GH):
                        score(g, s, hh)
                    k = STEPS * g + s - LAG
                    if k >= 0:
                        weigh_values(k)
                    for kind, u in extras(g, s):
                        if kind == "max":
                            maxima(u)
                        elif kind == "m":
                            turn_maxima(u)
                        elif kind in ("q", "k"):
                            project(kind, u)
                        elif kind == "o":
                            if u == 0:
                                pe.wait_ge(S["attn_lo_ready"], 2 * (KD - 1))
                                pe.wait_ge(S["w_lo"], len(ITEMS))
                            wait_slot(pe, ("o", u))
                            for t in (2 * u, 2 * u + 1):
                                out_project(t, range(KD - 1))
            for k in range(STEPS * GROUPS - LAG, STEPS * GROUPS):
                weigh_values(k)
            pe.wait_ge(S["exp_done"], GH * STEPS * GROUPS)
            pe.wait_ge(S["u_free"], 2 * GROUPS)
            for t in range(4, NT):
                out_project(t, range(KD - 1))
            pe.wait_ge(S["attn_lo_ready"], 2 * KD)
            for t in range(NT):
                out_project(t, [KD - 1]).then_inc(S["o_ready"], 1)

        @block.vector
        def _(dve):
            chain = [0]

            def then(ins):
                chain[0] += 1
                ins.then_inc(S["dve"], 1)
                dve.wait_ge(S["dve"], chain[0])

            def split_lo(n):
                dve.wait_ge(S["w_hi"], n + 1)
                hi, lo = destination(n)
                dve.tensor_tensor(lo, stage[:, n % 2, :], hi.bitcast(F32), ALU.subtract).then_inc(S["w_lo"], 1)

            def statistics(quad):
                t0 = HT * (quad % 2)
                for t in range(t0, t0 + HT):
                    if quad >= 2:
                        dve.wait_ge(S["out_free"], (quad - 1) * HT)
                    else:
                        dve.wait_ge(S[f"x_landed{(0, 1, 2, 2, 3, 3, 3, 3)[t]}"], 16)
                    last = dve.bn_stats(stats[:, t, :], x_sb[:, t, :])
                then(last)
                for t in range(t0, t0 + HT):
                    last = dve.bn_aggr(mean_var[:, t, :], stats[:, t, :])
                last.then_inc(S["stat_ready"], 1)

            def invert_std(quad):
                t0 = HT * (quad % 2)
                dve.wait_ge(S["std_ready"], quad + 1)
                then(dve.reciprocal(rstd[:, t0:t0 + HT], rstd[:, t0:t0 + HT]))

            def normalize(q):
                dst = xn if q < 6 else xn1
                if q >= 1:
                    dve.wait_ge(S["x_turned"], q)
                for n in range(2):
                    t = 2 * (q % 4) + n
                    dve.tensor_scalar(dst[:, n, :], x_sb[:, t, :], mean_var[:, t, 0:1], rstd[:, t:t + 1],
                                      ALU.subtract, ALU.mult).then_inc(S["xn_ready"], 1)

            def turned_lo(q):
                t = 2 * (q % 4) * P
                dve.wait_ge(S["xt_hi_ready"], q + 1)
                for n in range(2):
                    at = (slice(None), slice(None), slice(t + n * P, t + (n + 1) * P))
                    last = dve.tensor_tensor(xt_lo[at], slot_of(("x", q))[:, n, :].rearrange("p (k n) -> p k n", k=KD),
                                             xt_hi[at].bitcast(F32), ALU.subtract)
                last.then_inc(S["x_free"], 1)

            def wide(ap, *dims):
                return bass.AP(ap.tensor, ap.offset, [ap.ap[0], *[list(d) for d in dims]])

            def route(n_tok, routes, e):
                src = slot_of(("l", e))[:, 1, 0:HT * NE] if e < 2 else bank[0][:, 0:NT * ROUTES_PAD]
                w = NE if e < 2 else ROUTES_PAD
                src = src.rearrange("p (t e) -> p t e", e=w)[:, :, 0:routes]
                then(dve.tensor_reduce(rowmax[:, 0:n_tok], src, AX.X, ALU.max))
                dve.tensor_tensor(logit[:, 0:n_tok, 0:routes], src,
                                  wide(rowmax[:, 0:n_tok], (1, n_tok), (0, routes)), ALU.subtract
                                  ).then_inc(S["logit_ready"], 1)
                dve.wait_ge(S["exp_ready"], e + 1)
                for t in range(n_tok):
                    last = dve.max(top[:, t, :], prob[:, t, 0:routes])
                then(last)
                if e < 2:
                    then(dve.memset(top[:, 0:n_tok, 2:8], -1.0))
                span = ROUTES_PAD if e < 2 else ROUTES
                for t in range(n_tok):
                    last = dve.match_replace(rest[:, t, 0:span], top[:, t, :], prob[:, t, 0:span], 0.0)
                then(last)
                then(dve.tensor_tensor(chosen[:, 0:n_tok, 0:routes], prob[:, 0:n_tok, 0:routes],
                                       rest[:, 0:n_tok, 0:routes], ALU.subtract))
                over = chosen if e < 2 else prob
                then(dve.tensor_reduce(norm[:, 0:n_tok], over[:, 0:n_tok, 0:routes], AX.X, ALU.add))
                then(dve.reciprocal(norm[:, 0:n_tok], norm[:, 0:n_tok]))
                then(dve.tensor_scalar(norm[:, 0:n_tok], norm[:, 0:n_tok], SCALE0 if e < 2 else SCALE1, None, ALU.mult))

            def spread(dst, src, n_tok):
                for t in range(n_tok):
                    last = dve.tensor_scalar(dst[:, t], wide(src[:, t, 0:NE], (1, NE), (0, RANK)), norm[:, t:t + 1],
                                             None, ALU.mult)
                last.then_inc(S["gate_ready"], 1)

            statistics(0)
            dve.wait_ge(S["vec_landed"], 64)
            then(dve.tensor_copy(ratio[:, 1:], disc[:, 0:ORDERS - 1]))
            then(dve.memset(ratio[:, 0:1], 0.0))
            dve.tensor_tensor(disc[:], ratio[:], disc[:], ALU.subtract).then_inc(S["ratio_diff"], 1)
            invert_std(0)
            normalize(0)
            normalize(1)
            split_lo(0)
            turned_lo(0)
            turned_lo(1)
            split_lo(1)
            split_lo(2)
            dve.wait_ge(S["const_ready"], 3)
            dve.wait_ge(S["ratio_ready"], 1)

            def later_term(half, o):
                k = 7 * half + o
                if o >= 2:
                    ins = dve.scalar_tensor_tensor(term_f[:, o % 2, :], delta[:], ratio[:, o - 1:o],
                                                   term_f[:, (o - 1) % 2, :], ALU.mult, ALU.mult)
                    if o == ORDER_MIN + 1:
                        then(ins)
                        ins = dve.tensor_tensor(term_f[:, o % 2, :], term_f[:, o % 2, :], keep[:], ALU.mult)
                    ins.then_inc(S["t_f"], 1)
                dve.wait_ge(S["t_hi"], k + 1)
                dve.tensor_tensor(term_lo[:, k % 3, :], term_f[:, o % 2, :], term_hi[:, k % 3, :].bitcast(F32),
                                  ALU.subtract).then_inc(S["t_lo"], 1)

            def lora_weighted(half):
                dve.wait_ge(S["l_b_ready"], half + 1)
                dve.wait_ge(S["lora_h_ready"], half + 1)
                dve.tensor_tensor(lora_h[:], slot_of(("l", half))[:, 1, :], lora_h[:], ALU.mult
                                  ).then_inc(S["hw_f_ready"], 1)
                dve.wait_ge(S["hw_hi_ready"], half + 1)
                dve.tensor_tensor(hw_lo[:], lora_h[:], hw_hi[:].bitcast(F32), ALU.subtract).then_inc(S["l_free"], 1)

            def take_out(half):
                for t in range(HT):
                    dve.tensor_tensor(x_sb[:, half * HT + t, :], bank[t][:, :], x_sb[:, half * HT + t, :], ALU.add
                                      ).then_inc(S["out_free"], 1)

            for half in range(2):
                ps = slot_of(("s", half))
                dve.wait_ge(S["s_ready"], half + 1)
                then(dve.tensor_scalar(delta[:], ps[:, 0, :], vec_sb[:, VEC_POINT:VEC_POINT + 1], None, ALU.subtract))
                then(dve.scalar_tensor_tensor(keep[:], delta[:], -1.0, delta[:], ALU.mult, ALU.max))
                dve.tensor_scalar(keep[:], keep[:], DELTA_MAX, None, ALU.is_le)
                k = 7 * half
                dve.wait_ge(S["t_hi"], k + 1)
                dve.scalar_tensor_tensor(term_f[:, 1, :], delta[:], ratio[:, 0:1], ps[:, 1, :], ALU.mult, ALU.mult
                                         ).then_inc(S["t_f"], 1)
                dve.tensor_tensor(term_lo[:, k % 3, :], ps[:, 1, :], term_hi[:, k % 3, :].bitcast(F32), ALU.subtract
                                  ).then_inc(S["t_lo"], 1)
                if half == 1:
                    dve.wait_ge(S["h_used"], FC)
                    take_out(0)
                for c in range(FC):
                    if c + 1 < FC:
                        split_lo(item_at[(f"ffn{c + 1}", half)])
                        if half == 0:
                            split_lo(item_at[(f"res{c + 1}", 0)])
                    elif half == 0:
                        split_lo(item_at[("gate_up", 1)])
                    else:
                        split_lo(item_at[("qk0", 0)])
                    k = half * FC + c
                    m = FSHORT if c == 0 else P
                    ps = slot_of(("f", k))
                    if c == 1:
                        lora_weighted(half)
                    if c == 0:
                        dve.wait_ge(S["f_ready"], k + 1)
                        dve.tensor_scalar(lgt[FSHORT:FSHORT + NE, :], ps[FSHORT:FSHORT + NE, 0, :],
                                          vec_sb[FSHORT:FSHORT + NE, VEC_ROUTER0:VEC_ROUTER0 + 1], None, ALU.add
                                          ).then_inc(S["lgt_ready"], 1)
                    dve.wait_ge(S["silu_ready"], k + 1)
                    if k >= 1:
                        dve.wait_ge(S["h_hi_ready"], k)
                        dve.wait_ge(S["f_free"], k)
                    dve.tensor_tensor(h_f[0:m, :], ps[0:m, 1, :], silu[0:m, :], ALU.mult).then_inc(S["h_f_ready"], 1)
                    dve.wait_ge(S["h_hi_ready"], k + 1)
                    dve.tensor_tensor(h_lo[0:m, c % 2, :], h_f[0:m, :], h_hi[0:m, c % 2, :].bitcast(F32),
                                      ALU.subtract).then_inc(S["f_free"], 1)
                    if c == 0:
                        dve.wait_ge(S["l_a_ready"], half + 1)
                        route(HT, NE, half)
                        spread(gate_x, chosen, HT)
                    if 1 <= c <= ORDERS:
                        later_term(half, c)
                    if c == 1 and half == 0:
                        statistics(1)
                    if c == 1 and half == 1:
                        statistics(2)
                    if c == 2:
                        invert_std(1 + half)
                        normalize(2 + 2 * half)
                    if c in X_AFTER:
                        q = 2 + 2 * half + X_AFTER.index(c)
                        turned_lo(q)
                        if q % 2 == 0:
                            normalize(q + 1)
                    if c == FC - 1:
                        if half == 0:
                            split_lo(item_at[("ffn0", 1)])
                        else:
                            split_lo(item_at[("lora1", 0)])
            dve.wait_ge(S["h_used"], 2 * FC)
            take_out(1)
            statistics(3)
            invert_std(3)
            normalize(6)
            normalize(7)
            turned_lo(6)
            turned_lo(7)
            then(dve.tensor_copy(rw_hi[:].rearrange("p k n -> p (k n)"), rw_stage[:]))
            dve.tensor_tensor(rw_lo[:].rearrange("p k n -> p (k n)"), rw_stage[:],
                              rw_hi[:].rearrange("p k n -> p (k n)").bitcast(F32), ALU.subtract
                              ).then_inc(S["rw_ready"], 1)
            dve.wait_ge(S["const_ready"], 5)
            then(dve.tensor_copy(map_f[:], map_i[:]))
            then(dve.tensor_tensor(onehot[:], wide(map_f[:], (0, NE), (1, ROUTES)),
                                   wide(expert_id[:], (1, NE), (0, ROUTES)), ALU.is_equal))
            for name in ("wv0", "wv1", "base0", "base1"):
                split_lo(item_at[(name, 0)])

            def project_lo(which, m):
                col = (VEC_Q if which == "q" else VEC_K) + m
                dve.wait_ge(S[f"{which}_hi"], m + 1)
                dve.scalar_tensor_tensor(nat[which, 1], slot_of((which, m))[:].rearrange("p a n -> p (a n)"),
                                         vec_sb[:, col:col + 1], nat[which, 0].bitcast(F32), ALU.add, ALU.subtract
                                         ).then_inc(S[f"{which}_free"], 1)

            project_lo("q", 0)
            project_lo("k", 0)
            dve.wait_ge(S["r_ready"], 1)
            dve.tensor_scalar(lgt1, slot_of(("r", 0))[0:ROUTES_PAD].rearrange("p a n -> p (a n)"),
                              vec_sb[0:ROUTES_PAD, VEC_ROUTER1:VEC_ROUTER1 + 1], None, ALU.add
                              ).then_inc(S["r_free"], 1)
            dve.wait_ge(S["lt_ready"], 1)
            route(NT, ROUTES, 2)
            for t in range(NT):
                prod = hw_f1[:, t * NE * ROUTES:(t + 1) * NE * ROUTES].rearrange(
                    "p (e n) -> p e n", e=NE)
                last = dve.tensor_tensor(prod, wide(chosen[:, t, 0:ROUTES], (0, NE), (1, ROUTES)), onehot[:], ALU.mult)
            then(last)
            then(dve.tensor_reduce(gate[:].rearrange("p t e -> p (t e)"),
                                   hw_f1[:, 0:NT * NE * ROUTES].rearrange("p (e n) -> p e n", n=ROUTES), AX.X, ALU.add))
            spread(gate_x1, gate, NT)
            dve.wait_ge(S["w_ready"], 1)
            dve.wait_ge(S["a_free"], 1)
            dve.tensor_tensor(hw_f1, slot_of(("w", 0))[:].rearrange("p a n -> p (a n)"), lora_h1, ALU.mult
                              ).then_inc(S["w_free"], 1)
            dve.wait_ge(S["hw_hi_ready"], 3)
            dve.tensor_tensor(hw1[1], hw_f1, hw1[0].bitcast(F32), ALU.subtract
                              ).then_inc(S["hw1_ready"], 1)
            dve.wait_ge(S["bias_landed"], 48)
            dve.wait_ge(S["k_ones"], 2)

            def row_max(u):
                g, i, hh = u // UNITS, u % UNITS // GH, u % GH
                n = (i + 1) * P
                dve.wait_ge(S["max_ready"], u + 1)
                if g >= 2 and u % UNITS == 0:
                    dve.wait_ge(S["m_ready"], g - 1)
                score = slot_of(("max", u))[:].rearrange("p a n -> p (a n)")[:, 0:n]
                dve.tensor_tensor_reduce(score, score, causal[:, NT * P - n:], 1.0, -3.0e38, ALU.add, ALU.max,
                                         maxcol[:, g % 2, hh, i:i + 1]).then_inc(S["max_free"], 1)

            def neg_max_lo(g):
                dve.wait_ge(S["m_hi"], g + 1)
                dve.scalar_tensor_tensor(negm[:, g % 2, 1, :], slot_of(("m", g))[0:GH * NT, 0, 0:P], -1.0,
                                         negm[:, g % 2, 0, :].bitcast(F32), ALU.mult, ALU.subtract
                                         ).then_inc(S["m_free"], 1)

            def divide(m, half):
                k = 2 * m + half
                at = slice(half * HALF, (half + 1) * HALF)
                dve.wait_ge(S[f"u_landed{half}"], 16 * 2 * GH * (2 * m + 2))
                then(dve.reciprocal(den_all[:, at], den_all[:, at]))
                dve.tensor_tensor(u_all[:, at], u_all[:, at], den_all[:, at], ALU.mult).then_inc(S["attn_f"], 1)

            def attn_split_lo(m, half):
                k = 2 * m + half
                at = slice(half * HALF, (half + 1) * HALF)
                dve.wait_ge(S["attn_hi_ready"], k + 1)
                dve.tensor_tensor(attn_lo[:, m, at], u_all[:, at], attn_hi[:, m, at].bitcast(F32), ALU.subtract
                                  ).then_inc(S["attn_lo_ready"], 1)

            for t in range(NT):
                dve.wait_ge(S["v_done"], t + 1)
                dve.tensor_tensor(v_sb[:, t, :, 0:HD], bank[2 * (t % 2)][:].rearrange("p (h d) -> p h d", d=HD),
                                  bv_bc.rearrange("p (h d) -> p h d", d=HD), ALU.add
                                  ).then_inc(S["v_free"], 1)
                dve.wait_ge(S["y_done"], t + 1)
                dve.tensor_tensor(x_sb[:, t, :], bank[2 * (t % 2) + 1][:, :], x_sb[:, t, :], ALU.add
                                  ).then_inc(S["y_free"], 1)
                for u in range(GH * t, GH * (t + 1)):
                    row_max(u)
            neg_max_lo(0)
            split_lo(item_at[("qk1", 0)])
            for g in range(GROUPS):
                for s in range(STEPS):
                    for kind, k in extras(g, s):
                        if kind == "max":
                            row_max(k)
                        elif kind in ("q", "k"):
                            project_lo(kind, k)
                        elif kind == "m":
                            neg_max_lo(k)
                    if g % 2 == 0 and g > 0:
                        if s in (5, 6):
                            divide(g // 2 - 1, s - 5)
                            attn_split_lo(g // 2 - 1, s - 5)
                    if s == 10 and g in (0, 2, 4):
                        for name in {0: ["qk2"], 2: ["qk3"], 4: ["wo0", "wo1"]}[g]:
                            split_lo(item_at[(name, 0)])
            for half in range(2):
                divide(KD - 1, half)
                attn_split_lo(KD - 1, half)
            dve.wait_ge(S["y_biased"], NT)
            for t in range(NT):
                dve.wait_ge(S["o_ready"], t + 1)
                dve.tensor_tensor(x_sb[:, t, :], o_bank(t), x_sb[:, t, :], ALU.add).then_inc(S["out_sb_ready"], 1)


def kernel(**inputs):
    import concourse.bacc as bacc
    from concourse.bass_utils import run_bass_kernel_spmd

    w = {k: np.asarray(v) for k, v in inputs.items()}
    stream, router1 = lay_out_weights(w)
    vec = np.zeros((P, VECS), np.float32)
    vec[:, VEC_POINT] = w["L0_attn_local_point"]
    vec[FSHORT:FSHORT + NE, VEC_ROUTER0] = w["L0_ffn_router_b"]
    vec[:ROUTES, VEC_ROUTER1] = w["L1_ffn_router_b"]
    vec[:, VEC_Q:VEC_Q + KD] = w["L1_attn_bq"].reshape(KD, P).T
    vec[:, VEC_K:VEC_K + KD] = w["L1_attn_bk"].reshape(KD, P).T
    arrays = {
        "stream": stream, "router1": router1.reshape(P, -1),
        "x": np.ascontiguousarray(w["L0_attn_hidden_states"].reshape(NT, P, D)), "vec": vec,
        "bias_rows": np.stack([w["L1_attn_bv"], w["L1_ffn_base_b"], w["L1_attn_bo"]]),
        "discount": w["L0_attn_discount_factor"], "expert_map": w["L1_ffn_expert_map"],
    }
    nc = bacc.Bacc("TRN2", target_bir_lowering=False, num_devices=1)
    args = [nc.dram_tensor(f"in_{n}", a.shape, mybir.dt.from_np(a.dtype), kind="ExternalInput").ap()
            for n, a in arrays.items()]
    y = nc.dram_tensor("out_y", (NT, P, D), F32, kind="ExternalOutput").ap()
    build(nc, *args, y)
    result = run_bass_kernel_spmd(nc, [{f"in_{n}": a for n, a in arrays.items()}], core_ids=[0])
    return result.results[0]["out_y"].reshape(1, TOK, D)
```

```python
from contextlib import ExitStack

import numpy as np

import concourse.bass as bass
from concourse import mybir

F32 = mybir.dt.float32
F32R = mybir.dt.float32r
BF16 = mybir.dt.bfloat16
I32 = mybir.dt.int32
ALU = mybir.AluOpType
ACT = mybir.ActivationFunctionType
AX = mybir.AxisListType

P = 128
TOK, D = 1024, 512
KD = D // P
NT = TOK // P
HALF = TOK // 2
HT = HALF // P
FF = 1248
FC = -(-FF // P)
FSHORT = FF - (FC - 1) * P
ORDERS = 6
ORDER_MIN = 4
DELTA_MAX = 2.5
NE = 8
RANK = 16
SCALE0 = 8.0 / RANK
SCALE1 = 32.0 / 16.0
ROUTES = 2 * NE - 1
ROUTES_PAD = 16
HEADS, HD = 32, 16
GH = 4
GROUPS = HEADS // GH
QK_ROWS = 3 * HD
SIDE = 64
DOT_ROWS = SIDE + QK_ROWS
ST_ROWS = DOT_ROWS + 2
DEN_COLS = GH * HALF // P
EPS = 1e-5
MASKED = -1.0e30
SLOT = 1024

RESIDENT = ["lora_a", "lora_b"]
for _c in range(7):
    RESIDENT += [f"down{_c}", f"term{_c}"]
RESIDENT += ["down7", "down8", "down9", "pad"]
RES_AT = {name: n for n, name in enumerate(RESIDENT)}


def weight_items():
    items, arrays = [], []

    def add(dest, name):
        if name not in arrays:
            arrays.append(name)
        items.append((dest, name))

    for half in range(2):
        add("ring", "gate_up")
        for c in range(FC):
            add("ring", f"ffn{c}")
            if half == 0:
                add("resident", f"res{c}")
    for m in range(KD):
        add("ring", f"qk{m}")
    add("ring", "lora1")
    for n in range(2):
        add(f"v{n}", f"wv{n}")
    for n in range(2):
        add(f"base{n}", f"base{n}")
    for n in range(2):
        add(f"wo{n}", f"wo{n}")
    return items, arrays


ITEMS, ARRAYS = weight_items()


def lay_out_weights(w):
    def kxm(a):
        t = a.T
        return t.reshape(t.shape[0] // P, P, t.shape[1]).transpose(1, 0, 2)

    ffn_gate, ffn_up = kxm(w["L0_attn_ffn_gate_w"]), kxm(w["L0_attn_ffn_up_w"])
    down = w["L0_attn_ffn_down_w"].T
    router0 = kxm(w["L0_ffn_router_w"])
    out = np.zeros((len(ARRAYS), P, SLOT), np.float32)
    at = {name: n for n, name in enumerate(ARRAYS)}

    def put(name, n, a):
        if a.ndim == 3:
            a = a.reshape(P, -1)
        out[at[name], :a.shape[0], n:n + a.shape[1]] = a

    def pair(name, left, right):
        v = out[at[name]].reshape(P, KD, 2, P)
        v[:, :, 0, :left.shape[2]] = left
        v[:, :, 1, :right.shape[2]] = right

    pair("gate_up", kxm(w["L0_attn_gate_w"]), kxm(w["L0_attn_up_w"]))
    bounds = [0, FSHORT] + [FSHORT + P * c for c in range(1, FC)]
    for c in range(FC):
        a, b = bounds[c], bounds[c + 1]
        left = ffn_gate[:, :, a:b]
        if c == 0:
            left = np.concatenate([left, router0], axis=2)
        pair(f"ffn{c}", left, ffn_up[:, :, a:b])

    def resident(name):
        if name == "lora_a":
            return kxm(w["L0_ffn_A"].reshape(NE * RANK, D)).reshape(P, -1)
        if name == "lora_b":
            return w["L0_ffn_Bm"].transpose(0, 2, 1).reshape(NE * RANK, D)
        if name == "term0":
            return w["L0_attn_local_approx_output"].T
        if name.startswith("term"):
            return w["L0_attn_fuse_weight"][:, :, int(name[4:]) - 1].T
        c = int(name[4:])
        return down[bounds[c]:bounds[c + 1]]

    for n, name in enumerate(RESIDENT):
        if name != "pad":
            put(f"res{n // 2}", (n % 2) * D, resident(name))
    wq, wk = kxm(w["L1_attn_Wq"]), kxm(w["L1_attn_Wk"])
    for m in range(KD):
        pair(f"qk{m}", wq[:, :, m * P:(m + 1) * P], wk[:, :, m * P:(m + 1) * P])
    put("lora1", 0, kxm(w["L1_ffn_A"].reshape(NE * RANK, D)))
    put("lora1", D, w["L1_ffn_B"].transpose(0, 2, 1).reshape(NE * RANK, D))
    for name, a in (("wv", w["L1_attn_Wv"]), ("base", w["L1_ffn_base_W"]), ("wo", w["L1_attn_Wo"])):
        t = kxm(a)
        for n in range(2):
            put(f"{name}{n}", 0, t[:, 2 * n:2 * n + 2])
    router1 = np.zeros((P, KD, ROUTES_PAD), np.float32)
    router1[:, :, :ROUTES] = kxm(w["L1_ffn_router_W"])
    return out, router1

LAG = 2
NPROB = 12
VEC_POINT, VEC_ROUTER0, VEC_ROUTER1, VEC_Q, VEC_K = 0, 1, 2, 3, 3 + KD
VECS = VEC_K + KD


def psum_users():
    users = [("x", 0), ("x", 1)]
    for half in range(2):
        users += [("s", half), ("f", half * FC), ("l", half)]
        for c in range(1, FC):
            users.append(("f", half * FC + c))
            if c in X_AFTER:
                users.append(("x", 2 + 2 * half + X_AFTER.index(c)))
    users += [("r", 0)] + [(which, m) for m in range(KD) for which in ("q", "k")]
    users += [("a", 0), ("w", 0)]
    for g in range(2):
        users += [("max", g * UNITS + u) for u in range(UNITS)] + [("m", g)]
    users = [(user, n % 2) for n, user in enumerate(users)]
    held = None
    last = users[-1][1]
    for g in range(GROUPS):
        for s in range(STEPS):
            for hh in range(GH):
                for kind, k, part in extras(g, s, hh):
                    parts = PARTS.get(kind, 1)
                    if part == 0:
                        last = 1 - last if held is None else 1 - held
                        users.append(((kind, k), last))
                        if parts > 1:
                            held = last
                    if part == parts - 1 and parts > 1:
                        held = None
    return users


X_AFTER = (3, 4)
QSTEPS = [(0, j) for j in (0, 1, 2, 3)] + [(1, j) for j in range(NT)]
DIAGONAL = [s for s, (half, j) in enumerate(QSTEPS) if j >= HT * half]
STEPS = len(QSTEPS)
UNITS = GH * NT
MAX_START = 6
MAX_END = 5
PARTS = {"o": 6}


def step_width(s):
    half, j = QSTEPS[s]
    return HALF - max(0, P * j - HALF * half)


def per_bank(s):
    return {P: 4, 2 * P: 2}.get(step_width(s), 1)


def banks_before(g, s):
    per_group = [GH // per_bank(n) for n in range(STEPS)]
    return g * sum(per_group) + sum(per_group[:s])


VECTOR_COLUMNS = 400


def vector_extras(g, s):
    return 2 * ((g, s) in DIVIDE_AT) + 2 * len(SPLIT_AT.get((g, s), []))


def max_plan():
    plan = {}
    for g in range(2, GROUPS):
        first = STEPS * (g - 2) + MAX_START + (1 if g == 2 else 0)
        places = [(p // STEPS, p % STEPS, hh) for p in range(first, STEPS * (g - 1) + MAX_END + 1)
                  for hh in range(GH)]
        room = [GH * step_width(s) - VECTOR_COLUMNS * vector_extras(q, s) for q, s, _ in places]
        total = sum(room)
        work = sum(u // GH + 1.5 for u in range(UNITS))
        n, done = 0, 0
        passed = 0
        for place, r in zip(places, room):
            passed += r
            while n < UNITS and done * total < passed * work:
                plan.setdefault(place, []).append(("max", g * UNITS + n, 0))
                done += n // GH + 1.5
                n += 1
        assert n == UNITS
    return plan


OUT_AT = {("o", 0): (GROUPS - 1, 2), ("o", 1): (GROUPS - 1, 5)}


SPLIT_AT = {(0, 0): ["wo0"], (0, 1): ["wo1"]}
DIVIDE_AT = {(g, s): (g // 2 - 1, n) for g in range(2, GROUPS, 2) for n, s in ((0, 2), (1, 8))}
DIVIDE_AT[GROUPS - 1, STEPS - 1] = (KD - 1, 0)


MAX_PLAN = max_plan()


def extras(g, s, hh):
    todo = list(MAX_PLAN.get((g, s, hh), []))
    if 1 <= g and g + 1 < GROUPS and (s, hh) == (MAX_END + 1, GH - 1):
        todo.append(("m", g + 1, 0))
    for (kind, k), (g0, s0) in OUT_AT.items():
        part = GH * (s - s0) + hh
        if g == g0 and 0 <= part < PARTS[kind]:
            todo.append((kind, k, part))
    return todo


def finished(g, s):
    return [(kind, k) for hh in range(GH) for kind, k, part in extras(g, s, hh) if part == PARTS.get(kind, 1) - 1]


USERS = psum_users()
USER_AT = {u: n for n, (u, _) in enumerate(USERS)}


def build(nc, stream, router1, x_in, vec, bias_rows, discount, expert_map, heads_dram, max_dram, u_dram, den_dram, out):
    nodes = ExitStack()
    with nodes:
        def sem(name):
            return nodes.enter_context(nc.semaphore(name))

        def sb(stack, name, shape, dt=F32):
            return stack.enter_context(nc.sbuf_tensor(name, shape, dt))

        ident = sb(nodes, "ident", [P, P])
        causal = sb(nodes, "causal", [P, NT * P], BF16)
        x_sb = sb(nodes, "x_sb", [P, NT, D])
        xt_hi = sb(nodes, "xt_hi", [P, KD, TOK], F32R)
        xt_lo = sb(nodes, "xt_lo", [P, KD, TOK], F32R)
        stage = sb(nodes, "stage", [P, 2, SLOT])
        ring_hi = sb(nodes, "ring_hi", [P, 2, SLOT], F32R)
        ring_lo = sb(nodes, "ring_lo", [P, 2, SLOT], F32R)
        stats = sb(nodes, "stats", [P, NT, 6])
        mean_var = sb(nodes, "mean_var", [P, NT, 2])
        rstd = sb(nodes, "rstd", [P, NT])
        eps_col = sb(nodes, "eps_col", [P, 1])
        vec_sb = sb(nodes, "vec_sb", [P, VECS])
        disc = sb(nodes, "disc", [P, ORDERS])
        ratio = sb(nodes, "ratio", [P, ORDERS])
        logit = sb(nodes, "logit", [P, NT, ROUTES_PAD])
        prob = sb(nodes, "prob", [P, NT, ROUTES_PAD])
        rest = sb(nodes, "rest", [P, NT, ROUTES_PAD])
        chosen = sb(nodes, "chosen", [P, NT, ROUTES_PAD])
        top = sb(nodes, "top", [P, NT, 8])
        rowmax = sb(nodes, "rowmax", [P, NT])
        norm = sb(nodes, "norm", [P, NT])
        gate = sb(nodes, "gate", [P, NT, NE])
        map_i = sb(nodes, "map_i", [P, ROUTES], I32)
        map_f = sb(nodes, "map_f", [P, ROUTES])
        expert_id = sb(nodes, "expert_id", [P, NE])
        onehot = sb(nodes, "onehot", [P, NE, ROUTES])
        rw_stage = sb(nodes, "rw_stage", [P, KD * ROUTES_PAD])
        rw_hi = sb(nodes, "rw_hi", [P, KD, ROUTES_PAD], F32R)
        rw_lo = sb(nodes, "rw_lo", [P, KD, ROUTES_PAD], F32R)

        block0 = ExitStack()
        with block0:
            res_hi = sb(block0, "res_hi", [P, len(RESIDENT), D], F32R)
            res_lo = sb(block0, "res_lo", [P, len(RESIDENT), D], F32R)
            h_hi = sb(block0, "h_hi", [P, 2, HALF], F32R)
            h_lo = sb(block0, "h_lo", [P, 2, HALF], F32R)
            term_hi = sb(block0, "term_hi", [P, 3, HALF], F32R)
            term_lo = sb(block0, "term_lo", [P, 3, HALF], F32R)
            hw_hi = sb(block0, "hw_hi", [P, HALF], F32R)
            hw_lo = sb(block0, "hw_lo", [P, HALF], F32R)
            silu = sb(block0, "silu", [P, HALF])
            h_f = sb(block0, "h_f", [P, HALF])
            delta = sb(block0, "delta", [P, HALF])
            keep = sb(block0, "keep", [P, HALF])
            term_f = sb(block0, "term_f", [P, 2, HALF])
            lora_h = sb(block0, "lora_h", [P, HALF])
            gate_x = sb(block0, "gate_x", [P, HT, NE, RANK])
            lgt = sb(block0, "lgt", [P, HALF])
            xn = sb(block0, "xn", [P, 2, D])
        block1 = ExitStack()
        nodes.enter_context(block1)
        qst = sb(block1, "qst", [P, 2, GH, TOK], F32R)
        kst = sb(block1, "kst", [P, 2, 2, TOK], F32R)
        attn_hi = sb(block1, "attn_hi", [P, KD, TOK], F32R)
        attn_lo = sb(block1, "attn_lo", [P, KD, TOK], F32R)
        v_sb = sb(block1, "v_sb", [P, NT, HEADS, HD + 1])
        probs = sb(block1, "probs", [P, NPROB, HALF])
        u_sb = sb(block1, "u_sb", [P, 2, HALF])
        u_all, den_all = stage[:, 0, :], stage[:, 1, :]
        den = sb(block1, "den", [P, 2, DEN_COLS])
        maxcol = sb(block1, "maxcol", [P, 2, GH, NT])
        negm = sb(block1, "negm", [GH * NT, 2, 2, P], F32R)
        bv_bc = u_sb[:, 0, :]
        xn1 = probs[:, 8:10, :]
        bo_bc = probs[:, 10, :]
        lgt1 = probs[0:ROUTES_PAD, 0:2, :].rearrange("p a n -> p (a n)")
        lora_h1 = probs[:, 2:4, :].rearrange("p a n -> p (a n)")
        gate_x1 = probs[:, 4:6, :].rearrange("p a (t e r) -> p (a t) e r", e=NE, r=RANK)
        hw_f1 = probs[:, 6:8, :].rearrange("p a n -> p (a n)")
        base_bc = u_sb[:, 1, :]

        slot = [nodes.enter_context(nc.psum_tensor(f"slot{n}", [P, 2, 512], F32)) for n in range(2)]
        bank = [nodes.enter_context(nc.psum_tensor(f"bank{n}", [P, 512], F32)) for n in range(4)]

        S = {name: sem(name) for name in (
            "ident_ready const_ready x_landed0 x_landed1 x_landed2 x_landed3 vec_landed "
            "w_landed0 w_landed1 w_hi w_lo "
            "stat_ready std_ready xn_ready x_turned xt_hi_ready x_free "
            "ratio_diff ratio_ready s_ready t_hi t_f t_lo t_used "
            "f_ready silu_ready h_f_ready h_hi_ready f_free h_used "
            "lgt_ready l_a_ready lora_h_ready logit_ready exp_ready gate_ready l_b_ready hw_f_ready hw_hi_ready l_free "
            "out_ready out_free bias_landed rw_ready hw1_ready "
            "q_ready q_hi q_free k_ready k_hi k_free r_ready r_free a_ready a_free lt_ready w_ready w_free "
            "v_done v_free y_done y_free "
            "max_ready max_free m_ready m_hi m_free "
            "q_stored k_stored stacks0 stacks1 stacks2 negm_stored negm_landed0 negm_landed1 u_stored0 u_stored1 "
            "st_ready exp_done masked pv_done u_free den_landed0 den_landed1 den_inverted den_stored u_landed0 u_landed1 "
            "attn_f attn_hi_ready attn_lo_ready y_biased o_ready out_sb_ready stored dve k_ones blank "
        ).split()}

        def queries(g, side):
            if g % 3 == 2:
                return (ring_hi, ring_lo)[side][:]
            return qst[:, g % 3, 2 * side:2 * side + 2, :]

        def keys(g):
            if g % 3 == 2:
                return xt_hi[:, KD - 2:, :]
            return kst[:, g % 3]

        def blank(engine, g):
            for side in range(2):
                engine.memset(queries(g, side).rearrange("p b n -> p (b n)").bitcast(F32), 0.0
                              ).then_inc(S["blank"], 1)
            engine.memset(keys(g).rearrange("p b n -> p (b n)").bitcast(F32), 1.0).then_inc(S["blank"], 1)

        def slot_of(user):
            return slot[USERS[USER_AT[user]][1]]

        def freed(user):
            n = USER_AT[user]
            before = [u for u, at in USERS[:n] if at == USERS[n][1]]
            if not before:
                return None
            kind, k = before[-1]
            if kind == "s":
                return S["t_lo"], 7 * k + 1
            return S[f"{kind}_free"], k + 1

        def h_done(k):
            half, c = k // FC, k % FC
            return (S["out_ready"], HT * (half + 1)) if c == FC - 1 else (S["h_used"], (FC - 1) * half + c + 1)

        def x_bank(q, n):
            return slot_of(("x", q))[:, n, :] if q < 6 else bank[2 * (q - 6) + n][:, :]

        def o_bank(t):
            return slot_of(("o", t // 2))[:, t % 2, :] if t < 4 else bank[t - 4][:, :]

        def wait_slot(pe, user):
            f = freed(user)
            if f is not None:
                pe.wait_ge(*f)

        item_at, ring_at = {}, {}
        for n, (dest, name) in enumerate(ITEMS):
            item_at[(name, sum(1 for d, m in ITEMS[:n] if m == name))] = n
            if dest == "ring":
                ring_at[n] = len(ring_at)

        def ring_of(name, half=0):
            n = item_at[(name, half)]
            r = ring_at[n] % 2
            return n, ring_hi[:, r, :], ring_lo[:, r, :]

        hw1 = ring_of(f"qk{KD - 1}")[1:]

        def ring_done(r):
            name = [m for d, m in ITEMS if d == "ring"][r]
            half = int(r > FC)
            if name == "gate_up":
                return S["s_ready"], half + 1
            if name.startswith("ffn"):
                return S["f_ready"], half * FC + int(name[3:]) + 1
            return S["k_ready"], int(name[2:]) + 1

        def destination(n):
            dest, name = ITEMS[n]
            if dest == "ring":
                r = ring_at[n] % 2
                return ring_hi[:, r, :], ring_lo[:, r, :]
            if dest == "resident":
                c = int(name[3:])
                return tuple(t[:, 2 * c:2 * c + 2, :].rearrange("p a n -> p (a n)") for t in (res_hi, res_lo))
            i = int(dest[-1])
            if dest[0] == "v":
                return attn_hi[:, i, :], attn_lo[:, i, :]
            if dest[0] == "b":
                return attn_hi[:, 2 + i, :], attn_lo[:, 2 + i, :]
            return tuple(t[:, i, :] for t in (xt_hi, xt_lo))

        def res(name):
            return res_hi[:, RES_AT[name], :], res_lo[:, RES_AT[name], :]

        v_w = [t[:, 0:2, :].rearrange("p a (b n) -> p (a b) n", n=D) for t in (attn_hi, attn_lo)]
        base_w = [t[:, 2:4, :].rearrange("p a (b n) -> p (a b) n", n=D) for t in (attn_hi, attn_lo)]
        wo_w = [t[:, 0:2, :].rearrange("p a (b n) -> p (a b) n", n=D) for t in (xt_hi, xt_lo)]
        nat = {("q", 0): attn_hi[:, 2, :], ("q", 1): attn_lo[:, 2, :],
               ("k", 0): attn_hi[:, 3, :], ("k", 1): attn_lo[:, 3, :]}

        block = nodes.enter_context(nc.Block())

        @block.sync
        def _(sp):
            def weights(n):
                if n >= 2:
                    sp.wait_ge(S["w_lo"], n - 1)
                sp.dma_start(stage[:, n % 2, :], stream[ARRAYS.index(ITEMS[n][1])]).then_inc(S[f"w_landed{n % 2}"], 16)

            sp.dma_start(x_sb[:, 0, :], x_in[0]).then_inc(S["x_landed0"], 16)
            sp.dma_start(x_sb[:, 1, :], x_in[1]).then_inc(S["x_landed1"], 16)
            weights(0)
            sp.dma_start(x_sb[:, 2:4, :], x_in[2:4].rearrange("t p d -> p t d")).then_inc(S["x_landed2"], 16)
            weights(1)
            sp.dma_start(x_sb[:, 4:8, :], x_in[4:8].rearrange("t p d -> p t d")).then_inc(S["x_landed3"], 16)
            for n in range(2, item_at[("qk3", 0)] + 1):
                weights(n)

            def stack(g):
                m, z = g // 2, g % 3
                if g >= 3:
                    sp.wait_ge(S["st_ready"], banks_before(g - 2, 0))
                if g < 3:
                    sp.wait_ge(S["blank"], 3 * (g + 1))
                for n, which in enumerate("qk"):
                    sp.wait_ge(S[f"{which}_stored"], 32 * (m + 1))
                    for side in range(2):
                        first = heads_dram[m, n, GH * (g % 2) + side]
                        st = queries(g, side) if which == "q" else keys(g)
                        for row, rows in ((0, 2 * HD), (2 * HD, HD)) if which == "q" else ((0, HD), (HD, 2 * HD)):
                            at = SIDE * side + row
                            sp.dma_start(st[at:at + rows].bitcast(F32),
                                         bass.AP(first.tensor, first.offset,
                                                 [[TOK, rows], [2 * 2 * HD * TOK, 2], [1, TOK]])
                                         ).then_inc(S[f"stacks{z}"], 16)

            def store(which, m):
                sp.wait_ge(S[f"{which}_free"], m + 1)
                for part in range(2):
                    first = heads_dram[m, "qk".index(which), 0, part * HD]
                    sp.dma_start(bass.AP(first.tensor, first.offset, [[2 * HD * TOK, 2 * GH], [TOK, HD], [1, TOK]]),
                                 nat[which, part].bitcast(F32)).then_inc(S[f"{which}_stored"], 16)

            def neg_max(g):
                sp.wait_ge(S["m_free"], g + 1)
                first = max_dram[g, 0]
                sp.dma_start(bass.AP(first.tensor, first.offset, [[P, GH * NT], [GH * TOK, 2], [1, P]]),
                             negm[:, g % 2].bitcast(F32)).then_inc(S["negm_stored"], 16)
                sp.wait_ge(S["negm_stored"], 16 * (g + 1))
                for side in range(2):
                    first = max_dram[g, 0, 2 * side]
                    sp.dma_start(queries(g, side)[DOT_ROWS:ST_ROWS].bitcast(F32),
                                 bass.AP(first.tensor, first.offset, [[GH * TOK, 2], [1, 2 * TOK]])
                                 ).then_inc(S[f"negm_landed{g % 2}"], 16)

            def gather(g, half):
                e = 2 * g + half
                sp.wait_ge(S["u_free"], e + 1)
                if e == 0:
                    sp.wait_ge(S["w_lo"], len(ITEMS))
                if g % 2 == 0 and g > 0:
                    sp.wait_ge(S["attn_lo_ready"], 2 * (g // 2 - 1) + half + 1)
                sp.dma_start(u_dram[e], u_sb[:, e % 2, :]).then_inc(S[f"u_stored{half}"], 16)
                sp.wait_ge(S[f"u_stored{half}"], 16 * (g + 1))
                to = (slice(GH * HD * (g % 2), GH * HD * (g % 2 + 1)), slice(half * HALF, (half + 1) * HALF))
                sp.dma_start(u_all[to], bass.AP(u_dram.tensor, u_dram[e, 0].offset, [[32 * HALF, GH], [1, HD * HALF]])
                             ).then_inc(S[f"u_landed{half}"], 16)
                sp.dma_start(den[:, half, :],
                             bass.AP(u_dram.tensor, u_dram[e, HD].offset,
                                     [[32 * HALF, GH], [DEN_COLS, P // GH], [1, DEN_COLS]])
                             ).then_inc(S[f"den_landed{half}"], 16)

            def spread_den(g, half):
                e = 2 * g + half
                sp.wait_ge(S["den_inverted"], e + 1)
                sp.dma_start(den_dram[e].rearrange("h (c n) -> (h c) n", n=DEN_COLS), den[:, half, :]
                             ).then_inc(S["den_stored"], 16)
                sp.wait_ge(S["den_stored"], 16 * (e + 1))
                to = (slice(GH * HD * (g % 2), GH * HD * (g % 2 + 1)), slice(half * HALF, (half + 1) * HALF))
                sp.dma_start(den_all[to], bass.AP(den_dram.tensor, den_dram[e, 0].offset,
                                                  [[HALF, GH], [0, HD], [1, HALF]])
                             ).then_inc(S[f"u_landed{half}"], 16)

            for m, name in enumerate(("lora1", "wv0", "wv1", "base0")):
                store("q", m)
                store("k", m)
                weights(item_at[(name, 0)])
                if m in (1, 2):
                    stack(m - 1)
            weights(item_at[("base1", 0)])
            neg_max(0)
            for name in ("wo0", "wo1"):
                weights(item_at[(name, 0)])
            neg_max(1)
            for g in range(GROUPS):
                for s in range(STEPS):
                    if s == 0 and g + 2 < GROUPS:
                        stack(g + 2)
                    if s == LAG + 1 and g > 0:
                        gather(g - 1, 1)
                    if s == LAG + 4 and g > 0:
                        spread_den(g - 1, 1)
                    if s == HT + LAG + 1:
                        gather(g, 0)
                    if s == HT + LAG + 4:
                        spread_den(g, 0)
                    if s == MAX_END + 2 and 1 <= g and g + 1 < GROUPS:
                        neg_max(g + 1)
            def store_out(t):
                sp.wait_ge(S["out_sb_ready"], t + 1)
                sp.dma_start(out[t], x_sb[:, t, :]).then_inc(S["stored"], 16)

            gather(GROUPS - 1, 1)
            spread_den(GROUPS - 1, 1)
            for t in range(NT):
                store_out(t)
            sp.wait_ge(S["stored"], 16 * NT)

        @block.gpsimd
        def _(pool):
            pool.memset(ident[:], 0.0).then_inc(S["ident_ready"], 1)
            pool.wait_ge(S["ident_ready"], 1)
            pool.affine_select(out=ident[:], in_=ident[:], compare_op=ALU.not_equal, fill=1.0, base=0,
                               pattern=[[-1, P]], channel_multiplier=1).then_inc(S["ident_ready"], 1)
            pool.memset(eps_col[:], EPS).then_inc(S["const_ready"], 1)
            pool.memset(prob[:], -1.0).then_inc(S["const_ready"], 1)
            pool.memset(causal[:], 0.0).then_inc(S["const_ready"], 1)
            pool.dma_start(vec_sb[:], vec).then_inc(S["vec_landed"], 16)
            pool.dma_start(disc[:], discount.partition_broadcast(P)).then_inc(S["vec_landed"], 16)
            pool.dma_start(map_i[:], expert_map.partition_broadcast(P)).then_inc(S["vec_landed"], 16)
            pool.dma_start(rw_stage[:], router1).then_inc(S["vec_landed"], 16)
            pool.wait_ge(S["const_ready"], 3)
            pool.affine_select(out=causal[:, (NT - 1) * P:], in_=causal[:, (NT - 1) * P:], compare_op=ALU.is_ge,
                               fill=MASKED, base=0, pattern=[[-1, P]], channel_multiplier=1
                               ).then_inc(S["const_ready"], 1)
            pool.iota(expert_id[:], pattern=[[1, NE]], base=0, channel_multiplier=0,
                      allow_small_or_imprecise_dtypes=True).then_inc(S["const_ready"], 1)
            pool.wait_ge(S["out_free"], 8)
            for n, row in enumerate((bv_bc, base_bc, bo_bc)):
                pool.dma_start(row, bias_rows[n].partition_broadcast(P)).then_inc(S["bias_landed"], 16)
            blank(pool, 0)
            pool.memset(v_sb[:], 1.0).then_inc(S["k_ones"], 1)
            blank(pool, 1)
            pool.wait_ge(S["bias_landed"], 48)
            pool.tensor_tensor(bo_bc, bo_bc, base_bc, ALU.add).then_inc(S["k_ones"], 1)
            pool.wait_ge(S["k_ones"], 2)
            for t in range(NT):
                pool.wait_ge(S["y_free"], t + 1)
                pool.tensor_tensor(x_sb[:, t, :], x_sb[:, t, :], bo_bc, ALU.add).then_inc(S["y_biased"], 1)
            for g in range(GROUPS):
                for s, (half, j) in enumerate(QSTEPS):
                    if s in DIAGONAL:
                        b = GH * (STEPS * g + s) % NPROB
                        pool.wait_ge(S["exp_done"], banks_before(g, s + 1))
                        part = probs[:, b:b + GH, 0:P]
                        pool.affine_select(out=part, in_=part, compare_op=ALU.is_ge, fill=0.0, base=0,
                                           pattern=[[0, GH], [1, P]], channel_multiplier=-1
                                           ).then_inc(S["masked"], 1)

        @block.scalar
        def _(act):
            def split_hi(n):
                dest, name = ITEMS[n]
                act.wait_ge(S[f"w_landed{n % 2}"], 16 * (n // 2 + 1))
                if dest == "ring" and ring_at[n] >= 2:
                    act.wait_ge(*ring_done(ring_at[n] - 2))
                if dest == "v0":
                    act.wait_ge(S["out_free"], 8)
                if dest == "base0":
                    act.wait_ge(S["q_stored"], 32 * KD)
                    act.wait_ge(S["k_stored"], 32 * KD)
                if dest == "wo0":
                    act.wait_ge(S["y_done"], NT)
                act.activation(destination(n)[0], stage[:, n % 2, :], ACT.Copy).then_inc(S["w_hi"], 1)

            def std(quad):
                act.wait_ge(S["stat_ready"], quad + 1)
                t = HT * (quad % 2)
                if quad == 0:
                    act.wait_ge(S["const_ready"], 1)
                act.activation(rstd[:, t:t + HT], mean_var[:, t:t + HT, 1], ACT.Sqrt, bias=eps_col[:, 0:1]
                               ).then_inc(S["std_ready"], 1)

            def turned_hi(q):
                t = 2 * (q % 4) * P
                act.wait_ge(S["x_turned"], q + 1)
                if q < 6:
                    act.activation(xt_hi[:, :, t:t + 2 * P].rearrange("p k (t n) -> p t k n", t=2),
                                   slot_of(("x", q))[:].rearrange("p t (k n) -> p t k n", k=KD), ACT.Copy
                                   ).then_inc(S["xt_hi_ready"], 1)
                else:
                    for n in range(2):
                        last = act.activation(xt_hi[:, :, t + n * P:t + (n + 1) * P],
                                              x_bank(q, n).rearrange("p (k n) -> p k n", k=KD), ACT.Copy)
                    last.then_inc(S["xt_hi_ready"], 1)

            def term(half, o):
                k = 7 * half + o
                if o == 0:
                    act.wait_ge(S["s_ready"], half + 1)
                else:
                    act.wait_ge(S["t_f"], 6 * half + o)
                if k >= 3:
                    act.wait_ge(S["t_used"], k - 2)
                src = slot_of(("s", half))[:, 1, :] if o == 0 else term_f[:, o % 2, :]
                act.activation(term_hi[:, k % 3, :], src, ACT.Copy).then_inc(S["t_hi"], 1)

            act.wait_ge(S["ratio_diff"], 1)
            act.activation(ratio[:], disc[:], ACT.Exp).then_inc(S["ratio_ready"], 1)
            std(0)
            for n in range(1):
                split_hi(n)
            turned_hi(0)
            turned_hi(1)
            for n in range(1, 3):
                split_hi(n)
            for half in range(2):
                term(half, 0)
                for c in range(FC):
                    if c + 1 < FC:
                        split_hi(item_at[(f"ffn{c + 1}", half)])
                        if half == 0:
                            split_hi(item_at[(f"res{c + 1}", 0)])
                    elif half == 0:
                        split_hi(item_at[("gate_up", 1)])
                    else:
                        split_hi(item_at[("qk0", 0)])
                    k = half * FC + c
                    m = FSHORT if c == 0 else P
                    if c == 1:
                        act.wait_ge(S["hw_f_ready"], half + 1)
                        act.activation(hw_hi[:], lora_h[:], ACT.Copy).then_inc(S["hw_hi_ready"], 1)
                    act.wait_ge(S["f_ready"], k + 1)
                    if k >= 1:
                        act.wait_ge(S["h_f_ready"], k)
                    act.activation(silu[0:m, :], slot_of(("f", k))[0:m, 0, :], ACT.Silu).then_inc(S["silu_ready"], 1)
                    act.wait_ge(S["h_f_ready"], k + 1)
                    if k >= 2:
                        act.wait_ge(*h_done(k - 2))
                    act.activation(h_hi[0:m, c % 2, :], h_f[0:m, :], ACT.Copy).then_inc(S["h_hi_ready"], 1)
                    if c == 0:
                        act.wait_ge(S["l_a_ready"], half + 1)
                        act.activation(lora_h[:], slot_of(("l", half))[:, 0, :], ACT.Copy
                                       ).then_inc(S["lora_h_ready"], 1)
                        act.wait_ge(S["const_ready"], 2)
                        act.wait_ge(S["logit_ready"], half + 1)
                        act.activation(prob[:, 0:HT, 0:NE], logit[:, 0:HT, 0:NE], ACT.Exp).then_inc(S["exp_ready"], 1)
                    if 1 <= c <= ORDERS:
                        term(half, c)
                    if c == 2:
                        std(1 + half)
                    if c in X_AFTER:
                        turned_hi(2 + 2 * half + X_AFTER.index(c))
                    if c == FC - 1:
                        if half == 0:
                            split_hi(item_at[("ffn0", 1)])
                        else:
                            split_hi(item_at[("qk1", 0)])

            std(3)
            turned_hi(6)
            turned_hi(7)

            def project_hi(which, m):
                bias = vec_sb[:, VEC_Q + m:VEC_Q + m + 1] if which == "q" else vec_sb[:, VEC_K + m:VEC_K + m + 1]
                act.wait_ge(S[f"{which}_ready"], m + 1)
                if m >= 1:
                    act.wait_ge(S[f"{which}_stored"], 32 * m)
                act.activation(nat[which, 0], slot_of((which, m))[:].rearrange("p a n -> p (a n)"), ACT.Identity,
                               bias=bias).then_inc(S[f"{which}_hi"], 1)

            def neg_max_hi(g):
                act.wait_ge(S["m_ready"], g + 1)
                if g >= 2:
                    act.wait_ge(S["negm_stored"], 16 * (g - 1))
                act.activation(negm[:, g % 2, 0, :], slot_of(("m", g))[0:GH * NT, 0, 0:P], ACT.Copy, scale=-1.0
                               ).then_inc(S["m_hi"], 1)

            def take_u(g, half):
                e = 2 * g + half
                act.wait_ge(S["pv_done"], STEPS * g + HT + NT * half)
                if g >= 1:
                    act.wait_ge(S[f"u_stored{half}"], 16 * g)
                act.activation(u_sb[:, e % 2, :], bank[3][:], ACT.Copy).then_inc(S["u_free"], 1)

            def attn_split_hi(m, half):
                k = 2 * m + half
                act.wait_ge(S["attn_f"], k + 1)
                if k == 0:
                    act.wait_ge(S["y_done"], NT)
                at = slice(half * HALF, (half + 1) * HALF)
                act.activation(attn_hi[:, m, at], u_all[:, at], ACT.Copy).then_inc(S["attn_hi_ready"], 1)

            project_hi("q", 0)
            act.wait_ge(S["logit_ready"], 3)
            act.activation(prob[:, :, 0:ROUTES], logit[:, :, 0:ROUTES], ACT.Exp).then_inc(S["exp_ready"], 1)
            project_hi("k", 0)
            for m, name in enumerate(("qk2", "qk3", "lora1"), 1):
                split_hi(item_at[(name, 0)])
                project_hi("q", m)
                project_hi("k", m)
            split_hi(item_at[("wv0", 0)])
            split_hi(item_at[("wv1", 0)])
            act.wait_ge(S["a_ready"], 1)
            act.activation(lora_h1, slot_of(("a", 0))[:].rearrange("p a n -> p (a n)"), ACT.Copy
                           ).then_inc(S["a_free"], 1)
            act.wait_ge(S["w_free"], 1)
            act.wait_ge(S["k_ready"], KD)
            act.activation(hw1[0], hw_f1, ACT.Copy).then_inc(S["hw_hi_ready"], 1)
            for n in range(2):
                split_hi(item_at[(f"base{n}", 0)])
            for g in range(2):
                neg_max_hi(g)
            for g in range(GROUPS):
                for s, (half, j) in enumerate(QSTEPS):
                    if s == HT + LAG:
                        take_u(g, 0)
                    if s == LAG and g > 0:
                        take_u(g - 1, 1)
                    n, heads = step_width(s), per_bank(s)
                    if STEPS * g + s > LAG:
                        act.wait_ge(S["pv_done"], STEPS * g + s - LAG)
                    elif s == LAG:
                        act.wait_ge(S["y_biased"], NT)
                    for hh in range(0, GH, heads):
                        b = banks_before(g, s) + hh // heads
                        to = (GH * (STEPS * g + s) + hh) % NPROB
                        act.wait_ge(S["st_ready"], b + 1)
                        act.activation(probs[:, to:to + heads, 0:n],
                                       bank[b % 3][:, 0:heads * n].rearrange("p (h n) -> p h n", n=n),
                                       ACT.Exp, scale=HD ** -0.5).then_inc(S["exp_done"], 1)
                    for kind, k in finished(g, s):
                        if kind == "m":
                            neg_max_hi(k)
                    if (g, s) in DIVIDE_AT:
                        attn_split_hi(*DIVIDE_AT[g, s])
                    for name in SPLIT_AT.get((g, s), []):
                        split_hi(item_at[(name, 0)])
            take_u(GROUPS - 1, 1)
            attn_split_hi(KD - 1, 1)

        @block.tensor
        def _(pe):
            def product(out_ap, a, b, start, stop):
                pe.matmul(out_ap, a[0], b[0], start=start, stop=False)
                pe.matmul(out_ap, a[0], b[1], start=False, stop=False)
                return pe.matmul(out_ap, a[1], b[0], start=False, stop=stop)

            xt = (xt_hi, xt_lo)

            def turn(q):
                src = xn if q < 4 + 2 else xn1
                if q < 6:
                    wait_slot(pe, ("x", q))
                else:
                    pe.wait_ge(S["out_free"], 2 * HT)
                for n in range(2):
                    pe.wait_ge(S["xn_ready"], 2 * q + n + 1)
                    for k in range(KD):
                        last = pe.transpose(x_bank(q, n)[:, k * P:(k + 1) * P],
                                            src[:, n, k * P:(k + 1) * P], ident[:])
                last.then_inc(S["x_turned"], 1)

            def from_xt(dst, w, m0, m1, tok0, n, last_sem=None):
                for k in range(KD):
                    last = product(dst, (w[0][:, k, m0:m1], w[1][:, k, m0:m1]),
                                   (xt_hi[:, k, tok0:tok0 + n], xt_lo[:, k, tok0:tok0 + n]), k == 0, k == KD - 1)
                return last

            def weight(name, half=0):
                n, hi, lo = ring_of(name, half)
                pe.wait_ge(S["w_lo"], n + 1)
                return tuple(t.rearrange("p (k m) -> p k m", k=KD) for t in (hi, lo))

            pe.wait_ge(S["ident_ready"], 2)
            turn(0)
            turn(1)
            for half in range(2):
                tok0 = half * HALF
                pe.wait_ge(S["x_free"], 2 + 2 * half)
                w = weight("gate_up", half)
                ps = slot_of(("s", half))
                wait_slot(pe, ("s", half))
                from_xt(ps[:, 0, :], w, 0, P, tok0, HALF)
                from_xt(ps[:, 1, :], w, P, 2 * P, tok0, HALF).then_inc(S["s_ready"], 1)

                def out_products(a, names, sem_name, start=False, stop=False, k_rows=P):
                    for t in range(HT):
                        last = product(bank[t][:, :], (a[0][0:k_rows, t * P:(t + 1) * P], a[1][0:k_rows, t * P:(t + 1) * P]),
                                       tuple(x[0:k_rows] for x in res(names)), start, stop)
                        if stop:
                            last.then_inc(S["out_ready"], 1)
                    if sem_name and not stop:
                        last.then_inc(S[sem_name], 1)
                    return last

                def down(c):
                    k = half * FC + c
                    pe.wait_ge(S["f_free"], k + 1)
                    pe.wait_ge(S["w_lo"], res_item(f"down{c}") + 1)
                    if c == 0 and half == 1:
                        pe.wait_ge(S["out_free"], HT)
                    last = out_products((h_hi[:, c % 2, :], h_lo[:, c % 2, :]), f"down{c}", "h_used",
                                        start=(c == 0), stop=(c == FC - 1), k_rows=FSHORT if c == 0 else P)
                    return last

                def res_item(name):
                    return item_at[(f"res{RES_AT[name] // 2}", 0)]

                for c in range(FC):
                    k = half * FC + c
                    w = weight(f"ffn{c}", half)
                    wait_slot(pe, ("f", k))
                    ps = slot_of(("f", k))
                    mg, mu = (FSHORT + NE, FSHORT) if c == 0 else (P, P)
                    from_xt(ps[0:mg, 0, :], w, 0, mg, tok0, HALF)
                    from_xt(ps[0:mu, 1, :], w, P, P + mu, tok0, HALF).then_inc(S["f_ready"], 1)
                    if c == 0:
                        wait_slot(pe, ("l", half))
                        pe.wait_ge(S["w_lo"], res_item("lora_a") + 1)
                        ps = slot_of(("l", half))
                        w = tuple(t.rearrange("p (k m) -> p k m", k=KD) for t in res("lora_a"))
                        from_xt(ps[:, 0, :], w, 0, P, tok0, HALF)
                        pe.wait_ge(S["lgt_ready"], half + 1)
                        for t in range(HT):
                            last = pe.transpose(ps[:, 1, t * NE:(t + 1) * NE], lgt[FSHORT:FSHORT + NE, t * P:(t + 1) * P],
                                                ident[FSHORT:FSHORT + NE, FSHORT:FSHORT + NE])
                        last.then_inc(S["l_a_ready"], 1)
                    if c == 1:
                        pe.wait_ge(S["gate_ready"], half + 1)
                        ps = slot_of(("l", half))
                        for t in range(HT):
                            last = pe.transpose(ps[:, 1, t * P:(t + 1) * P],
                                                gate_x[:, t].rearrange("p e r -> p (e r)"), ident[:])
                        last.then_inc(S["l_b_ready"], 1)
                    if c in X_AFTER:
                        turn(2 + 2 * half + X_AFTER.index(c))
                    if c >= 1:
                        down(c - 1)
                        if c - 1 <= ORDERS:
                            o = 7 * half + c - 1
                            pe.wait_ge(S["t_lo"], o + 1)
                            out_products((term_hi[:, o % 3, :], term_lo[:, o % 3, :]), f"term{c - 1}", "t_used")
                    if c == FC - 2:
                        pe.wait_ge(S["l_free"], half + 1)
                        out_products((hw_hi, hw_lo), "lora_b", None)
                down(FC - 1)
            def project(which, m, halves=range(2)):
                w = weight(f"qk{m}")
                at = 0 if which == "q" else P
                if 0 in halves:
                    wait_slot(pe, (which, m))
                for n in halves:
                    last = from_xt(slot_of((which, m))[:, n, :], w, at, at + P, n * HALF, HALF)
                if 1 in halves:
                    last.then_inc(S[f"{which}_ready"], 1)

            def route_logits(n):
                return from_xt(slot_of(("r", 0))[0:ROUTES_PAD, n, :], (rw_hi, rw_lo), 0, ROUTES_PAD, n * HALF, HALF)

            wait_slot(pe, ("r", 0))
            pe.wait_ge(S["rw_ready"], 1)
            route_logits(0)
            project("q", 0, [0])
            turn(6)
            turn(7)

            pe.wait_ge(S["x_free"], 8)
            route_logits(1).then_inc(S["r_ready"], 1)
            project("q", 0, [1])
            pe.wait_ge(S["r_free"], 1)
            pe.wait_ge(S["out_free"], 8)
            for t in range(NT):
                last = pe.transpose(bank[0][:, t * ROUTES_PAD:(t + 1) * ROUTES_PAD], lgt1[:, t * P:(t + 1) * P],
                                    ident[0:ROUTES_PAD, 0:ROUTES_PAD])
            last.then_inc(S["lt_ready"], 1)
            project("k", 0)
            for m in range(1, KD):
                project("q", m)
                project("k", m)
            pe.wait_ge(S["w_lo"], item_at[("lora1", 0)] + 1)
            wait_slot(pe, ("a", 0))
            n1, hi1, lo1 = ring_of("lora1")
            a1 = tuple(t[:, 0:D].rearrange("p (k m) -> p k m", k=KD) for t in (hi1, lo1))
            b1 = (hi1[:, D:], lo1[:, D:])
            for n in range(2):
                last = from_xt(slot_of(("a", 0))[:, n, :], a1, 0, P, n * HALF, HALF)
            last.then_inc(S["a_ready"], 1)

            def maxima(u):
                g, i, hh = u // UNITS, u % UNITS // GH, u % GH
                wait_slot(pe, ("max", u))
                if u % UNITS == 0:
                    pe.wait_ge(S[f"stacks{g % 3}"], 128 * (g // 3 + 1))
                n = (i + 1) * P
                for b in range(-(-n // 512)):
                    c = min(n, 512 * (b + 1))
                    last = pe.matmul(slot_of(("max", u))[:, b, 0:c - 512 * b],
                                     queries(g, hh % 2)[0:DOT_ROWS, hh // 2, i * P:(i + 1) * P],
                                     keys(g)[0:DOT_ROWS, hh // 2, 512 * b:c], start=True, stop=True)
                last.then_inc(S["max_ready"], 1)

            def turn_maxima(g):
                pe.wait_ge(S["max_free"], UNITS * (g + 1))
                wait_slot(pe, ("m", g))
                pe.transpose(slot_of(("m", g))[0:GH * NT, 0, 0:P],
                             maxcol[:, g % 2].rearrange("p h i -> p (h i)"), ident[:]).then_inc(S["m_ready"], 1)

            def values(t):
                if t >= 4:
                    pe.wait_ge(S["v_free"], t - 3)
                for k in range(KD):
                    last = product(bank[t % 4][:, :], tuple(x[:, k, t * P:(t + 1) * P] for x in xt),
                                   tuple(x[:, k, :] for x in v_w), k == 0, k == KD - 1)
                    if k == KD - 1:
                        last.then_inc(S["v_done"], 1)
                    maxima(GH * t + k)

            def linear(t):
                if t == 0:
                    pe.wait_ge(S["v_free"], NT)
                if t >= 4:
                    pe.wait_ge(S["y_free"], t - 3)
                for k in range(KD):
                    product(bank[t % 4][:, :], tuple(x[:, k, t * P:(t + 1) * P] for x in xt),
                            tuple(x[:, k, :] for x in base_w), k == 0, False)
                    if k < KD - 1:
                        maxima(UNITS + GH * t + k)
                product(bank[t % 4][:, :], tuple(x[:, t * P:(t + 1) * P] for x in hw1), b1, False, True
                        ).then_inc(S["y_done"], 1)
                maxima(UNITS + GH * t + KD - 1)

            pe.wait_ge(S["gate_ready"], 3)
            wait_slot(pe, ("w", 0))
            for t in range(NT):
                last = pe.transpose(slot_of(("w", 0))[:, t // 4, t % 4 * P:(t % 4 + 1) * P],
                                    gate_x1[:, t].rearrange("p e r -> p (e r)"), ident[:])
            last.then_inc(S["w_ready"], 1)
            pe.wait_ge(S["w_lo"], item_at[("wv1", 0)] + 1)
            for t in range(NT):
                values(t)
            turn_maxima(0)
            pe.wait_ge(S["w_lo"], item_at[("base1", 0)] + 1)
            pe.wait_ge(S["hw1_ready"], 1)
            for t in range(NT):
                linear(t)
            turn_maxima(1)

            def score(g, s, hh):
                half, j = QSTEPS[s]
                heads = per_bank(s)
                b = banks_before(g, s) + hh // heads
                n = step_width(s)
                q0 = HALF * (half + 1) - n
                if hh % heads == 0 and b >= 3:
                    pe.wait_ge(S["exp_done"], b - 2)
                if b == 0:
                    pe.wait_ge(S["v_free"], NT)
                    pe.wait_ge(S["y_free"], NT)
                if s == 0 and hh == 0:
                    pe.wait_ge(S[f"negm_landed{g % 2}"], 32 * (g // 2 + 1))
                at = hh % heads * n
                last = pe.matmul(bank[b % 3][:, at:at + n], keys(g)[0:ST_ROWS, hh // 2, j * P:(j + 1) * P],
                                 queries(g, hh % 2)[0:ST_ROWS, hh // 2, q0:q0 + n], start=True, stop=True)
                if hh % heads == heads - 1:
                    last.then_inc(S["st_ready"], 1)

            def weigh_values(k):
                g, s = k // STEPS, k % STEPS
                half, j = QSTEPS[s]
                c0 = max(0, P * j - HALF * half)
                pe.wait_ge(S["exp_done"], banks_before(g, s + 1))
                if s in DIAGONAL:
                    pe.wait_ge(S["masked"], NT * g + DIAGONAL.index(s) + 1)
                if j == 0 and 2 * g + half > 0:
                    pe.wait_ge(S["u_free"], 2 * g + half)
                stop = s in (HT - 1, STEPS - 1)
                for hh in range(GH):
                    last = pe.matmul(bank[3][32 * hh:32 * hh + HD + 1, c0:HALF], v_sb[:, j, GH * g + hh, :],
                                     probs[:, (GH * k + hh) % NPROB, 0:HALF - c0], start=(j == 0), stop=stop)
                last.then_inc(S["pv_done"], 1)
                return last


            def out_project(t, k):
                return product(o_bank(t), tuple(x[:, k, t * P:(t + 1) * P] for x in (attn_hi, attn_lo)),
                               tuple(x[:, k, :] for x in wo_w), k == 0, k == KD - 1)

            for g in range(GROUPS):
                for s in range(STEPS):
                    for hh in range(GH):
                        score(g, s, hh)
                        for kind, u, part in extras(g, s, hh):
                            if kind == "max":
                                maxima(u)
                            elif kind == "m":
                                turn_maxima(u)
                            elif kind == "o":
                                if part == 0:
                                    pe.wait_ge(S["attn_lo_ready"], 2 * (KD - 1))
                                    pe.wait_ge(S["w_lo"], len(ITEMS))
                                    wait_slot(pe, ("o", u))
                                out_project(2 * u + part // (KD - 1), part % (KD - 1))
                        k = STEPS * g + s - LAG
                        if hh == GH - 1 and k >= 0:
                            weigh_values(k)
            for k in range(STEPS * GROUPS - LAG, STEPS * GROUPS):
                weigh_values(k)
            pe.wait_ge(S["exp_done"], banks_before(GROUPS, 0))
            pe.wait_ge(S["u_free"], 2 * GROUPS)
            pe.wait_ge(S["attn_lo_ready"], 2 * KD - 1)
            for t in range(HT):
                out_project(t, KD - 1).then_inc(S["o_ready"], 1)
            for t in range(HT, NT):
                for k in range(KD - 1):
                    out_project(t, k)
            pe.wait_ge(S["attn_lo_ready"], 2 * KD)
            for t in range(HT, NT):
                out_project(t, KD - 1).then_inc(S["o_ready"], 1)

        @block.vector
        def _(dve):
            chain = [0]

            def then(ins):
                chain[0] += 1
                ins.then_inc(S["dve"], 1)
                dve.wait_ge(S["dve"], chain[0])

            def split_lo(n):
                dve.wait_ge(S["w_hi"], n + 1)
                hi, lo = destination(n)
                dve.tensor_tensor(lo, stage[:, n % 2, :], hi.bitcast(F32), ALU.subtract).then_inc(S["w_lo"], 1)

            def statistics(quad):
                t0 = HT * (quad % 2)
                for t in range(t0, t0 + HT):
                    if quad >= 2:
                        dve.wait_ge(S["out_free"], (quad - 1) * HT)
                    else:
                        dve.wait_ge(S[f"x_landed{(0, 1, 2, 2, 3, 3, 3, 3)[t]}"], 16)
                    last = dve.bn_stats(stats[:, t, :], x_sb[:, t, :])
                then(last)
                for t in range(t0, t0 + HT):
                    last = dve.bn_aggr(mean_var[:, t, :], stats[:, t, :])
                last.then_inc(S["stat_ready"], 1)

            def invert_std(quad):
                t0 = HT * (quad % 2)
                dve.wait_ge(S["std_ready"], quad + 1)
                then(dve.reciprocal(rstd[:, t0:t0 + HT], rstd[:, t0:t0 + HT]))

            def normalize(q):
                dst = xn if q < 6 else xn1
                if q >= 1:
                    dve.wait_ge(S["x_turned"], q)
                for n in range(2):
                    t = 2 * (q % 4) + n
                    dve.tensor_scalar(dst[:, n, :], x_sb[:, t, :], mean_var[:, t, 0:1], rstd[:, t:t + 1],
                                      ALU.subtract, ALU.mult).then_inc(S["xn_ready"], 1)

            def turned_lo(q):
                t = 2 * (q % 4) * P
                dve.wait_ge(S["xt_hi_ready"], q + 1)
                for n in range(2):
                    at = (slice(None), slice(None), slice(t + n * P, t + (n + 1) * P))
                    last = dve.tensor_tensor(xt_lo[at], x_bank(q, n).rearrange("p (k n) -> p k n", k=KD),
                                             xt_hi[at].bitcast(F32), ALU.subtract)
                last.then_inc(S["x_free"], 1)

            def wide(ap, *dims):
                return bass.AP(ap.tensor, ap.offset, [ap.ap[0], *[list(d) for d in dims]])

            def route(n_tok, routes, e):
                src = slot_of(("l", e))[:, 1, 0:HT * NE] if e < 2 else bank[0][:, 0:NT * ROUTES_PAD]
                w = NE if e < 2 else ROUTES_PAD
                src = src.rearrange("p (t e) -> p t e", e=w)[:, :, 0:routes]
                then(dve.tensor_reduce(rowmax[:, 0:n_tok], src, AX.X, ALU.max))
                dve.tensor_tensor(logit[:, 0:n_tok, 0:routes], src,
                                  wide(rowmax[:, 0:n_tok], (1, n_tok), (0, routes)), ALU.subtract
                                  ).then_inc(S["logit_ready"], 1)
                dve.wait_ge(S["exp_ready"], e + 1)
                for t in range(n_tok):
                    last = dve.max(top[:, t, :], prob[:, t, 0:routes])
                then(last)
                if e < 2:
                    then(dve.memset(top[:, 0:n_tok, 2:8], -1.0))
                span = ROUTES_PAD if e < 2 else ROUTES
                for t in range(n_tok):
                    last = dve.match_replace(rest[:, t, 0:span], top[:, t, :], prob[:, t, 0:span], 0.0)
                then(last)
                then(dve.tensor_tensor(chosen[:, 0:n_tok, 0:routes], prob[:, 0:n_tok, 0:routes],
                                       rest[:, 0:n_tok, 0:routes], ALU.subtract))
                over = chosen if e < 2 else prob
                then(dve.tensor_reduce(norm[:, 0:n_tok], over[:, 0:n_tok, 0:routes], AX.X, ALU.add))
                then(dve.reciprocal(norm[:, 0:n_tok], norm[:, 0:n_tok]))
                then(dve.tensor_scalar(norm[:, 0:n_tok], norm[:, 0:n_tok], SCALE0 if e < 2 else SCALE1, None, ALU.mult))

            def spread(dst, src, n_tok):
                for t in range(n_tok):
                    last = dve.tensor_scalar(dst[:, t], wide(src[:, t, 0:NE], (1, NE), (0, RANK)), norm[:, t:t + 1],
                                             None, ALU.mult)
                last.then_inc(S["gate_ready"], 1)

            statistics(0)
            dve.wait_ge(S["vec_landed"], 64)
            then(dve.tensor_copy(ratio[:, 1:], disc[:, 0:ORDERS - 1]))
            then(dve.memset(ratio[:, 0:1], 0.0))
            dve.tensor_tensor(disc[:], ratio[:], disc[:], ALU.subtract).then_inc(S["ratio_diff"], 1)
            invert_std(0)
            normalize(0)
            normalize(1)
            split_lo(0)
            turned_lo(0)
            turned_lo(1)
            split_lo(1)
            split_lo(2)
            dve.wait_ge(S["const_ready"], 3)
            dve.wait_ge(S["ratio_ready"], 1)

            def later_term(half, o):
                k = 7 * half + o
                if o >= 2:
                    ins = dve.scalar_tensor_tensor(term_f[:, o % 2, :], delta[:], ratio[:, o - 1:o],
                                                   term_f[:, (o - 1) % 2, :], ALU.mult, ALU.mult)
                    if o == ORDER_MIN + 1:
                        then(ins)
                        ins = dve.tensor_tensor(term_f[:, o % 2, :], term_f[:, o % 2, :], keep[:], ALU.mult)
                    ins.then_inc(S["t_f"], 1)
                dve.wait_ge(S["t_hi"], k + 1)
                dve.tensor_tensor(term_lo[:, k % 3, :], term_f[:, o % 2, :], term_hi[:, k % 3, :].bitcast(F32),
                                  ALU.subtract).then_inc(S["t_lo"], 1)

            def lora_weighted(half):
                dve.wait_ge(S["l_b_ready"], half + 1)
                dve.wait_ge(S["lora_h_ready"], half + 1)
                dve.tensor_tensor(lora_h[:], slot_of(("l", half))[:, 1, :], lora_h[:], ALU.mult
                                  ).then_inc(S["hw_f_ready"], 1)
                dve.wait_ge(S["hw_hi_ready"], half + 1)
                dve.tensor_tensor(hw_lo[:], lora_h[:], hw_hi[:].bitcast(F32), ALU.subtract).then_inc(S["l_free"], 1)

            def take_out(half):
                for t in range(HT):
                    dve.wait_ge(S["out_ready"], HT * half + t + 1)
                    dve.tensor_tensor(x_sb[:, half * HT + t, :], bank[t][:, :], x_sb[:, half * HT + t, :], ALU.add
                                      ).then_inc(S["out_free"], 1)

            then(dve.tensor_copy(rw_hi[:].rearrange("p k n -> p (k n)"), rw_stage[:]))
            dve.tensor_tensor(rw_lo[:].rearrange("p k n -> p (k n)"), rw_stage[:],
                              rw_hi[:].rearrange("p k n -> p (k n)").bitcast(F32), ALU.subtract
                              ).then_inc(S["rw_ready"], 1)
            for half in range(2):
                ps = slot_of(("s", half))
                dve.wait_ge(S["s_ready"], half + 1)
                then(dve.tensor_scalar(delta[:], ps[:, 0, :], vec_sb[:, VEC_POINT:VEC_POINT + 1], None, ALU.subtract))
                then(dve.scalar_tensor_tensor(keep[:], delta[:], -1.0, delta[:], ALU.mult, ALU.max))
                dve.tensor_scalar(keep[:], keep[:], DELTA_MAX, None, ALU.is_le)
                k = 7 * half
                dve.wait_ge(S["t_hi"], k + 1)
                dve.scalar_tensor_tensor(term_f[:, 1, :], delta[:], ratio[:, 0:1], ps[:, 1, :], ALU.mult, ALU.mult
                                         ).then_inc(S["t_f"], 1)
                dve.tensor_tensor(term_lo[:, k % 3, :], ps[:, 1, :], term_hi[:, k % 3, :].bitcast(F32), ALU.subtract
                                  ).then_inc(S["t_lo"], 1)
                if half == 1:
                    take_out(0)
                for c in range(FC):
                    if c + 1 < FC:
                        split_lo(item_at[(f"ffn{c + 1}", half)])
                        if half == 0:
                            split_lo(item_at[(f"res{c + 1}", 0)])
                    elif half == 0:
                        split_lo(item_at[("gate_up", 1)])
                    else:
                        split_lo(item_at[("qk0", 0)])
                    k = half * FC + c
                    m = FSHORT if c == 0 else P
                    ps = slot_of(("f", k))
                    if c == 1:
                        lora_weighted(half)
                    if c == 0:
                        dve.wait_ge(S["f_ready"], k + 1)
                        dve.tensor_scalar(lgt[FSHORT:FSHORT + NE, :], ps[FSHORT:FSHORT + NE, 0, :],
                                          vec_sb[FSHORT:FSHORT + NE, VEC_ROUTER0:VEC_ROUTER0 + 1], None, ALU.add
                                          ).then_inc(S["lgt_ready"], 1)
                    dve.wait_ge(S["silu_ready"], k + 1)
                    if k >= 1:
                        dve.wait_ge(S["h_hi_ready"], k)
                        dve.wait_ge(S["f_free"], k)
                    dve.tensor_tensor(h_f[0:m, :], ps[0:m, 1, :], silu[0:m, :], ALU.mult).then_inc(S["h_f_ready"], 1)
                    dve.wait_ge(S["h_hi_ready"], k + 1)
                    dve.tensor_tensor(h_lo[0:m, c % 2, :], h_f[0:m, :], h_hi[0:m, c % 2, :].bitcast(F32),
                                      ALU.subtract).then_inc(S["f_free"], 1)
                    if c == 0:
                        dve.wait_ge(S["l_a_ready"], half + 1)
                        route(HT, NE, half)
                        spread(gate_x, chosen, HT)
                    if 1 <= c <= ORDERS:
                        later_term(half, c)
                    if c == 1 and half == 0:
                        statistics(1)
                    if c == 1 and half == 1:
                        statistics(2)
                    if c == 2:
                        invert_std(1 + half)
                        normalize(2 + 2 * half)
                    if c in X_AFTER:
                        q = 2 + 2 * half + X_AFTER.index(c)
                        turned_lo(q)
                        if q % 2 == 0:
                            normalize(q + 1)
                    if c == FC - 1:
                        if half == 0:
                            split_lo(item_at[("ffn0", 1)])
                        else:
                            split_lo(item_at[("qk1", 0)])
            take_out(1)
            statistics(3)
            invert_std(3)
            normalize(6)
            normalize(7)
            turned_lo(6)
            turned_lo(7)
            dve.wait_ge(S["const_ready"], 5)
            then(dve.tensor_copy(map_f[:], map_i[:]))
            then(dve.tensor_tensor(onehot[:], wide(map_f[:], (0, NE), (1, ROUTES)),
                                   wide(expert_id[:], (1, NE), (0, ROUTES)), ALU.is_equal))

            def project_lo(which, m):
                col = (VEC_Q if which == "q" else VEC_K) + m
                dve.wait_ge(S[f"{which}_hi"], m + 1)
                dve.scalar_tensor_tensor(nat[which, 1], slot_of((which, m))[:].rearrange("p a n -> p (a n)"),
                                         vec_sb[:, col:col + 1], nat[which, 0].bitcast(F32), ALU.add, ALU.subtract
                                         ).then_inc(S[f"{which}_free"], 1)

            dve.wait_ge(S["r_ready"], 1)
            dve.tensor_scalar(lgt1, slot_of(("r", 0))[0:ROUTES_PAD].rearrange("p a n -> p (a n)"),
                              vec_sb[0:ROUTES_PAD, VEC_ROUTER1:VEC_ROUTER1 + 1], None, ALU.add
                              ).then_inc(S["r_free"], 1)
            project_lo("q", 0)
            dve.wait_ge(S["lt_ready"], 1)
            route(NT, ROUTES, 2)
            for t in range(NT):
                prod = hw_f1[:, t * NE * ROUTES:(t + 1) * NE * ROUTES].rearrange(
                    "p (e n) -> p e n", e=NE)
                last = dve.tensor_tensor(prod, wide(chosen[:, t, 0:ROUTES], (0, NE), (1, ROUTES)), onehot[:], ALU.mult)
            then(last)
            then(dve.tensor_reduce(gate[:].rearrange("p t e -> p (t e)"),
                                   hw_f1[:, 0:NT * NE * ROUTES].rearrange("p (e n) -> p e n", n=ROUTES), AX.X, ALU.add))
            spread(gate_x1, gate, NT)
            project_lo("k", 0)
            for m, name in enumerate(("qk2", "qk3", "lora1"), 1):
                split_lo(item_at[(name, 0)])
                project_lo("q", m)
                project_lo("k", m)
            split_lo(item_at[("wv0", 0)])
            split_lo(item_at[("wv1", 0)])
            dve.wait_ge(S["w_ready"], 1)
            dve.wait_ge(S["a_free"], 1)
            dve.tensor_tensor(hw_f1, slot_of(("w", 0))[:].rearrange("p a n -> p (a n)"), lora_h1, ALU.mult
                              ).then_inc(S["w_free"], 1)
            dve.wait_ge(S["hw_hi_ready"], 3)
            dve.tensor_tensor(hw1[1], hw_f1, hw1[0].bitcast(F32), ALU.subtract
                              ).then_inc(S["hw1_ready"], 1)
            dve.wait_ge(S["bias_landed"], 48)
            dve.wait_ge(S["k_ones"], 1)

            def row_max(u):
                g, i, hh = u // UNITS, u % UNITS // GH, u % GH
                n = (i + 1) * P
                dve.wait_ge(S["max_ready"], u + 1)
                if g >= 2 and u % UNITS == 0:
                    dve.wait_ge(S["m_ready"], g - 1)
                score = slot_of(("max", u))[:].rearrange("p a n -> p (a n)")[:, 0:n]
                dve.tensor_tensor_reduce(score, score, causal[:, NT * P - n:], 1.0, -3.0e38, ALU.add, ALU.max,
                                         maxcol[:, g % 2, 2 * (hh % 2) + hh // 2, i:i + 1]).then_inc(S["max_free"], 1)

            def neg_max_lo(g):
                dve.wait_ge(S["m_hi"], g + 1)
                dve.scalar_tensor_tensor(negm[:, g % 2, 1, :], slot_of(("m", g))[0:GH * NT, 0, 0:P], -1.0,
                                         negm[:, g % 2, 0, :].bitcast(F32), ALU.mult, ALU.subtract
                                         ).then_inc(S["m_free"], 1)

            def invert_den(g, half):
                dve.wait_ge(S[f"den_landed{half}"], 16 * (g + 1))
                dve.reciprocal(den[:, half, :], den[:, half, :]).then_inc(S["den_inverted"], 1)

            def divide(m, half):
                k = 2 * m + half
                at = slice(half * HALF, (half + 1) * HALF)
                dve.wait_ge(S[f"u_landed{half}"], 32 * (2 * m + 2))
                dve.tensor_tensor(u_all[:, at], u_all[:, at], den_all[:, at], ALU.mult).then_inc(S["attn_f"], 1)

            def attn_split_lo(m, half):
                k = 2 * m + half
                at = slice(half * HALF, (half + 1) * HALF)
                dve.wait_ge(S["attn_hi_ready"], k + 1)
                dve.tensor_tensor(attn_lo[:, m, at], u_all[:, at], attn_hi[:, m, at].bitcast(F32), ALU.subtract
                                  ).then_inc(S["attn_lo_ready"], 1)

            for t in range(NT):
                for hh in range(GH - 1):
                    row_max(GH * t + hh)
                dve.wait_ge(S["v_done"], t + 1)
                dve.tensor_tensor(v_sb[:, t, :, 0:HD], bank[t % 4][:].rearrange("p (h d) -> p h d", d=HD),
                                  bv_bc.rearrange("p (h d) -> p h d", d=HD), ALU.add
                                  ).then_inc(S["v_free"], 1)
                row_max(GH * t + GH - 1)
                if t in (1, 3):
                    split_lo(item_at[(f"base{t // 2}", 0)])
            neg_max_lo(0)
            for t in range(NT):
                for hh in range(GH - 1):
                    row_max(UNITS + GH * t + hh)
                dve.wait_ge(S["y_done"], t + 1)
                dve.tensor_tensor(x_sb[:, t, :], bank[t % 4][:, :], x_sb[:, t, :], ALU.add).then_inc(S["y_free"], 1)
                row_max(UNITS + GH * t + GH - 1)
            neg_max_lo(1)
            blank(dve, 2)
            for g in range(GROUPS):
                for s in range(STEPS):
                    for kind, k in finished(g, s):
                        if kind == "max":
                            row_max(k)
                        elif kind == "m":
                            neg_max_lo(k)
                    if s == LAG + 3 and g > 0:
                        invert_den(g - 1, 1)
                    if s == HT + LAG + 3:
                        invert_den(g, 0)
                    if (g, s) in DIVIDE_AT:
                        divide(*DIVIDE_AT[g, s])
                        attn_split_lo(*DIVIDE_AT[g, s])
                    for name in SPLIT_AT.get((g, s), []):
                        split_lo(item_at[(name, 0)])
            invert_den(GROUPS - 1, 1)

            def take_out_project(t):
                dve.wait_ge(S["o_ready"], t + 1)
                dve.tensor_tensor(x_sb[:, t, :], o_bank(t), x_sb[:, t, :], ALU.add).then_inc(S["out_sb_ready"], 1)

            dve.wait_ge(S["y_biased"], NT)
            for t in range(HT):
                take_out_project(t)
            divide(KD - 1, 1)
            attn_split_lo(KD - 1, 1)
            for t in range(HT, NT):
                take_out_project(t)


def kernel(**inputs):
    import concourse.bacc as bacc
    from concourse.bass_utils import run_bass_kernel_spmd

    w = {k: np.asarray(v) for k, v in inputs.items()}
    stream, router1 = lay_out_weights(w)
    vec = np.zeros((P, VECS), np.float32)
    vec[:, VEC_POINT] = w["L0_attn_local_point"]
    vec[FSHORT:FSHORT + NE, VEC_ROUTER0] = w["L0_ffn_router_b"]
    vec[:ROUTES, VEC_ROUTER1] = w["L1_ffn_router_b"]
    vec[:, VEC_Q:VEC_Q + KD] = w["L1_attn_bq"].reshape(KD, P).T
    vec[:, VEC_K:VEC_K + KD] = w["L1_attn_bk"].reshape(KD, P).T
    arrays = {
        "stream": stream, "router1": router1.reshape(P, -1),
        "x": np.ascontiguousarray(w["L0_attn_hidden_states"].reshape(NT, P, D)), "vec": vec,
        "bias_rows": np.stack([w["L1_attn_bv"], w["L1_ffn_base_b"], w["L1_attn_bo"]]),
        "discount": w["L0_attn_discount_factor"], "expert_map": w["L1_ffn_expert_map"],
    }
    nc = bacc.Bacc("TRN2", target_bir_lowering=False, num_devices=1)
    args = [nc.dram_tensor(f"in_{n}", a.shape, mybir.dt.from_np(a.dtype), kind="ExternalInput").ap()
            for n, a in arrays.items()]
    y = nc.dram_tensor("out_y", (NT, P, D), F32, kind="ExternalOutput").ap()
    heads_dram = nc.dram_tensor("heads_dram", (KD, 2, 2 * GH, 2 * HD, TOK), F32).ap()
    max_dram = nc.dram_tensor("max_dram", (GROUPS, 2, GH, TOK), F32).ap()
    u_dram = nc.dram_tensor("u_dram", (2 * GROUPS, P, HALF), F32).ap()
    den_dram = nc.dram_tensor("den_dram", (2 * GROUPS, GH, HALF), F32).ap()
    build(nc, *args, heads_dram, max_dram, u_dram, den_dram, y)
    result = run_bass_kernel_spmd(nc, [{f"in_{n}": a for n, a in arrays.items()}], core_ids=[0])
    return result.results[0]["out_y"].reshape(1, TOK, D)
```

```python
from contextlib import ExitStack

import numpy as np

import concourse.bass as bass
from concourse import mybir

F32 = mybir.dt.float32
F32R = mybir.dt.float32r
BF16 = mybir.dt.bfloat16
I32 = mybir.dt.int32
ALU = mybir.AluOpType
ACT = mybir.ActivationFunctionType
AX = mybir.AxisListType

P = 128
TOK, D = 1024, 512
KD = D // P
NT = TOK // P
HALF = TOK // 2
HT = HALF // P
FF = 1248
FC = -(-FF // P)
FSHORT = FF - (FC - 1) * P
ORDERS = 6
ORDER_MIN = 4
DELTA_MAX = 2.5
NE = 8
RANK = 16
SCALE0 = 8.0 / RANK
SCALE1 = 32.0 / 16.0
ROUTES = 2 * NE - 1
ROUTES_PAD = 16
HEADS, HD = 32, 16
GH = 4
GROUPS = HEADS // GH
QK_ROWS = 3 * HD
SIDE = 64
DOT_ROWS = SIDE + QK_ROWS
ST_ROWS = DOT_ROWS + 2
DEN_COLS = GH * HALF // P
EPS = 1e-5
MASKED = -1.0e30
SLOT = 1024

RESIDENT = ["lora_a", "lora_b"]
for _c in range(7):
    RESIDENT += [f"down{_c}", f"term{_c}"]
RESIDENT += ["down7", "down8", "down9", "pad"]
RES_AT = {name: n for n, name in enumerate(RESIDENT)}


def weight_items():
    items, arrays = [], []

    def add(dest, name):
        if name not in arrays:
            arrays.append(name)
        items.append((dest, name))

    for half in range(2):
        add("ring", "gate_up")
        for c in range(FC):
            add("ring", f"ffn{c}")
            if half == 0:
                add("resident", f"res{c}")
    for m in range(KD):
        add("ring", f"qk{m}")
    add("ring", "lora1")
    for n in range(2):
        add(f"v{n}", f"wv{n}")
    for n in range(2):
        add(f"base{n}", f"base{n}")
    for n in range(2):
        add(f"wo{n}", f"wo{n}")
    return items, arrays


ITEMS, ARRAYS = weight_items()


def lay_out_weights(w):
    def kxm(a):
        t = a.T
        return t.reshape(t.shape[0] // P, P, t.shape[1]).transpose(1, 0, 2)

    ffn_gate, ffn_up = kxm(w["L0_attn_ffn_gate_w"]), kxm(w["L0_attn_ffn_up_w"])
    down = w["L0_attn_ffn_down_w"].T
    router0 = kxm(w["L0_ffn_router_w"])
    out = np.zeros((len(ARRAYS), P, SLOT), np.float32)
    at = {name: n for n, name in enumerate(ARRAYS)}

    def put(name, n, a):
        if a.ndim == 3:
            a = a.reshape(P, -1)
        out[at[name], :a.shape[0], n:n + a.shape[1]] = a

    def pair(name, left, right):
        v = out[at[name]].reshape(P, KD, 2, P)
        v[:, :, 0, :left.shape[2]] = left
        v[:, :, 1, :right.shape[2]] = right

    pair("gate_up", kxm(w["L0_attn_gate_w"]), kxm(w["L0_attn_up_w"]))
    bounds = [0, FSHORT] + [FSHORT + P * c for c in range(1, FC)]
    for c in range(FC):
        a, b = bounds[c], bounds[c + 1]
        left = ffn_gate[:, :, a:b]
        if c == 0:
            left = np.concatenate([left, router0], axis=2)
        pair(f"ffn{c}", left, ffn_up[:, :, a:b])

    def resident(name):
        if name == "lora_a":
            return kxm(w["L0_ffn_A"].reshape(NE * RANK, D)).reshape(P, -1)
        if name == "lora_b":
            return w["L0_ffn_Bm"].transpose(0, 2, 1).reshape(NE * RANK, D)
        if name == "term0":
            return w["L0_attn_local_approx_output"].T
        if name.startswith("term"):
            return w["L0_attn_fuse_weight"][:, :, int(name[4:]) - 1].T
        c = int(name[4:])
        return down[bounds[c]:bounds[c + 1]]

    for n, name in enumerate(RESIDENT):
        if name != "pad":
            put(f"res{n // 2}", (n % 2) * D, resident(name))
    wq, wk = kxm(w["L1_attn_Wq"]), kxm(w["L1_attn_Wk"])
    for m in range(KD):
        pair(f"qk{m}", wq[:, :, m * P:(m + 1) * P], wk[:, :, m * P:(m + 1) * P])
    put("lora1", 0, kxm(w["L1_ffn_A"].reshape(NE * RANK, D)))
    put("lora1", D, w["L1_ffn_B"].transpose(0, 2, 1).reshape(NE * RANK, D))
    for name, a in (("wv", w["L1_attn_Wv"]), ("base", w["L1_ffn_base_W"]), ("wo", w["L1_attn_Wo"])):
        t = kxm(a)
        for n in range(2):
            put(f"{name}{n}", 0, t[:, 2 * n:2 * n + 2])
    router1 = np.zeros((P, KD, ROUTES_PAD), np.float32)
    router1[:, :, :ROUTES] = kxm(w["L1_ffn_router_W"])
    return out, router1



VEC_POINT, VEC_ROUTER0, VEC_ROUTER1, VEC_Q, VEC_K, VEC_V = 0, 1, 2, 3, 3 + KD, 3 + 2 * KD
VECS = VEC_V + KD

QSTEPS = [(0, j) for j in range(HT)] + [(1, j) for j in range(NT)]
STEPS = len(QSTEPS)
DIAGONAL = [s for s, (half, j) in enumerate(QSTEPS) if j >= HT * half]
LAG = 2
NPROB = GH * (LAG + 1)
MAX_UNITS = [(i, hh, c, min(512, (i + 1) * P - c)) for i in range(NT) for hh in range(GH)
             for c in range(0, (i + 1) * P, 512)]
UNITS = len(MAX_UNITS)
UNIT_COST = 64
MAX_START = 6
MAX_END = 5
EARLY_UNITS = KD * NT
VECTOR_COLUMNS = 400
SPLIT_AT = {(0, 0): "wo0", (0, 1): "wo1"}
DIVIDE_AT = {(g, s): (g // 2 - 1, half) for g in range(2, GROUPS, 2) for half, s in ((0, 1), (1, 9))}
DIVIDE_AT[GROUPS - 1, STEPS - 2] = (KD - 1, 0)
OUT_AT = {0: (GROUPS - 1, 2), 1: (GROUPS - 1, 5)}
OUT_PARTS = 2 * (KD - 1)
X_AFTER = (3, 4)


def step_width(s):
    half, j = QSTEPS[s]
    return HALF - max(0, P * j - HALF * half)


def per_bank(s):
    return {P: 4, 2 * P: 2}.get(step_width(s), 1)


def banks_before(g, s):
    per_group = [GH // per_bank(n) for n in range(STEPS)]
    return g * sum(per_group) + sum(per_group[:s])


def max_plan():
    plan = {}
    for g in range(1, GROUPS):
        first = 0 if g == 1 else STEPS * (g - 2) + MAX_START + (g == 2)
        places = [(p // STEPS, p % STEPS, hh) for p in range(first, STEPS * (g - 1) + MAX_END + 1)
                  for hh in range(GH)]
        room = [GH * step_width(s) - 2 * VECTOR_COLUMNS * ((q, s) in DIVIDE_AT or (q, s) in SPLIT_AT)
                for q, s, _ in places]
        n = EARLY_UNITS if g == 1 else 0
        work = sum(MAX_UNITS[u][3] + UNIT_COST for u in range(n, UNITS))
        done = passed = 0
        for place, r in zip(places, room):
            passed += r
            while n < UNITS and done * sum(room) < passed * work:
                plan.setdefault(place, []).append(("max", g * UNITS + n, 0))
                done += MAX_UNITS[n][3] + UNIT_COST
                n += 1
        assert n == UNITS
    return plan


MAX_PLAN = max_plan()


def extras(g, s, hh):
    todo = list(MAX_PLAN.get((g, s, hh), []))
    if g + 1 < GROUPS and (s, hh) == (MAX_END + 1, GH - 1):
        todo.append(("m", g + 1, 0))
    for k, (g0, s0) in OUT_AT.items():
        part = GH * (s - s0) + hh
        if g == g0 and 0 <= part < OUT_PARTS:
            todo.append(("o", k, part))
    return todo


def psum_users():
    users = [("x", 0), ("x", 1)]
    for half in range(2):
        users += [("s", half), ("f", half * FC), ("l", half)]
        for c in range(1, FC):
            users.append(("f", half * FC + c))
            if c in X_AFTER:
                users.append(("x", 2 + 2 * half + X_AFTER.index(c)))
    users += [("r", 0)] + [(which, m) for m in range(KD) for which in ("q", "k")]
    users += [("a", 0), ("w", 0)]
    users = [(user, (2 * (n % 2), 2 * (n % 2) + 1)) for n, user in enumerate(users)]
    single = [("max", u) for u in range(UNITS)] + [("m", 0)] + [("max", UNITS + u) for u in range(EARLY_UNITS)]
    single += [(kind, k) for g in range(GROUPS) for s in range(STEPS) for hh in range(GH)
               for kind, k, _ in extras(g, s, hh) if kind != "o"]
    users += [(user, (n % 4,)) for n, user in enumerate(single)]
    return users + [(("o", n), (2 * n, 2 * n + 1)) for n in range(2)]


USERS = psum_users()
USER_AT = {u: n for n, (u, _) in enumerate(USERS)}


def build(nc, stream, router1, x_in, vec, bias_rows, discount, expert_map, heads_dram, max_dram, u_dram, den_dram, out):
    nodes = ExitStack()
    with nodes:
        def sem(name):
            return nodes.enter_context(nc.semaphore(name))

        def sb(stack, name, shape, dt=F32):
            return stack.enter_context(nc.sbuf_tensor(name, shape, dt))

        ident = sb(nodes, "ident", [P, P])
        causal = sb(nodes, "causal", [P, NT * P], BF16)
        x_sb = sb(nodes, "x_sb", [P, NT, D])
        xt_hi = sb(nodes, "xt_hi", [P, KD, TOK], F32R)
        xt_lo = sb(nodes, "xt_lo", [P, KD, TOK], F32R)
        stage = sb(nodes, "stage", [P, 2, SLOT])
        ring_hi = sb(nodes, "ring_hi", [P, 2, SLOT], F32R)
        ring_lo = sb(nodes, "ring_lo", [P, 2, SLOT], F32R)
        stats = sb(nodes, "stats", [P, NT, 6])
        mean_var = sb(nodes, "mean_var", [P, NT, 2])
        rstd = sb(nodes, "rstd", [P, NT])
        eps_col = sb(nodes, "eps_col", [P, 1])
        vec_sb = sb(nodes, "vec_sb", [P, VECS])
        disc = sb(nodes, "disc", [P, ORDERS])
        ratio = sb(nodes, "ratio", [P, ORDERS])
        logit = sb(nodes, "logit", [P, NT, ROUTES_PAD])
        prob = sb(nodes, "prob", [P, NT, ROUTES_PAD])
        rest = sb(nodes, "rest", [P, NT, ROUTES_PAD])
        chosen = sb(nodes, "chosen", [P, NT, ROUTES_PAD])
        top = sb(nodes, "top", [P, NT, 8])
        rowmax = sb(nodes, "rowmax", [P, NT])
        norm = sb(nodes, "norm", [P, NT])
        gate = sb(nodes, "gate", [P, NT, NE])
        map_i = sb(nodes, "map_i", [P, ROUTES], I32)
        map_f = sb(nodes, "map_f", [P, ROUTES])
        expert_id = sb(nodes, "expert_id", [P, NE])
        onehot = sb(nodes, "onehot", [P, NE, ROUTES])
        rw_stage = sb(nodes, "rw_stage", [P, KD * ROUTES_PAD])
        rw_hi = sb(nodes, "rw_hi", [P, KD, ROUTES_PAD], F32R)
        rw_lo = sb(nodes, "rw_lo", [P, KD, ROUTES_PAD], F32R)

        block0 = ExitStack()
        with block0:
            res_hi = sb(block0, "res_hi", [P, len(RESIDENT), D], F32R)
            res_lo = sb(block0, "res_lo", [P, len(RESIDENT), D], F32R)
            h_hi = sb(block0, "h_hi", [P, 2, HALF], F32R)
            h_lo = sb(block0, "h_lo", [P, 2, HALF], F32R)
            term_hi = sb(block0, "term_hi", [P, 3, HALF], F32R)
            term_lo = sb(block0, "term_lo", [P, 3, HALF], F32R)
            hw_hi = sb(block0, "hw_hi", [P, HALF], F32R)
            hw_lo = sb(block0, "hw_lo", [P, HALF], F32R)
            silu = sb(block0, "silu", [P, HALF])
            h_f = sb(block0, "h_f", [P, HALF])
            delta = sb(block0, "delta", [P, HALF])
            keep = sb(block0, "keep", [P, HALF])
            term_f = sb(block0, "term_f", [P, 2, HALF])
            lora_h = sb(block0, "lora_h", [P, HALF])
            gate_x = sb(block0, "gate_x", [P, HT, NE, RANK])
            lgt = sb(block0, "lgt", [P, HALF])
            xn = sb(block0, "xn", [P, 2, D])
        block1 = ExitStack()
        nodes.enter_context(block1)
        qst = sb(block1, "qst", [P, 2, GH, TOK], F32R)
        kst = sb(block1, "kst", [P, 2, 2, TOK], F32R)
        attn_hi = sb(block1, "attn_hi", [P, KD, TOK], F32R)
        attn_lo = sb(block1, "attn_lo", [P, KD, TOK], F32R)
        v_sb = sb(block1, "v_sb", [P, NT, HEADS, HD + 1])
        probs = sb(block1, "probs", [P, NPROB, HALF])
        u_sb = sb(block1, "u_sb", [P, 2, HALF])
        u_all, den_all = stage[:, 0, :], stage[:, 1, :]
        den = sb(block1, "den", [P, 2, DEN_COLS])
        maxcol = sb(block1, "maxcol", [P, 2, GH, NT])
        maxrest = sb(block1, "maxrest", [P, 2, GH, NT // 2])
        negm = sb(block1, "negm", [GH * NT, 2, 2, P], F32R)
        xn1 = probs[:, 8:10, :]
        bo_bc = probs[:, 10, :]
        y_sb = [probs[:, 8 + n, :] for n in range(2)]
        lgt1 = probs[0:ROUTES_PAD, 0:2, :].rearrange("p a n -> p (a n)")
        lora_h1 = probs[:, 2:4, :].rearrange("p a n -> p (a n)")
        gate_x1 = probs[:, 4:6, :].rearrange("p a (t e r) -> p (a t) e r", e=NE, r=RANK)
        hw_f1 = probs[:, 6:8, :].rearrange("p a n -> p (a n)")
        base_bc = u_sb[:, 1, :]

        slot = [nodes.enter_context(nc.psum_tensor(f"slot{n}", [P, 2, 512], F32)) for n in range(2)]
        bank = [nodes.enter_context(nc.psum_tensor(f"bank{n}", [P, 512], F32)) for n in range(4)]

        S = {name: sem(name) for name in (
            "ident_ready const_ready x_landed0 x_landed1 x_landed2 x_landed3 vec_landed "
            "w_landed0 w_landed1 w_hi w_lo "
            "stat_ready std_ready xn_ready x_turned xt_hi_ready x_free "
            "ratio_diff ratio_ready s_ready t_hi t_f t_lo t_used "
            "f_ready silu_ready h_f_ready h_hi_ready f_free h_used "
            "lgt_ready l_a_ready lora_h_ready logit_ready exp_ready gate_ready l_b_ready hw_f_ready hw_hi_ready l_free "
            "out_ready out_free bias_landed rw_ready hw1_ready "
            "q_ready q_hi q_free k_ready k_hi k_free r_ready r_free a_ready a_free lt_ready w_ready w_free "
            "v_done v_free y_done y_free "
            "max_ready max_free max_joined m_ready m_hi m_free "
            "q_stored k_stored stacks0 stacks1 stacks2 negm_stored negm_landed0 negm_landed1 u_stored0 u_stored1 "
            "st_ready exp_done masked pv_done u_free u_landed0 u_landed1 "
            "den_landed0 den_landed1 den_inverted den_stored "
            "attn_f attn_hi_ready attn_lo_ready y_biased y_added o_ready out_sb_ready stored dve k_ones blank blank2 "
        ).split()}

        def queries(g, side):
            if g % 3 == 2:
                return (ring_hi, ring_lo)[side][:]
            return qst[:, g % 3, 2 * side:2 * side + 2, :]

        def keys(g):
            if g % 3 == 2:
                return xt_hi[:, KD - 2:, :]
            return kst[:, g % 3]

        def slot_of(user):
            return slot[USERS[USER_AT[user]][1][0] // 2]

        def bank_of(user):
            n = USERS[USER_AT[user]][1][0]
            return slot[n // 2][:, n % 2, :]

        def freed(user):
            n = USER_AT[user]
            waits = []
            for b in USERS[n][1]:
                before = [u for u, at in USERS[:n] if b in at]
                if before:
                    kind, k = before[-1]
                    waits.append((S["t_lo"], 7 * k + 1) if kind == "s" else (S[f"{kind}_free"], k + 1))
            return waits[:1] if len(set(str(w) for w in waits)) == 1 else waits

        def h_done(k):
            half, c = k // FC, k % FC
            return (S["out_ready"], HT * (half + 1)) if c == FC - 1 else (S["h_used"], (FC - 1) * half + c + 1)

        def x_bank(q, n):
            return slot_of(("x", q))[:, n, :] if q < 6 else bank[2 * (q - 6) + n][:, :]

        def o_bank(t):
            return slot_of(("o", t // 2))[:, t % 2, :] if t < 4 else bank[t - 4][:, :]

        def wait_slot(pe, user):
            for f in freed(user):
                pe.wait_ge(*f)

        item_at, ring_at = {}, {}
        for n, (dest, name) in enumerate(ITEMS):
            item_at[(name, sum(1 for d, m in ITEMS[:n] if m == name))] = n
            if dest == "ring":
                ring_at[n] = len(ring_at)

        def ring_of(name, half=0):
            n = item_at[(name, half)]
            r = ring_at[n] % 2
            return n, ring_hi[:, r, :], ring_lo[:, r, :]

        hw1 = ring_of(f"qk{KD - 1}")[1:]

        def ring_done(r):
            name = [m for d, m in ITEMS if d == "ring"][r]
            half = int(r > FC)
            if name == "gate_up":
                return S["s_ready"], half + 1
            if name.startswith("ffn"):
                return S["f_ready"], half * FC + int(name[3:]) + 1
            return S["k_ready"], int(name[2:]) + 1

        def destination(n):
            dest, name = ITEMS[n]
            if dest == "ring":
                r = ring_at[n] % 2
                return ring_hi[:, r, :], ring_lo[:, r, :]
            if dest == "resident":
                c = int(name[3:])
                return tuple(t[:, 2 * c:2 * c + 2, :].rearrange("p a n -> p (a n)") for t in (res_hi, res_lo))
            i = int(dest[-1])
            if dest[0] == "v":
                return attn_hi[:, i, :], attn_lo[:, i, :]
            if dest[0] == "b":
                return attn_hi[:, 2 + i, :], attn_lo[:, 2 + i, :]
            return tuple(t[:, i, :] for t in (xt_hi, xt_lo))

        def res(name):
            return res_hi[:, RES_AT[name], :], res_lo[:, RES_AT[name], :]

        v_w = [t[:, 0:2, :].rearrange("p a (b n) -> p (a b) n", n=D) for t in (attn_hi, attn_lo)]
        base_w = [t[:, 2:4, :].rearrange("p a (b n) -> p (a b) n", n=D) for t in (attn_hi, attn_lo)]
        wo_w = [t[:, 0:2, :].rearrange("p a (b n) -> p (a b) n", n=D) for t in (xt_hi, xt_lo)]
        nat = {("q", 0): attn_hi[:, 2, :], ("q", 1): attn_lo[:, 2, :],
               ("k", 0): attn_hi[:, 3, :], ("k", 1): attn_lo[:, 3, :]}

        block = nodes.enter_context(nc.Block())

        @block.sync
        def _(sp):
            def weights(n):
                if n >= 2:
                    sp.wait_ge(S["w_lo"], n - 1)
                sp.dma_start(stage[:, n % 2, :], stream[ARRAYS.index(ITEMS[n][1])]).then_inc(S[f"w_landed{n % 2}"], 16)

            sp.dma_start(x_sb[:, 0, :], x_in[0]).then_inc(S["x_landed0"], 16)
            sp.dma_start(x_sb[:, 1, :], x_in[1]).then_inc(S["x_landed1"], 16)
            sp.dma_start(x_sb[:, 2:4, :], x_in[2:4].rearrange("t p d -> p t d")).then_inc(S["x_landed2"], 16)
            weights(0)
            weights(1)
            sp.dma_start(x_sb[:, 4:8, :], x_in[4:8].rearrange("t p d -> p t d")).then_inc(S["x_landed3"], 16)
            for n in range(2, item_at[("qk3", 0)] + 1):
                weights(n)

            def stack(g):
                m, z = g // 2, g % 3
                if g >= 3:
                    sp.wait_ge(S["st_ready"], banks_before(g - 2, 0))
                if g < 2:
                    sp.wait_ge(S["blank"], 3 * (g + 1))
                if g == 2:
                    sp.wait_ge(S["blank2"], 3)
                for n, which in enumerate("qk"):
                    sp.wait_ge(S[f"{which}_stored"], 32 * (m + 1))
                    for side in range(2):
                        first = heads_dram[m, n, GH * (g % 2) + side]
                        st = queries(g, side) if which == "q" else keys(g)
                        for row, rows in ((0, 2 * HD), (2 * HD, HD)) if which == "q" else ((0, HD), (HD, 2 * HD)):
                            at = SIDE * side + row
                            sp.dma_start(st[at:at + rows].bitcast(F32),
                                         bass.AP(first.tensor, first.offset,
                                                 [[TOK, rows], [2 * 2 * HD * TOK, 2], [1, TOK]])
                                         ).then_inc(S[f"stacks{z}"], 16)

            def store(which, m):
                sp.wait_ge(S[f"{which}_free"], m + 1)
                for part in range(2):
                    first = heads_dram[m, "qk".index(which), 0, part * HD]
                    sp.dma_start(bass.AP(first.tensor, first.offset, [[2 * HD * TOK, 2 * GH], [TOK, HD], [1, TOK]]),
                                 nat[which, part].bitcast(F32)).then_inc(S[f"{which}_stored"], 16)

            def neg_max(g):
                sp.wait_ge(S["m_free"], g + 1)
                first = max_dram[g, 0]
                sp.dma_start(bass.AP(first.tensor, first.offset, [[P, GH * NT], [GH * TOK, 2], [1, P]]),
                             negm[:, g % 2].bitcast(F32)).then_inc(S["negm_stored"], 16)
                sp.wait_ge(S["negm_stored"], 16 * (g + 1))
                for side in range(2):
                    first = max_dram[g, 0, 2 * side]
                    sp.dma_start(queries(g, side)[DOT_ROWS:ST_ROWS].bitcast(F32),
                                 bass.AP(first.tensor, first.offset, [[GH * TOK, 2], [1, 2 * TOK]])
                                 ).then_inc(S[f"negm_landed{g % 2}"], 16)

            def gather(g, half):
                e = 2 * g + half
                sp.wait_ge(S["u_free"], e + 1)
                if e == 0:
                    sp.wait_ge(S["w_lo"], len(ITEMS))
                if g % 2 == 0 and g > 0:
                    sp.wait_ge(S["attn_lo_ready"], 2 * (g // 2 - 1) + half + 1)
                sp.dma_start(u_dram[e], u_sb[:, e % 2, :]).then_inc(S[f"u_stored{half}"], 16)
                sp.wait_ge(S[f"u_stored{half}"], 16 * (g + 1))
                to = (slice(GH * HD * (g % 2), GH * HD * (g % 2 + 1)), slice(half * HALF, (half + 1) * HALF))
                sp.dma_start(u_all[to], bass.AP(u_dram.tensor, u_dram[e, 0].offset, [[32 * HALF, GH], [1, HD * HALF]])
                             ).then_inc(S[f"u_landed{half}"], 16)
                sp.dma_start(den[:, half, :],
                             bass.AP(u_dram.tensor, u_dram[e, HD].offset,
                                     [[32 * HALF, GH], [DEN_COLS, P // GH], [1, DEN_COLS]])
                             ).then_inc(S[f"den_landed{half}"], 16)

            def spread_den(g, half):
                e = 2 * g + half
                sp.wait_ge(S["den_inverted"], e + 1)
                sp.dma_start(den_dram[e].rearrange("h (c n) -> (h c) n", n=DEN_COLS), den[:, half, :]
                             ).then_inc(S["den_stored"], 16)
                sp.wait_ge(S["den_stored"], 16 * (e + 1))
                to = (slice(GH * HD * (g % 2), GH * HD * (g % 2 + 1)), slice(half * HALF, (half + 1) * HALF))
                sp.dma_start(den_all[to], bass.AP(den_dram.tensor, den_dram[e, 0].offset,
                                                  [[HALF, GH], [0, HD], [1, HALF]])
                             ).then_inc(S[f"u_landed{half}"], 16)

            for m, name in enumerate(("lora1", "wv0", "wv1", "base0")):
                store("q", m)
                store("k", m)
                weights(item_at[(name, 0)])
                if m in (1, 2):
                    stack(m - 1)
            weights(item_at[("base1", 0)])
            neg_max(0)
            for name in ("wo0", "wo1"):
                weights(item_at[(name, 0)])
            for g in range(GROUPS):
                for s in range(STEPS):
                    if s == 0 and g + 2 < GROUPS:
                        stack(g + 2)
                    if s == LAG and g > 0:
                        gather(g - 1, 1)
                    if s == LAG + 3 and g > 0:
                        spread_den(g - 1, 1)
                    if s == HT + LAG:
                        gather(g, 0)
                    if s == HT + LAG + 3:
                        spread_den(g, 0)
                    if s == MAX_END + 2 and g + 1 < GROUPS:
                        neg_max(g + 1)
            def store_out(t):
                sp.wait_ge(S["out_sb_ready"], t + 1)
                sp.dma_start(out[t], x_sb[:, t, :]).then_inc(S["stored"], 16)

            gather(GROUPS - 1, 1)
            spread_den(GROUPS - 1, 1)
            for t in range(NT):
                store_out(t)
            sp.wait_ge(S["stored"], 16 * NT)

        @block.gpsimd
        def _(pool):
            pool.memset(ident[:], 0.0).then_inc(S["ident_ready"], 1)
            pool.wait_ge(S["ident_ready"], 1)
            pool.affine_select(out=ident[:], in_=ident[:], compare_op=ALU.not_equal, fill=1.0, base=0,
                               pattern=[[-1, P]], channel_multiplier=1).then_inc(S["ident_ready"], 1)
            pool.memset(eps_col[:], EPS).then_inc(S["const_ready"], 1)
            pool.memset(prob[:], -1.0).then_inc(S["const_ready"], 1)
            pool.memset(causal[:], 0.0).then_inc(S["const_ready"], 1)
            pool.dma_start(vec_sb[:], vec).then_inc(S["vec_landed"], 16)
            pool.dma_start(disc[:], discount.partition_broadcast(P)).then_inc(S["vec_landed"], 16)
            pool.dma_start(map_i[:], expert_map.partition_broadcast(P)).then_inc(S["vec_landed"], 16)
            pool.dma_start(rw_stage[:], router1).then_inc(S["vec_landed"], 16)
            pool.wait_ge(S["const_ready"], 3)
            pool.affine_select(out=causal[:, (NT - 1) * P:], in_=causal[:, (NT - 1) * P:], compare_op=ALU.is_ge,
                               fill=MASKED, base=0, pattern=[[-1, P]], channel_multiplier=1
                               ).then_inc(S["const_ready"], 1)
            pool.iota(expert_id[:], pattern=[[1, NE]], base=0, channel_multiplier=0,
                      allow_small_or_imprecise_dtypes=True).then_inc(S["const_ready"], 1)
            pool.wait_ge(S["out_free"], 8)
            for n, row in enumerate((base_bc, bo_bc)):
                pool.dma_start(row, bias_rows[n].partition_broadcast(P)).then_inc(S["bias_landed"], 16)

            def blank(g):
                for side in range(2):
                    pool.memset(queries(g, side).rearrange("p b n -> p (b n)").bitcast(F32), 0.0
                                ).then_inc(S["blank"], 1)
                pool.memset(keys(g).rearrange("p b n -> p (b n)").bitcast(F32), 1.0).then_inc(S["blank"], 1)

            blank(0)
            pool.memset(v_sb[:], 1.0).then_inc(S["k_ones"], 1)
            blank(1)
            pool.wait_ge(S["bias_landed"], 32)
            pool.tensor_tensor(bo_bc, bo_bc, base_bc, ALU.add).then_inc(S["k_ones"], 1)
            pool.wait_ge(S["k_ones"], 2)
            pool.wait_ge(S["xn_ready"], 2 * NT)
            for t in range(NT):
                pool.tensor_tensor(x_sb[:, t, :], x_sb[:, t, :], bo_bc, ALU.add).then_inc(S["y_biased"], 1)
            for t in range(NT):
                pool.wait_ge(S["y_free"], t + 1)
                pool.wait_ge(S["y_biased"], t + 1)
                pool.tensor_tensor(x_sb[:, t, :], x_sb[:, t, :], y_sb[t % 2], ALU.add).then_inc(S["y_added"], 1)
            for side in range(2):
                pool.memset(queries(2, side).rearrange("p b n -> p (b n)").bitcast(F32), 0.0).then_inc(S["blank2"], 1)
            for g in range(GROUPS):
                for s, (half, j) in enumerate(QSTEPS):
                    if s in DIAGONAL:
                        b = GH * (STEPS * g + s) % NPROB
                        pool.wait_ge(S["exp_done"], banks_before(g, s + 1))
                        part = probs[:, b:b + GH, 0:P]
                        pool.affine_select(out=part, in_=part, compare_op=ALU.is_ge, fill=0.0, base=0,
                                           pattern=[[0, GH], [1, P]], channel_multiplier=-1
                                           ).then_inc(S["masked"], 1)

        @block.scalar
        def _(act):
            def split_hi(n):
                dest, name = ITEMS[n]
                act.wait_ge(S[f"w_landed{n % 2}"], 16 * (n // 2 + 1))
                if dest == "ring" and ring_at[n] >= 2:
                    act.wait_ge(*ring_done(ring_at[n] - 2))
                if dest == "v0":
                    act.wait_ge(S["out_free"], 8)
                if dest == "base0":
                    act.wait_ge(S["q_stored"], 32 * KD)
                    act.wait_ge(S["k_stored"], 32 * KD)
                if dest == "wo0":
                    act.wait_ge(S["y_done"], NT)
                act.activation(destination(n)[0], stage[:, n % 2, :], ACT.Copy).then_inc(S["w_hi"], 1)

            def std(q):
                act.wait_ge(S["stat_ready"], q + 1)
                t = 2 * (q % 4)
                if q == 0:
                    act.wait_ge(S["const_ready"], 1)
                act.activation(rstd[:, t:t + 2], mean_var[:, t:t + 2, 1], ACT.Sqrt, bias=eps_col[:, 0:1]
                               ).then_inc(S["std_ready"], 1)

            def turned_hi(q):
                t = 2 * (q % 4) * P
                act.wait_ge(S["x_turned"], q + 1)
                if q < 6:
                    act.activation(xt_hi[:, :, t:t + 2 * P].rearrange("p k (t n) -> p t k n", t=2),
                                   slot_of(("x", q))[:].rearrange("p t (k n) -> p t k n", k=KD), ACT.Copy
                                   ).then_inc(S["xt_hi_ready"], 1)
                else:
                    for n in range(2):
                        last = act.activation(xt_hi[:, :, t + n * P:t + (n + 1) * P],
                                              x_bank(q, n).rearrange("p (k n) -> p k n", k=KD), ACT.Copy)
                    last.then_inc(S["xt_hi_ready"], 1)

            def term(half, o):
                k = 7 * half + o
                if o == 0:
                    act.wait_ge(S["s_ready"], half + 1)
                else:
                    act.wait_ge(S["t_f"], 6 * half + o)
                if k >= 3:
                    act.wait_ge(S["t_used"], k - 2)
                src = slot_of(("s", half))[:, 1, :] if o == 0 else term_f[:, o % 2, :]
                act.activation(term_hi[:, k % 3, :], src, ACT.Copy).then_inc(S["t_hi"], 1)

            std(0)
            split_hi(0)
            std(1)
            turned_hi(0)
            turned_hi(1)
            act.wait_ge(S["ratio_diff"], 1)
            act.activation(ratio[:], disc[:], ACT.Exp).then_inc(S["ratio_ready"], 1)
            for n in range(1, 3):
                split_hi(n)
            for half in range(2):
                term(half, 0)
                for c in range(FC):
                    if c + 1 < FC:
                        split_hi(item_at[(f"ffn{c + 1}", half)])
                        if half == 0:
                            split_hi(item_at[(f"res{c + 1}", 0)])
                    elif half == 0:
                        split_hi(item_at[("gate_up", 1)])
                    else:
                        split_hi(item_at[("qk0", 0)])
                    k = half * FC + c
                    m = FSHORT if c == 0 else P
                    if c == 1:
                        act.wait_ge(S["hw_f_ready"], half + 1)
                        act.activation(hw_hi[:], lora_h[:], ACT.Copy).then_inc(S["hw_hi_ready"], 1)
                    act.wait_ge(S["f_ready"], k + 1)
                    if k >= 1:
                        act.wait_ge(S["h_f_ready"], k)
                    act.activation(silu[0:m, :], slot_of(("f", k))[0:m, 0, :], ACT.Silu).then_inc(S["silu_ready"], 1)
                    act.wait_ge(S["h_f_ready"], k + 1)
                    if k >= 2:
                        act.wait_ge(*h_done(k - 2))
                    act.activation(h_hi[0:m, c % 2, :], h_f[0:m, :], ACT.Copy).then_inc(S["h_hi_ready"], 1)
                    if c == 0:
                        act.wait_ge(S["l_a_ready"], half + 1)
                        act.activation(lora_h[:], slot_of(("l", half))[:, 0, :], ACT.Copy
                                       ).then_inc(S["lora_h_ready"], 1)
                        act.wait_ge(S["const_ready"], 2)
                        act.wait_ge(S["logit_ready"], half + 1)
                        act.activation(prob[:, 0:HT, 0:NE], logit[:, 0:HT, 0:NE], ACT.Exp).then_inc(S["exp_ready"], 1)
                    if 1 <= c <= ORDERS:
                        term(half, c)
                    if c == 2:
                        std(2 + 2 * half)
                        std(3 + 2 * half)
                    if c in X_AFTER:
                        turned_hi(2 + 2 * half + X_AFTER.index(c))
                    if c == FC - 1:
                        if half == 0:
                            split_hi(item_at[("ffn0", 1)])
                        else:
                            split_hi(item_at[("qk1", 0)])

            std(6)
            std(7)
            turned_hi(6)
            turned_hi(7)

            def project_hi(which, m):
                bias = vec_sb[:, VEC_Q + m:VEC_Q + m + 1] if which == "q" else vec_sb[:, VEC_K + m:VEC_K + m + 1]
                act.wait_ge(S[f"{which}_ready"], m + 1)
                if m >= 1:
                    act.wait_ge(S[f"{which}_stored"], 32 * m)
                act.activation(nat[which, 0], slot_of((which, m))[:].rearrange("p a n -> p (a n)"), ACT.Identity,
                               bias=bias).then_inc(S[f"{which}_hi"], 1)

            def neg_max_hi(g):
                act.wait_ge(S["m_ready"], g + 1)
                if g >= 2:
                    act.wait_ge(S["negm_stored"], 16 * (g - 1))
                act.activation(negm[:, g % 2, 0, :], bank_of(("m", g))[0:GH * NT, 0:P], ACT.Copy, scale=-1.0
                               ).then_inc(S["m_hi"], 1)

            def take_u(g, half):
                e = 2 * g + half
                act.wait_ge(S["pv_done"], STEPS * g + HT + NT * half)
                if g >= 1:
                    act.wait_ge(S[f"u_stored{half}"], 16 * g)
                act.activation(u_sb[:, e % 2, :], bank[3][:], ACT.Copy).then_inc(S["u_free"], 1)

            def attn_split_hi(m, half):
                k = 2 * m + half
                act.wait_ge(S["attn_f"], k + 1)
                if k == 0:
                    act.wait_ge(S["y_done"], NT)
                at = slice(half * HALF, (half + 1) * HALF)
                act.activation(attn_hi[:, m, at], u_all[:, at], ACT.Identity, bias=vec_sb[:, VEC_V + m:VEC_V + m + 1]
                               ).then_inc(S["attn_hi_ready"], 1)

            project_hi("q", 0)
            act.wait_ge(S["logit_ready"], 3)
            act.activation(prob[:, :, 0:ROUTES], logit[:, :, 0:ROUTES], ACT.Exp).then_inc(S["exp_ready"], 1)
            project_hi("k", 0)
            for m, names in enumerate((["qk2"], ["qk3"], ["lora1", "wv0"]), 1):
                for name in names:
                    split_hi(item_at[(name, 0)])
                project_hi("q", m)
                project_hi("k", m)
            split_hi(item_at[("wv1", 0)])
            act.wait_ge(S["a_ready"], 1)
            act.activation(lora_h1, slot_of(("a", 0))[:].rearrange("p a n -> p (a n)"), ACT.Copy
                           ).then_inc(S["a_free"], 1)
            act.wait_ge(S["w_free"], 1)
            act.wait_ge(S["k_ready"], KD)
            act.activation(hw1[0], hw_f1, ACT.Copy).then_inc(S["hw_hi_ready"], 1)
            act.wait_ge(S["k_ones"], 1)
            for t in range(NT):
                act.wait_ge(S["v_done"], t + 1)
                act.activation(v_sb[:, t, :, 0:HD], bank[t % 4][:].rearrange("p (h d) -> p h d", d=HD), ACT.Copy
                               ).then_inc(S["v_free"], 1)
                if t in (1, 3):
                    split_hi(item_at[(f"base{t // 2}", 0)])
            neg_max_hi(0)
            for t in range(NT):
                act.wait_ge(S["y_done"], t + 1)
                if t >= 2:
                    act.wait_ge(S["y_added"], t - 1)
                act.activation(y_sb[t % 2], bank[t % 4][:, :], ACT.Copy).then_inc(S["y_free"], 1)
            for g in range(GROUPS):
                for s, (half, j) in enumerate(QSTEPS):
                    if s == HT + LAG:
                        take_u(g, 0)
                    if s == LAG and g > 0:
                        take_u(g - 1, 1)
                    n, heads = step_width(s), per_bank(s)
                    if STEPS * g + s > LAG:
                        act.wait_ge(S["pv_done"], STEPS * g + s - LAG)
                    elif s == LAG:
                        act.wait_ge(S["y_added"], NT)
                    for hh in range(0, GH, heads):
                        b = banks_before(g, s) + hh // heads
                        to = (GH * (STEPS * g + s) + hh) % NPROB
                        act.wait_ge(S["st_ready"], b + 1)
                        act.activation(probs[:, to:to + heads, 0:n],
                                       bank[b % 3][:, 0:heads * n].rearrange("p (h n) -> p h n", n=n),
                                       ACT.Exp, scale=HD ** -0.5).then_inc(S["exp_done"], 1)
                    if s == MAX_END + 1 and g + 1 < GROUPS:
                        neg_max_hi(g + 1)
                    if (g, s - 1) in DIVIDE_AT:
                        attn_split_hi(*DIVIDE_AT[g, s - 1])
                    if (g, s) in SPLIT_AT:
                        split_hi(item_at[(SPLIT_AT[g, s], 0)])
            take_u(GROUPS - 1, 1)
            attn_split_hi(KD - 1, 1)

        @block.tensor
        def _(pe):
            def product(out_ap, a, b, start, stop):
                pe.matmul(out_ap, a[0], b[0], start=start, stop=False)
                pe.matmul(out_ap, a[0], b[1], start=False, stop=False)
                return pe.matmul(out_ap, a[1], b[0], start=False, stop=stop)

            xt = (xt_hi, xt_lo)

            def turn(q):
                src = xn if q < 4 + 2 else xn1
                if q < 6:
                    wait_slot(pe, ("x", q))
                else:
                    pe.wait_ge(S["out_free"], 2 * HT)
                for n in range(2):
                    pe.wait_ge(S["xn_ready"], 2 * q + n + 1)
                    for k in range(KD):
                        last = pe.transpose(x_bank(q, n)[:, k * P:(k + 1) * P],
                                            src[:, n, k * P:(k + 1) * P], ident[:])
                last.then_inc(S["x_turned"], 1)

            def from_xt(dst, w, m0, m1, tok0, n, last_sem=None):
                for k in range(KD):
                    last = product(dst, (w[0][:, k, m0:m1], w[1][:, k, m0:m1]),
                                   (xt_hi[:, k, tok0:tok0 + n], xt_lo[:, k, tok0:tok0 + n]), k == 0, k == KD - 1)
                return last

            def weight(name, half=0):
                n, hi, lo = ring_of(name, half)
                pe.wait_ge(S["w_lo"], n + 1)
                return tuple(t.rearrange("p (k m) -> p k m", k=KD) for t in (hi, lo))

            pe.wait_ge(S["ident_ready"], 2)
            turn(0)
            turn(1)
            for half in range(2):
                tok0 = half * HALF
                pe.wait_ge(S["x_free"], 2 + 2 * half)
                w = weight("gate_up", half)
                ps = slot_of(("s", half))
                wait_slot(pe, ("s", half))
                from_xt(ps[:, 0, :], w, 0, P, tok0, HALF)
                from_xt(ps[:, 1, :], w, P, 2 * P, tok0, HALF).then_inc(S["s_ready"], 1)

                def out_products(a, names, sem_name, start=False, stop=False, k_rows=P):
                    for t in range(HT):
                        last = product(bank[t][:, :], tuple(x[0:k_rows, t * P:(t + 1) * P] for x in a),
                                       tuple(x[0:k_rows] for x in res(names)), start, stop)
                        if stop:
                            last.then_inc(S["out_ready"], 1)
                    if sem_name and not stop:
                        last.then_inc(S[sem_name], 1)
                    return last

                def down(c):
                    k = half * FC + c
                    pe.wait_ge(S["f_free"], k + 1)
                    pe.wait_ge(S["w_lo"], res_item(f"down{c}") + 1)
                    if c == 0 and half == 1:
                        pe.wait_ge(S["out_free"], HT)
                    last = out_products((h_hi[:, c % 2, :], h_lo[:, c % 2, :]), f"down{c}", "h_used",
                                        start=(c == 0), stop=(c == FC - 1), k_rows=FSHORT if c == 0 else P)
                    return last

                def res_item(name):
                    return item_at[(f"res{RES_AT[name] // 2}", 0)]

                for c in range(FC):
                    k = half * FC + c
                    w = weight(f"ffn{c}", half)
                    wait_slot(pe, ("f", k))
                    ps = slot_of(("f", k))
                    mg, mu = (FSHORT + NE, FSHORT) if c == 0 else (P, P)
                    from_xt(ps[0:mg, 0, :], w, 0, mg, tok0, HALF)
                    from_xt(ps[0:mu, 1, :], w, P, P + mu, tok0, HALF).then_inc(S["f_ready"], 1)
                    if c == 0:
                        wait_slot(pe, ("l", half))
                        pe.wait_ge(S["w_lo"], res_item("lora_a") + 1)
                        ps = slot_of(("l", half))
                        w = tuple(t.rearrange("p (k m) -> p k m", k=KD) for t in res("lora_a"))
                        from_xt(ps[:, 0, :], w, 0, P, tok0, HALF)
                        pe.wait_ge(S["lgt_ready"], half + 1)
                        for t in range(HT):
                            last = pe.transpose(ps[:, 1, t * NE:(t + 1) * NE],
                                                lgt[FSHORT:FSHORT + NE, t * P:(t + 1) * P],
                                                ident[FSHORT:FSHORT + NE, FSHORT:FSHORT + NE])
                        last.then_inc(S["l_a_ready"], 1)
                    if c == 1:
                        pe.wait_ge(S["gate_ready"], half + 1)
                        ps = slot_of(("l", half))
                        for t in range(HT):
                            last = pe.transpose(ps[:, 1, t * P:(t + 1) * P],
                                                gate_x[:, t].rearrange("p e r -> p (e r)"), ident[:])
                        last.then_inc(S["l_b_ready"], 1)
                    if c in X_AFTER:
                        turn(2 + 2 * half + X_AFTER.index(c))
                    if c >= 1:
                        down(c - 1)
                        if c - 1 <= ORDERS:
                            o = 7 * half + c - 1
                            pe.wait_ge(S["t_lo"], o + 1)
                            out_products((term_hi[:, o % 3, :], term_lo[:, o % 3, :]), f"term{c - 1}", "t_used")
                    if c == FC - 2:
                        pe.wait_ge(S["l_free"], half + 1)
                        out_products((hw_hi, hw_lo), "lora_b", None)
                down(FC - 1)
            def project(which, m, halves=range(2)):
                w = weight(f"qk{m}")
                at = 0 if which == "q" else P
                if 0 in halves:
                    wait_slot(pe, (which, m))
                for n in halves:
                    last = from_xt(slot_of((which, m))[:, n, :], w, at, at + P, n * HALF, HALF)
                if 1 in halves:
                    last.then_inc(S[f"{which}_ready"], 1)

            def route_logits(n):
                return from_xt(slot_of(("r", 0))[0:ROUTES_PAD, n, :], (rw_hi, rw_lo), 0, ROUTES_PAD, n * HALF, HALF)

            wait_slot(pe, ("r", 0))
            pe.wait_ge(S["rw_ready"], 1)
            route_logits(0)
            project("q", 0, [0])
            turn(6)
            turn(7)

            pe.wait_ge(S["x_free"], 8)
            route_logits(1).then_inc(S["r_ready"], 1)
            project("q", 0, [1])
            pe.wait_ge(S["r_free"], 1)
            pe.wait_ge(S["out_free"], 8)
            for t in range(NT):
                last = pe.transpose(bank[0][:, t * ROUTES_PAD:(t + 1) * ROUTES_PAD], lgt1[:, t * P:(t + 1) * P],
                                    ident[0:ROUTES_PAD, 0:ROUTES_PAD])
            last.then_inc(S["lt_ready"], 1)
            project("k", 0)
            for m in range(1, KD):
                project("q", m)
                project("k", m)
            pe.wait_ge(S["w_lo"], item_at[("lora1", 0)] + 1)
            wait_slot(pe, ("a", 0))
            n1, hi1, lo1 = ring_of("lora1")
            a1 = tuple(t[:, 0:D].rearrange("p (k m) -> p k m", k=KD) for t in (hi1, lo1))
            b1 = (hi1[:, D:], lo1[:, D:])
            for n in range(2):
                last = from_xt(slot_of(("a", 0))[:, n, :], a1, 0, P, n * HALF, HALF)
            last.then_inc(S["a_ready"], 1)

            def maxima(u):
                g = u // UNITS
                i, hh, c, n = MAX_UNITS[u % UNITS]
                wait_slot(pe, ("max", u))
                if u % UNITS == 0:
                    pe.wait_ge(S[f"stacks{g % 3}"], 128 * (g // 3 + 1))
                pe.matmul(bank_of(("max", u))[:, 0:n], queries(g, hh % 2)[0:DOT_ROWS, hh // 2, i * P:(i + 1) * P],
                          keys(g)[0:DOT_ROWS, hh // 2, c:c + n], start=True, stop=True).then_inc(S["max_ready"], 1)

            def turn_maxima(g):
                pe.wait_ge(S["max_joined"], g + 1)
                wait_slot(pe, ("m", g))
                pe.transpose(bank_of(("m", g))[0:GH * NT, 0:P],
                             maxcol[:, g % 2].rearrange("p h i -> p (h i)"), ident[:]).then_inc(S["m_ready"], 1)

            def values(t):
                if t >= 4:
                    pe.wait_ge(S["v_free"], t - 3)
                for k in range(KD):
                    last = product(bank[t % 4][:, :], tuple(x[:, k, t * P:(t + 1) * P] for x in xt),
                                   tuple(x[:, k, :] for x in v_w), k == 0, k == KD - 1)
                    if k == KD - 1:
                        last.then_inc(S["v_done"], 1)
                    p = GH * t + k
                    for u in range(UNITS * p // (KD * NT), UNITS * (p + 1) // (KD * NT)):
                        maxima(u)

            def linear(t):
                if t == 0:
                    pe.wait_ge(S["v_free"], NT)
                if t >= 4:
                    pe.wait_ge(S["y_free"], t - 3)
                for k in range(KD):
                    product(bank[t % 4][:, :], tuple(x[:, k, t * P:(t + 1) * P] for x in xt),
                            tuple(x[:, k, :] for x in base_w), k == 0, False)
                    if t == 0 and k == 1:
                        turn_maxima(0)
                        maxima(UNITS)
                    if t > 0 or k > 0:
                        maxima(UNITS + 4 * t + k)
                product(bank[t % 4][:, :], tuple(x[:, t * P:(t + 1) * P] for x in hw1), b1, False, True
                        ).then_inc(S["y_done"], 1)

            pe.wait_ge(S["gate_ready"], 3)
            wait_slot(pe, ("w", 0))
            for t in range(NT):
                last = pe.transpose(slot_of(("w", 0))[:, t // 4, t % 4 * P:(t % 4 + 1) * P],
                                    gate_x1[:, t].rearrange("p e r -> p (e r)"), ident[:])
            last.then_inc(S["w_ready"], 1)
            pe.wait_ge(S["w_lo"], item_at[("wv1", 0)] + 1)
            for t in range(NT):
                values(t)
            pe.wait_ge(S["w_lo"], item_at[("base1", 0)] + 1)
            pe.wait_ge(S["hw1_ready"], 1)
            for t in range(NT):
                linear(t)

            def score(g, s, hh):
                half, j = QSTEPS[s]
                heads = per_bank(s)
                b = banks_before(g, s) + hh // heads
                n = step_width(s)
                q0 = HALF * (half + 1) - n
                if hh % heads == 0 and b >= 3:
                    pe.wait_ge(S["exp_done"], b - 2)
                if b == 0:
                    pe.wait_ge(S["v_free"], NT)
                    pe.wait_ge(S["y_free"], NT)
                if s == 0 and hh == 0:
                    pe.wait_ge(S[f"negm_landed{g % 2}"], 32 * (g // 2 + 1))
                at = hh % heads * n
                last = pe.matmul(bank[b % 3][:, at:at + n], keys(g)[0:ST_ROWS, hh // 2, j * P:(j + 1) * P],
                                 queries(g, hh % 2)[0:ST_ROWS, hh // 2, q0:q0 + n], start=True, stop=True)
                if hh % heads == heads - 1:
                    last.then_inc(S["st_ready"], 1)

            def weigh_values(k):
                g, s = k // STEPS, k % STEPS
                half, j = QSTEPS[s]
                c0 = max(0, P * j - HALF * half)
                pe.wait_ge(S["exp_done"], banks_before(g, s + 1))
                if s in DIAGONAL:
                    pe.wait_ge(S["masked"], NT * g + DIAGONAL.index(s) + 1)
                if j == 0 and 2 * g + half > 0:
                    pe.wait_ge(S["u_free"], 2 * g + half)
                stop = s in (HT - 1, STEPS - 1)
                for hh in range(GH):
                    last = pe.matmul(bank[3][32 * hh:32 * hh + HD + 1, c0:HALF], v_sb[:, j, GH * g + hh, :],
                                     probs[:, (GH * k + hh) % NPROB, 0:HALF - c0], start=(j == 0), stop=stop)
                last.then_inc(S["pv_done"], 1)
                return last


            def out_project(t, k):
                return product(o_bank(t), tuple(x[:, k, t * P:(t + 1) * P] for x in (attn_hi, attn_lo)),
                               tuple(x[:, k, :] for x in wo_w), k == 0, k == KD - 1)

            for g in range(GROUPS):
                for s in range(STEPS):
                    for hh in range(GH):
                        score(g, s, hh)
                        for kind, u, part in extras(g, s, hh):
                            if kind == "max":
                                maxima(u)
                            elif kind == "m":
                                turn_maxima(u)
                            elif kind == "o":
                                if part == 0:
                                    pe.wait_ge(S["attn_lo_ready"], 2 * (KD - 1))
                                    pe.wait_ge(S["w_lo"], len(ITEMS))
                                    wait_slot(pe, ("o", u))
                                out_project(2 * u + part // (KD - 1), part % (KD - 1))
                        k = STEPS * g + s - LAG
                        if hh == GH - 1 and k >= 0:
                            weigh_values(k)
            for k in range(STEPS * GROUPS - LAG, STEPS * GROUPS):
                weigh_values(k)
            pe.wait_ge(S["exp_done"], banks_before(GROUPS, 0))
            pe.wait_ge(S["u_free"], 2 * GROUPS)
            pe.wait_ge(S["attn_lo_ready"], 2 * KD - 1)
            for t in range(HT):
                out_project(t, KD - 1).then_inc(S["o_ready"], 1)
            for t in range(HT, NT):
                for k in range(KD - 1):
                    out_project(t, k)
            pe.wait_ge(S["attn_lo_ready"], 2 * KD)
            for t in range(HT, NT):
                out_project(t, KD - 1).then_inc(S["o_ready"], 1)

        @block.vector
        def _(dve):
            chain = [0]

            def then(ins):
                chain[0] += 1
                ins.then_inc(S["dve"], 1)
                dve.wait_ge(S["dve"], chain[0])

            def split_lo(n):
                dve.wait_ge(S["w_hi"], n + 1)
                hi, lo = destination(n)
                dve.tensor_tensor(lo, stage[:, n % 2, :], hi.bitcast(F32), ALU.subtract).then_inc(S["w_lo"], 1)

            def statistics(q):
                t0 = 2 * (q % 4)
                for t in range(t0, t0 + 2):
                    if q >= 4:
                        dve.wait_ge(S["out_free"], t + 1)
                    else:
                        dve.wait_ge(S[f"x_landed{(0, 1, 2, 2, 3, 3, 3, 3)[t]}"], 16)
                    last = dve.bn_stats(stats[:, t, :], x_sb[:, t, :])
                then(last)
                for t in range(t0, t0 + 2):
                    last = dve.bn_aggr(mean_var[:, t, :], stats[:, t, :])
                last.then_inc(S["stat_ready"], 1)

            def invert_std(q):
                t0 = 2 * (q % 4)
                dve.wait_ge(S["std_ready"], q + 1)
                then(dve.reciprocal(rstd[:, t0:t0 + 2], rstd[:, t0:t0 + 2]))

            def normalize(q):
                dst = xn if q < 6 else xn1
                if q >= 1:
                    dve.wait_ge(S["x_turned"], q)
                for n in range(2):
                    t = 2 * (q % 4) + n
                    dve.tensor_scalar(dst[:, n, :], x_sb[:, t, :], mean_var[:, t, 0:1], rstd[:, t:t + 1],
                                      ALU.subtract, ALU.mult).then_inc(S["xn_ready"], 1)

            def turned_lo(q):
                t = 2 * (q % 4) * P
                dve.wait_ge(S["xt_hi_ready"], q + 1)
                for n in range(2):
                    at = (slice(None), slice(None), slice(t + n * P, t + (n + 1) * P))
                    last = dve.tensor_tensor(xt_lo[at], x_bank(q, n).rearrange("p (k n) -> p k n", k=KD),
                                             xt_hi[at].bitcast(F32), ALU.subtract)
                last.then_inc(S["x_free"], 1)

            def wide(ap, *dims):
                return bass.AP(ap.tensor, ap.offset, [ap.ap[0], *[list(d) for d in dims]])

            def route(n_tok, routes, e):
                src = slot_of(("l", e))[:, 1, 0:HT * NE] if e < 2 else bank[0][:, 0:NT * ROUTES_PAD]
                w = NE if e < 2 else ROUTES_PAD
                src = src.rearrange("p (t e) -> p t e", e=w)[:, :, 0:routes]
                then(dve.tensor_reduce(rowmax[:, 0:n_tok], src, AX.X, ALU.max))
                dve.tensor_tensor(logit[:, 0:n_tok, 0:routes], src,
                                  wide(rowmax[:, 0:n_tok], (1, n_tok), (0, routes)), ALU.subtract
                                  ).then_inc(S["logit_ready"], 1)
                dve.wait_ge(S["exp_ready"], e + 1)
                for t in range(n_tok):
                    last = dve.max(top[:, t, :], prob[:, t, 0:routes])
                then(last)
                if e < 2:
                    then(dve.memset(top[:, 0:n_tok, 2:8], -1.0))
                span = ROUTES_PAD if e < 2 else ROUTES
                for t in range(n_tok):
                    last = dve.match_replace(rest[:, t, 0:span], top[:, t, :], prob[:, t, 0:span], 0.0)
                then(last)
                then(dve.tensor_tensor(chosen[:, 0:n_tok, 0:routes], prob[:, 0:n_tok, 0:routes],
                                       rest[:, 0:n_tok, 0:routes], ALU.subtract))
                over = chosen if e < 2 else prob
                then(dve.tensor_reduce(norm[:, 0:n_tok], over[:, 0:n_tok, 0:routes], AX.X, ALU.add))
                then(dve.reciprocal(norm[:, 0:n_tok], norm[:, 0:n_tok]))
                then(dve.tensor_scalar(norm[:, 0:n_tok], norm[:, 0:n_tok], SCALE0 if e < 2 else SCALE1, None, ALU.mult))

            def spread(dst, src, n_tok):
                for t in range(n_tok):
                    last = dve.tensor_scalar(dst[:, t], wide(src[:, t, 0:NE], (1, NE), (0, RANK)), norm[:, t:t + 1],
                                             None, ALU.mult)
                last.then_inc(S["gate_ready"], 1)

            statistics(0)
            invert_std(0)
            normalize(0)
            statistics(1)
            invert_std(1)
            normalize(1)
            split_lo(0)
            turned_lo(0)
            turned_lo(1)
            dve.wait_ge(S["vec_landed"], 64)
            then(dve.tensor_copy(ratio[:, 1:], disc[:, 0:ORDERS - 1]))
            then(dve.memset(ratio[:, 0:1], 0.0))
            dve.tensor_tensor(disc[:], ratio[:], disc[:], ALU.subtract).then_inc(S["ratio_diff"], 1)
            split_lo(1)
            split_lo(2)
            dve.wait_ge(S["const_ready"], 3)
            dve.wait_ge(S["ratio_ready"], 1)

            def later_term(half, o):
                k = 7 * half + o
                if o >= 2:
                    ins = dve.scalar_tensor_tensor(term_f[:, o % 2, :], delta[:], ratio[:, o - 1:o],
                                                   term_f[:, (o - 1) % 2, :], ALU.mult, ALU.mult)
                    if o == ORDER_MIN + 1:
                        then(ins)
                        ins = dve.tensor_tensor(term_f[:, o % 2, :], term_f[:, o % 2, :], keep[:], ALU.mult)
                    ins.then_inc(S["t_f"], 1)
                dve.wait_ge(S["t_hi"], k + 1)
                dve.tensor_tensor(term_lo[:, k % 3, :], term_f[:, o % 2, :], term_hi[:, k % 3, :].bitcast(F32),
                                  ALU.subtract).then_inc(S["t_lo"], 1)

            def lora_weighted(half):
                dve.wait_ge(S["l_b_ready"], half + 1)
                dve.wait_ge(S["lora_h_ready"], half + 1)
                dve.tensor_tensor(lora_h[:], slot_of(("l", half))[:, 1, :], lora_h[:], ALU.mult
                                  ).then_inc(S["hw_f_ready"], 1)
                dve.wait_ge(S["hw_hi_ready"], half + 1)
                dve.tensor_tensor(hw_lo[:], lora_h[:], hw_hi[:].bitcast(F32), ALU.subtract).then_inc(S["l_free"], 1)

            def take_out(t):
                dve.wait_ge(S["out_ready"], t + 1)
                dve.tensor_tensor(x_sb[:, t, :], bank[t % HT][:, :], x_sb[:, t, :], ALU.add
                                  ).then_inc(S["out_free"], 1)

            then(dve.tensor_copy(rw_hi[:].rearrange("p k n -> p (k n)"), rw_stage[:]))
            dve.tensor_tensor(rw_lo[:].rearrange("p k n -> p (k n)"), rw_stage[:],
                              rw_hi[:].rearrange("p k n -> p (k n)").bitcast(F32), ALU.subtract
                              ).then_inc(S["rw_ready"], 1)
            for half in range(2):
                ps = slot_of(("s", half))
                dve.wait_ge(S["s_ready"], half + 1)
                then(dve.tensor_scalar(delta[:], ps[:, 0, :], vec_sb[:, VEC_POINT:VEC_POINT + 1], None, ALU.subtract))
                then(dve.scalar_tensor_tensor(keep[:], delta[:], -1.0, delta[:], ALU.mult, ALU.max))
                dve.tensor_scalar(keep[:], keep[:], DELTA_MAX, None, ALU.is_le)
                k = 7 * half
                dve.wait_ge(S["t_hi"], k + 1)
                dve.scalar_tensor_tensor(term_f[:, 1, :], delta[:], ratio[:, 0:1], ps[:, 1, :], ALU.mult, ALU.mult
                                         ).then_inc(S["t_f"], 1)
                dve.tensor_tensor(term_lo[:, k % 3, :], ps[:, 1, :], term_hi[:, k % 3, :].bitcast(F32), ALU.subtract
                                  ).then_inc(S["t_lo"], 1)
                if half == 1:
                    for t in range(HT):
                        take_out(t)
                for c in range(FC):
                    if c + 1 < FC:
                        split_lo(item_at[(f"ffn{c + 1}", half)])
                        if half == 0:
                            split_lo(item_at[(f"res{c + 1}", 0)])
                    elif half == 0:
                        split_lo(item_at[("gate_up", 1)])
                    else:
                        split_lo(item_at[("qk0", 0)])
                    k = half * FC + c
                    m = FSHORT if c == 0 else P
                    ps = slot_of(("f", k))
                    if c == 1:
                        lora_weighted(half)
                    if c == 0:
                        dve.wait_ge(S["f_ready"], k + 1)
                        dve.tensor_scalar(lgt[FSHORT:FSHORT + NE, :], ps[FSHORT:FSHORT + NE, 0, :],
                                          vec_sb[FSHORT:FSHORT + NE, VEC_ROUTER0:VEC_ROUTER0 + 1], None, ALU.add
                                          ).then_inc(S["lgt_ready"], 1)
                    dve.wait_ge(S["silu_ready"], k + 1)
                    if k >= 1:
                        dve.wait_ge(S["h_hi_ready"], k)
                        dve.wait_ge(S["f_free"], k)
                    dve.tensor_tensor(h_f[0:m, :], ps[0:m, 1, :], silu[0:m, :], ALU.mult).then_inc(S["h_f_ready"], 1)
                    dve.wait_ge(S["h_hi_ready"], k + 1)
                    dve.tensor_tensor(h_lo[0:m, c % 2, :], h_f[0:m, :], h_hi[0:m, c % 2, :].bitcast(F32),
                                      ALU.subtract).then_inc(S["f_free"], 1)
                    if c == 0:
                        dve.wait_ge(S["l_a_ready"], half + 1)
                        route(HT, NE, half)
                        spread(gate_x, chosen, HT)
                    if 1 <= c <= ORDERS:
                        later_term(half, c)
                    if c == 1:
                        statistics(2 + 2 * half)
                        statistics(3 + 2 * half)
                    if c == 2:
                        invert_std(2 + 2 * half)
                        invert_std(3 + 2 * half)
                        normalize(2 + 2 * half)
                    if c in X_AFTER:
                        q = 2 + 2 * half + X_AFTER.index(c)
                        turned_lo(q)
                        if q % 2 == 0:
                            normalize(q + 1)
                    if c == FC - 1:
                        if half == 0:
                            split_lo(item_at[("ffn0", 1)])
                        else:
                            split_lo(item_at[("qk1", 0)])
            for q in (6, 7):
                for t in range(2 * q - 8, 2 * q - 6):
                    take_out(t)
                statistics(q)
            for q in (6, 7):
                invert_std(q)
                normalize(q)
            turned_lo(6)
            turned_lo(7)
            dve.wait_ge(S["const_ready"], 5)
            then(dve.tensor_copy(map_f[:], map_i[:]))
            then(dve.tensor_tensor(onehot[:], wide(map_f[:], (0, NE), (1, ROUTES)),
                                   wide(expert_id[:], (1, NE), (0, ROUTES)), ALU.is_equal))

            def project_lo(which, m):
                col = (VEC_Q if which == "q" else VEC_K) + m
                dve.wait_ge(S[f"{which}_hi"], m + 1)
                dve.scalar_tensor_tensor(nat[which, 1], slot_of((which, m))[:].rearrange("p a n -> p (a n)"),
                                         vec_sb[:, col:col + 1], nat[which, 0].bitcast(F32), ALU.add, ALU.subtract
                                         ).then_inc(S[f"{which}_free"], 1)

            dve.wait_ge(S["r_ready"], 1)
            dve.tensor_scalar(lgt1, slot_of(("r", 0))[0:ROUTES_PAD].rearrange("p a n -> p (a n)"),
                              vec_sb[0:ROUTES_PAD, VEC_ROUTER1:VEC_ROUTER1 + 1], None, ALU.add
                              ).then_inc(S["r_free"], 1)
            project_lo("q", 0)
            dve.wait_ge(S["lt_ready"], 1)
            route(NT, ROUTES, 2)
            for t in range(NT):
                prod = hw_f1[:, t * NE * ROUTES:(t + 1) * NE * ROUTES].rearrange(
                    "p (e n) -> p e n", e=NE)
                last = dve.tensor_tensor(prod, wide(chosen[:, t, 0:ROUTES], (0, NE), (1, ROUTES)), onehot[:], ALU.mult)
            then(last)
            then(dve.tensor_reduce(gate[:].rearrange("p t e -> p (t e)"),
                                   hw_f1[:, 0:NT * NE * ROUTES].rearrange("p (e n) -> p e n", n=ROUTES), AX.X, ALU.add))
            spread(gate_x1, gate, NT)
            project_lo("k", 0)
            for m, names in enumerate((["qk2"], ["qk3"], ["lora1", "wv0"]), 1):
                for name in names:
                    split_lo(item_at[(name, 0)])
                project_lo("q", m)
                project_lo("k", m)
            split_lo(item_at[("wv1", 0)])
            dve.wait_ge(S["w_ready"], 1)
            dve.wait_ge(S["a_free"], 1)
            dve.tensor_tensor(hw_f1, slot_of(("w", 0))[:].rearrange("p a n -> p (a n)"), lora_h1, ALU.mult
                              ).then_inc(S["w_free"], 1)
            dve.wait_ge(S["hw_hi_ready"], 3)
            dve.tensor_tensor(hw1[1], hw_f1, hw1[0].bitcast(F32), ALU.subtract
                              ).then_inc(S["hw1_ready"], 1)

            def row_max(u):
                g = u // UNITS
                i, hh, c, n = MAX_UNITS[u % UNITS]
                dve.wait_ge(S["max_ready"], u + 1)
                if g >= 2 and u % UNITS == 0:
                    dve.wait_ge(S["m_ready"], g - 1)
                score = bank_of(("max", u))[:, 0:n]
                mask = (NT - 1 - i) * P + c
                h = 2 * (hh % 2) + hh // 2
                to = maxcol[:, g % 2, h, i:i + 1] if c == 0 else maxrest[:, g % 2, h, i - NT // 2:i - NT // 2 + 1]
                dve.tensor_tensor_reduce(score, score, causal[:, mask:mask + n], 1.0, -3.0e38, ALU.add, ALU.max, to
                                         ).then_inc(S["max_free"], 1)
                if u % UNITS == UNITS - 1:
                    dve.wait_ge(S["max_free"], u + 1)
                    dve.tensor_tensor(maxcol[:, g % 2, :, NT // 2:], maxcol[:, g % 2, :, NT // 2:],
                                      maxrest[:, g % 2], ALU.max).then_inc(S["max_joined"], 1)

            def neg_max_lo(g):
                dve.wait_ge(S["m_hi"], g + 1)
                dve.scalar_tensor_tensor(negm[:, g % 2, 1, :], bank_of(("m", g))[0:GH * NT, 0:P], -1.0,
                                         negm[:, g % 2, 0, :].bitcast(F32), ALU.mult, ALU.subtract
                                         ).then_inc(S["m_free"], 1)

            def invert_den(g, half):
                dve.wait_ge(S[f"den_landed{half}"], 16 * (g + 1))
                dve.reciprocal(den[:, half, :], den[:, half, :]).then_inc(S["den_inverted"], 1)

            def divide(m, half):
                k = 2 * m + half
                at = slice(half * HALF, (half + 1) * HALF)
                dve.wait_ge(S[f"u_landed{half}"], 32 * (2 * m + 2))
                dve.tensor_tensor(u_all[:, at], u_all[:, at], den_all[:, at], ALU.mult).then_inc(S["attn_f"], 1)

            def attn_split_lo(m, half):
                k = 2 * m + half
                at = slice(half * HALF, (half + 1) * HALF)
                dve.wait_ge(S["attn_hi_ready"], k + 1)
                dve.scalar_tensor_tensor(attn_lo[:, m, at], u_all[:, at], vec_sb[:, VEC_V + m:VEC_V + m + 1],
                                         attn_hi[:, m, at].bitcast(F32), ALU.add, ALU.subtract
                                         ).then_inc(S["attn_lo_ready"], 1)

            for t in range(NT):
                for u in range(UNITS * t // NT, UNITS * (t + 1) // NT):
                    row_max(u)
                if t in (2, 4):
                    split_lo(item_at[(f"base{t // 2 - 1}", 0)])
            neg_max_lo(0)
            for u in range(UNITS, UNITS + EARLY_UNITS):
                row_max(u)
            dve.wait_ge(S["y_done"], NT)
            dve.memset(keys(2).rearrange("p b n -> p (b n)").bitcast(F32), 1.0).then_inc(S["blank2"], 1)
            for g in range(GROUPS):
                for s in range(STEPS):
                    if s == MAX_END + 2 and g + 1 < GROUPS:
                        neg_max_lo(g + 1)
                    for hh in range(GH):
                        for kind, u, _ in extras(g, s, hh):
                            if kind == "max":
                                row_max(u)
                    if s == LAG + 2 and g > 0:
                        invert_den(g - 1, 1)
                    if s == HT + LAG + 2:
                        invert_den(g, 0)
                    if (g, s) in DIVIDE_AT:
                        divide(*DIVIDE_AT[g, s])
                    if (g, s - 2) in DIVIDE_AT:
                        attn_split_lo(*DIVIDE_AT[g, s - 2])
                    if (g, s) in SPLIT_AT:
                        split_lo(item_at[(SPLIT_AT[g, s], 0)])
            attn_split_lo(KD - 1, 0)
            invert_den(GROUPS - 1, 1)

            def take_out_project(t):
                dve.wait_ge(S["o_ready"], t + 1)
                dve.tensor_tensor(x_sb[:, t, :], o_bank(t), x_sb[:, t, :], ALU.add).then_inc(S["out_sb_ready"], 1)

            dve.wait_ge(S["y_added"], NT)
            for t in range(HT):
                take_out_project(t)
            divide(KD - 1, 1)
            attn_split_lo(KD - 1, 1)
            for t in range(HT, NT):
                take_out_project(t)


def kernel(**inputs):
    import concourse.bacc as bacc
    from concourse.bass_utils import run_bass_kernel_spmd

    w = {k: np.asarray(v) for k, v in inputs.items()}
    stream, router1 = lay_out_weights(w)
    vec = np.zeros((P, VECS), np.float32)
    vec[:, VEC_POINT] = w["L0_attn_local_point"]
    vec[FSHORT:FSHORT + NE, VEC_ROUTER0] = w["L0_ffn_router_b"]
    vec[:ROUTES, VEC_ROUTER1] = w["L1_ffn_router_b"]
    vec[:, VEC_Q:VEC_Q + KD] = w["L1_attn_bq"].reshape(KD, P).T
    vec[:, VEC_K:VEC_K + KD] = w["L1_attn_bk"].reshape(KD, P).T
    vec[:, VEC_V:VEC_V + KD] = w["L1_attn_bv"].reshape(KD, P).T
    arrays = {
        "stream": stream, "router1": router1.reshape(P, -1),
        "x": np.ascontiguousarray(w["L0_attn_hidden_states"].reshape(NT, P, D)), "vec": vec,
        "bias_rows": np.stack([w["L1_ffn_base_b"], w["L1_attn_bo"]]),
        "discount": w["L0_attn_discount_factor"], "expert_map": w["L1_ffn_expert_map"],
    }
    nc = bacc.Bacc("TRN2", target_bir_lowering=False, num_devices=1)
    args = [nc.dram_tensor(f"in_{n}", a.shape, mybir.dt.from_np(a.dtype), kind="ExternalInput").ap()
            for n, a in arrays.items()]
    y = nc.dram_tensor("out_y", (NT, P, D), F32, kind="ExternalOutput").ap()
    heads_dram = nc.dram_tensor("heads_dram", (KD, 2, 2 * GH, 2 * HD, TOK), F32).ap()
    max_dram = nc.dram_tensor("max_dram", (GROUPS, 2, GH, TOK), F32).ap()
    u_dram = nc.dram_tensor("u_dram", (2 * GROUPS, P, HALF), F32).ap()
    den_dram = nc.dram_tensor("den_dram", (2 * GROUPS, GH, HALF), F32).ap()
    build(nc, *args, heads_dram, max_dram, u_dram, den_dram, y)
    result = run_bass_kernel_spmd(nc, [{f"in_{n}": a for n, a in arrays.items()}], core_ids=[0])
    return result.results[0]["out_y"].reshape(1, TOK, D)
```
